# Optimizing a Trainium2 kernel written in Bass

```python
import numpy as np
import jax
import jax.numpy as jnp

def _softmax(x, axis=-1):
    return jax.nn.softmax(x, axis=axis)

def _gelu(x):
    return jax.nn.gelu(x, approximate=True)

def _silu(x):
    return jax.nn.silu(x)

def _sigmoid(x):
    return jax.nn.sigmoid(x)

def _layernorm(x, axis=-1, eps=1e-05):
    m = jnp.mean(x, axis=axis, keepdims=True)
    v = jnp.var(x, axis=axis, keepdims=True)
    return (x - m) / jnp.sqrt(v + eps)

def _scatter_add(tgt, idx, src, axis=0):
    return tgt.at[idx].add(src)

def _segment_sum(src, seg, n):
    return jax.ops.segment_sum(src, seg, n)
kernel_name = 'mk_lm_tower_d1_tok_ids768_r4_c7bfab'

def setup_inputs(seed: int=0):
    np.random.seed(seed)
    _w = jnp.asarray

    def _rec_inputs():
        import jax
        import jax.numpy as jnp
        _rk = jax.random.key(seed)
        x = jax.random.randint(jax.random.fold_in(_rk, 1), (32, 128), 0, 30521, jnp.int32)
        mask_BS_i1_0 = jnp.where(jnp.ones((32, 128), dtype=bool), 1, 0).astype(jnp.int32)
        pos_BS = jnp.broadcast_to(jnp.arange(128, dtype=jnp.int32), (32, 128))
        return (x, mask_BS_i1_0, pos_BS)
    x, mask_BS_i1_0, pos_BS = _rec_inputs()

    def _L0_tok_setup():
        import jax, jax.numpy as jnp
        import numpy as np
        EPS = 1e-12
        key = jax.random.key(seed)
        ks = jax.random.split(key, 8)
        B, S, H = (32, 128, 192)
        V, P, T = (30522, 128, 2)
        input_ids = jax.random.randint(ks[0], (B, S), 0, V, dtype=jnp.int32)
        token_type_ids = jax.random.randint(ks[1], (B, S), 0, T, dtype=jnp.int32)
        position_ids = jnp.broadcast_to(jnp.arange(S, dtype=jnp.int32), (B, S))
        word_emb = jax.random.normal(ks[2], (V, H), dtype=jnp.float32) * 0.02
        word_emb = word_emb.at[0].set(0.0)
        pos_emb = jax.random.normal(ks[3], (P, H), dtype=jnp.float32) * 0.02
        type_emb = jax.random.normal(ks[4], (T, H), dtype=jnp.float32) * 0.02
        gamma = jnp.ones((H,), dtype=jnp.float32)
        beta = jnp.zeros((H,), dtype=jnp.float32)
        return {'input_ids': input_ids, 'token_type_ids': token_type_ids, 'position_ids': position_ids, 'word_emb': word_emb, 'pos_emb': pos_emb, 'type_emb': type_emb, 'gamma': gamma, 'beta': beta}
    _L0_tok_all = _L0_tok_setup()
    _L0_tok_in = {k: v for k, v in _L0_tok_all.items() if k in ('word_emb', 'pos_emb', 'type_emb', 'gamma', 'beta')}
    del _L0_tok_all

    def _L0_attn_setup():
        import jax, jax.numpy as jnp
        import numpy as np
        B, C, D = (8, 512, 192)
        EPS = 1e-05
        key = jax.random.key(seed)
        kx, kk, kq, kv = jax.random.split(key, 4)
        x = jax.random.normal(kx, (B, C, D), dtype=jnp.float32)
        s = 1.0 / np.sqrt(D)
        Wk = jax.random.uniform(kk, (D, D), dtype=jnp.float32, minval=-s, maxval=s)
        Wq = jax.random.uniform(kq, (D, D), dtype=jnp.float32, minval=-s, maxval=s)
        Wv = jax.random.uniform(kv, (D, D), dtype=jnp.float32, minval=-s, maxval=s)
        return {'x': x, 'Wk': Wk, 'Wq': Wq, 'Wv': Wv}
    _L0_attn_all = _L0_attn_setup()
    _L0_attn_in = {k: v for k, v in _L0_attn_all.items() if k in ('Wk', 'Wq', 'Wv')}
    del _L0_attn_all

    def _L0_ffn_setup():
        import jax, jax.numpy as jnp
        import numpy as np
        DECAY = 0.9
        EPS = 0.01
        TOP_K = 2
        key = jax.random.key(seed)
        k1, k2, k3, k4 = jax.random.split(key, 4)
        B, S, H, I, E = (4, 512, 192, 512, 8)
        return {'hidden_states': jax.random.normal(k1, (B, S, H), jnp.float32), 'router_w': jax.random.normal(k2, (E, H), jnp.float32) * 0.02, 'w1': jax.random.normal(k3, (E, I, H), jnp.float32) * 0.02, 'w2': jax.random.normal(k4, (E, H, I), jnp.float32) * 0.02}
    _L0_ffn_all = _L0_ffn_setup()
    _L0_ffn_in = {k: v for k, v in _L0_ffn_all.items() if k in ('router_w', 'w1', 'w2')}
    del _L0_ffn_all
    return {'x': x, 'mask_BS_i1_0': mask_BS_i1_0, 'pos_BS': pos_BS, 'L0_tok_word_emb': _L0_tok_in['word_emb'], 'L0_tok_pos_emb': _L0_tok_in['pos_emb'], 'L0_tok_type_emb': _L0_tok_in['type_emb'], 'L0_tok_gamma': _L0_tok_in['gamma'], 'L0_tok_beta': _L0_tok_in['beta'], 'L0_attn_Wk': _L0_attn_in['Wk'], 'L0_attn_Wq': _L0_attn_in['Wq'], 'L0_attn_Wv': _L0_attn_in['Wv'], 'L0_ffn_router_w': _L0_ffn_in['router_w'], 'L0_ffn_w1': _L0_ffn_in['w1'], 'L0_ffn_w2': _L0_ffn_in['w2']}

def reference(x, mask_BS_i1_0, pos_BS, L0_tok_word_emb, L0_tok_pos_emb, L0_tok_type_emb, L0_tok_gamma, L0_tok_beta, L0_attn_Wk, L0_attn_Wq, L0_attn_Wv, L0_ffn_router_w, L0_ffn_w1, L0_ffn_w2):
    import jax
    import jax.numpy as jnp

    def _L0_tok_ref(input_ids, token_type_ids, position_ids, word_emb, pos_emb, type_emb, gamma, beta):
        import jax, jax.numpy as jnp
        import numpy as np
        EPS = 1e-12
        x = word_emb[input_ids] + pos_emb[position_ids] + type_emb[token_type_ids]
        mu = jnp.mean(x, axis=-1, keepdims=True)
        var = jnp.mean(jnp.square(x - mu), axis=-1, keepdims=True)
        y = (x - mu) * jax.lax.rsqrt(var + EPS) * gamma + beta
        return y

    def _L0_attn_ref(x, Wk, Wq, Wv):
        import jax, jax.numpy as jnp
        import numpy as np
        B, C, D = (8, 512, 192)
        EPS = 1e-05
        mean = jnp.mean(x, axis=(-2, -1), keepdims=True)
        var = jnp.mean(jnp.square(x - mean), axis=(-2, -1), keepdims=True)
        xn = (x - mean) * jax.lax.rsqrt(var + EPS)
        keys = jnp.einsum('bcd,od->bco', xn, Wk)
        queries = jnp.einsum('bcd,od->bco', xn, Wq)
        values = jnp.einsum('bcd,od->bco', xn, Wv)
        att = jax.nn.softmax(jnp.einsum('bid,bjd->bij', queries, keys), axis=-1)
        return jnp.einsum('bjd,bij->bid', values, att)

    def _L0_ffn_ref(hidden_states, router_w, w1, w2):
        import jax, jax.numpy as jnp
        import numpy as np
        DECAY = 0.9
        EPS = 0.01
        TOP_K = 2
        B, S, H = hidden_states.shape
        E = router_w.shape[0]
        flat = hidden_states.reshape(B * S, H)
        logits = flat @ router_w.T
        probs = jax.nn.softmax(logits, axis=-1)
        topk_probs, topk_idx = jax.lax.top_k(probs, TOP_K)
        importance = jax.lax.stop_gradient(probs).sum(axis=0)
        running = jnp.ones((E,), dtype=flat.dtype)
        blended = running + (1.0 - DECAY) * (importance - running)
        running = blended + EPS
        balance = running[topk_idx]
        balanced = topk_probs / balance
        balanced = balanced / balanced.sum(axis=-1, keepdims=True)
        h = jnp.einsum('th,eih->tei', flat, w1)
        h = jax.nn.silu(h)
        outs = jnp.einsum('tei,ehi->teh', h, w2)
        sel = jnp.take_along_axis(outs, topk_idx[:, :, None], axis=1)
        combined = (sel * balanced[..., None]).sum(axis=1)
        return combined.reshape(B, S, H)
    h = _L0_tok_ref(x, mask_BS_i1_0, pos_BS, L0_tok_word_emb, L0_tok_pos_emb, L0_tok_type_emb, L0_tok_gamma, L0_tok_beta)
    h = h + _L0_attn_ref(_layernorm(h, axis=-1), L0_attn_Wk, L0_attn_Wq, L0_attn_Wv)
    h = h + _L0_ffn_ref(_layernorm(h, axis=-1), L0_ffn_router_w, L0_ffn_w1, L0_ffn_w2)
    return h

_drawn_inputs = setup_inputs


def setup_inputs(seed=0):
    import zlib

    import numpy as np

    out = dict(_drawn_inputs(seed))
    spreads = {'L0_tok_gamma': (1.0, 0.2), 'L0_tok_beta': (0.0, 0.1)}
    factors = {}
    for name, (base, spread) in spreads.items():
        noise = np.random.default_rng([zlib.crc32(name.encode()), seed]).standard_normal(out[name].shape)
        drawn = base * np.exp(spread * noise) if base else spread * noise
        out[name] = jnp.asarray(drawn.astype(out[name].dtype))
    for name, factor in factors.items():
        out[name] = (out[name] * factor).astype(out[name].dtype)
    return out
```

```python
import concourse.bass as bass
from concourse import mybir
from contextlib import ExitStack


def tower_kernel(nc, ids, pos_ids, type_ids, word_emb, pos_emb, type_emb, gamma, beta,
                 wq, wk, wv_t, router_t, w1_t, w2_t, out):
    fp32, fp16, bf16, i32, u32 = (mybir.dt.float32, mybir.dt.float16, mybir.dt.bfloat16,
                                  mybir.dt.int32, mybir.dt.uint32)
    ALU = mybir.AluOpType
    ACT = mybir.ActivationFunctionType
    AX = mybir.AxisListType.X

    P = 128
    D = word_emb.shape[1]
    D2 = D - P
    TILES = ids.shape[1]
    TOKENS = TILES * P
    E = router_t.shape[1]
    I = w1_t.shape[1] // E
    IC = I // P
    TOP = 2
    CH = 8
    CHUNKS = TILES // CH
    PAIRS = TILES // 2
    XC = 2 * D
    ROW = XC + 4
    REGION = TOKENS + P
    SLOTS = (TOP * TOKENS + E * (P - 1)) // P
    SLOTS = SLOTS + (-SLOTS) % 4
    REST = E * P
    PADS = 2 * E
    TRASH = PADS * TOP * P
    LEAD = 2
    NL = 11

    ctx = ExitStack()
    with ctx:
        def sb(name, shape, dt=fp32):
            return ctx.enter_context(nc.sbuf_tensor(name, shape, dt))

        def sem(name):
            return ctx.enter_context(nc.semaphore(name))

        sorted_rows = nc.dram_tensor("sorted_rows", (E * REGION + REST, ROW), fp16, kind="Internal").ap()
        y_rows = nc.dram_tensor("y_rows", (TOP * TOKENS + TRASH, D), fp32, kind="Internal").ap()

        stage = sb("stage", [P, E, 2, I])
        carved = [0]

        def carve(shape, dt=fp32):
            n = 1
            for x in shape:
                n *= x
            words = n if dt == fp32 else n // 2
            at, carved[0] = carved[0], carved[0] + words
            ap = stage[:].rearrange("p e a i -> p (e a i)")[:, at:at + words]
            ap = ap if dt == fp32 else ap.bitcast(dt)
            names = " ".join("abc"[:len(shape)])
            return ap.rearrange(f"p ({names}) -> p {names}", **dict(zip("abc", shape))) if len(shape) > 1 else ap

        ident = sb("ident", [P, P])
        ident16 = sb("ident16", [P, P], fp16)
        before = sb("before", [P, P], bf16)
        ones_b = sb("ones_b", [P, P], bf16)
        mean_w = sb("mean_w", [P, P])
        ones_f = sb("ones_f", [P, P])
        part = sb("part", [P, 2])
        part_i = sb("part_i", [P, 2], i32)
        iota_e = sb("iota_e", [P, E])
        token2 = sb("token2", [P, TILES])
        base = sb("base", [P, E])
        upto = sb("upto", [P, E, E])
        tile_no = sb("tile_no", [P, SLOTS])
        ids_sb = sb("ids_sb", [P, TILES], i32)
        gb = sb("gb", [P, 2, D])
        tab = sb("tab", [P, 2, D])
        tab_r = sb("tab_r", [P, 2, D])
        tab_p = [sb(f"tab_p{n}", [P, 2, D], bf16) for n in range(3)]
        type_p = sb("type_p", [P, D], bf16)
        pt_ids = sb("pt_ids", [P, 2, CH * P], i32)
        onehot = sb("onehot", [P, 2, CH * P], bf16)
        h = sb("h", [P, TILES, D])
        word = sb("word", [P, TILES, D])
        st = sb("st", [P, CH, 6])
        mv = sb("mv", [P, CH, 2])
        nv = sb("nv", [P, CH])
        ny = sb("ny", [P, CH])
        nt = sb("nt", [P, CH])
        rowvar = sb("rowvar", [P, CH])
        rstd1 = sb("rstd1", [P, CH])
        mean1 = sb("mean1", [P, TILES])
        coef1 = sb("coef1", [P, TILES])
        mv2 = sb("mv2", [P, TILES, 2])
        wq_sb = sb("wq_sb", [P, 2, D])
        wk_sb = sb("wk_sb", [P, 2, D])
        wv_sb = sb("wv_sb", [P, 2, D])
        wqk = sb("wqk", [P, 2, D])
        xn = [sb(f"xn{n}", [P, 2, D]) for n in range(2)]
        xnT = [sb(f"xnT{n}", [P, 2, 2 * P]) for n in range(2)]
        gT = [sb(f"gT{n}", [P, 2, 2 * P]) for n in range(2)]
        v_sb = [sb(f"v_sb{n}", [P, 2, D]) for n in range(2)]
        pr = [sb(f"pr{n}", [P, 2, P]) for n in range(2)]
        prT = [sb(f"prT{n}", [P, 2, P]) for n in range(2)]
        nmax = [sb(f"nmax{n}", [P, 2]) for n in range(2)]
        rsum = [sb(f"rsum{n}", [P, 2]) for n in range(2)]
        rinv = [sb(f"rinv{n}", [P, 2]) for n in range(2)]
        mvp = sb("mvp", [P, 2, 2])
        st2 = [sb(f"st2{n}", [P, 2, 6]) for n in range(2)]
        x2 = carve((CH, D))
        rows = [carve((CH, ROW), fp16) for n in range(2)]
        x2T = carve((CH, 3, P), fp16)
        rt_f = sb("rt_f", [P, 2, E])
        rt = sb("rt", [P, 4, E], fp16)
        lmax = sb("lmax", [P, CH])
        lg = sb("lg", [P, CH, E])
        esum = sb("esum", [P, CH])
        probs = sb("probs", [P, TILES, E])
        top8 = sb("top8", [P, CH, 8])
        idx8 = sb("idx8", [P, CH, 8], u32)
        idxf = sb("idxf", [P, CH, TOP])
        picked = sb("picked", [P, TOP, TILES, E])
        top_p = sb("top_p", [P, TOP, TILES])
        marks = sb("marks", [P, CH + 1, E], bf16)
        place = sb("place", [P, CH, E])
        place_k = sb("place_k", [P, TOP, CH, E])
        slot_f = sb("slot_f", [P, TOP, CH])
        slot = [sb(f"slot{n}", [P, TOP, CH], i32) for n in range(2)]
        w1 = sb("w1", [P, E, 4, I], fp16)
        w2 = sb("w2", [P, E, IC, 2, D], fp16)
        sq = sb("sq", [P, 3, 16])
        sqs = sb("sqs", [P, 3])
        scale_i = sb("scale_i", [P, 4, 2], i32)
        scale = sb("scale", [P, 8])
        cnt = sb("cnt", [P, E])
        cnt_i = sb("cnt_i", [P, E], i32)
        tiles_e = sb("tiles_e", [P, E])
        jump = sb("jump", [P, E])
        last_e = sb("last_e", [P, E])
        passed = sb("passed", [P, SLOTS, E])
        e_f = sb("e_f", [P, SLOTS])
        row_f = sb("row_f", [P, SLOTS])
        e_i = sb("e_i", [P, SLOTS], i32)
        row_i = sb("row_i", [P, SLOTS], i32)
        base_i = sb("base_i", [P, E], i32)
        xin = [carve((ROW,), fp16) for n in range(4)]
        xT = [sb(f"xT{n}", [P, 3, P], fp16) for n in range(2)]
        hs = [sb(f"hs{n}", [P, I]) for n in range(2)]
        hT = [sb(f"hT{n}", [P, 2, IC, P], fp16) for n in range(2)]
        y_lo = [carve((D,)) for n in range(2)]
        y_sb = [carve((D,)) for n in range(4)]
        y_to = [sb(f"y_to{n}", [P, 1], i32) for n in range(4)]
        imp = sb("imp", [P, E])
        bal = sb("bal", [P, TOP, TILES, E])
        wgt = sb("wgt", [P, TOP, TILES])
        wsum = sb("wsum", [P, TILES])
        pads = word[:].rearrange("p t d -> p (t d)")[:, 0:PADS * ROW // 2].rearrange("p (n r) -> p n r", n=PADS)
        back = [word[:, 8 * n:8 * n + 8, :].rearrange("p (b k) d -> p b k d", k=2) for n in range(4)]

        bank = [ctx.enter_context(nc.psum_tensor(f"bank{n}", [P, 512], fp32)) for n in range(8)]

        s_ids, s_small, s_attw, s_gb = sem("ids_in"), sem("small_in"), sem("attn_w_in"), sem("gb_in")
        s_w1in, s_w2in, s_rin = sem("w1_in"), sem("w2_in"), sem("router_in")
        s_word = [sem(f"words_in{n}") for n in range(2)]
        s_pt = sem("pt_ids_in")
        s_const = sem("const_ready")
        s_vc, s_ac, s_gc = sem("vector_step"), sem("scalar_step"), sem("gpsimd_step")
        s_alone = sem("waits_alone")
        s_tab = sem("tables_ready")
        s_wqk, s_wqk_sb = sem("wqk_done"), sem("wqk_ready")
        s_oh, s_emb, s_embadd = sem("onehot_ready"), sem("emb_done"), sem("emb_added")
        s_rv, s_bv, s_h = sem("rowvar_ready"), sem("batchvar_done"), sem("h_ready")
        s_xn, s_xt, s_xtsb = sem("xn_ready"), sem("xnT_done"), sem("xnT_ready")
        s_g, s_gsb, s_v, s_vsb = sem("g_done"), sem("g_ready"), sem("v_done"), sem("v_ready")
        s_s, s_max, s_p = sem("scores_done"), sem("max_ready"), sem("p_ready")
        s_pt_, s_ptsb, s_o, s_res = sem("pT_done"), sem("pT_ready"), sem("o_done"), sem("residual_added")
        s_rows, s_x2t, s_x2tsb, s_lg = sem("rows_ready"), sem("x2T_done"), sem("x2T_ready"), sem("logits_done")
        s_lgx, s_ex, s_mk, s_rk = sem("logits_shifted"), sem("exp_ready"), sem("marks_ready"), sem("ranks_done")
        s_slot = sem("slots_ready")
        s_scat = [sem(f"scattered{n}") for n in range(2)]
        s_sq, s_sqs, s_scale = sem("squares_ready"), sem("squares_summed"), sem("scale_ready")
        s_whi, s_wlo = sem("w_high_ready"), sem("w_low_ready")
        s_plan, s_pads, s_pad = sem("plan_ready"), sem("padding_ready"), sem("padding_written")
        s_xin = [sem(f"x_in{n}") for n in range(4)]
        s_xft, s_xftsb, s_h1, s_hs = sem("xT_done"), sem("xT_ready"), sem("h_done"), sem("silu_ready")
        s_ht, s_hi, s_lo = sem("hT_done"), sem("hT_high_ready"), sem("hT_low_ready")
        s_y, s_ylo, s_ysb, s_to = sem("y_done"), sem("y_low_ready"), sem("y_ready"), sem("y_place_ready")
        s_ysc = [sem(f"y_scattered{n}") for n in range(4)]
        s_imp, s_wgt = sem("importance_done"), sem("weights_ready")
        s_back = [sem(f"y_back{n}") for n in range(4)]
        s_fin = sem("result_ready")
        s_out = [sem(f"result_out{n}") for n in range(4)]

        class Steps:

            def __init__(self, eng, s):
                self.eng, self.s, self.base, self.n = eng, s, 0, 0

            def did(self, ins):
                self.n += 1
                ins.then_inc(self.s, 1)

            def wait(self):
                self.eng.wait_ge(self.s, self.base + self.n)

            def round(self, i, links):
                self.start = self.base + self.n if self.n else self.base
                self.base, self.n, self.links = self.start + i * links, 0, links

            def end(self, rounds):
                assert self.n == self.links, (self.n, self.links)
                self.base, self.n = self.start + rounds * self.links, 0

        def alone(eng):
            eng.sem_inc(s_alone, 1)

        def mm(out_, lhsT, rhs, start, stop):
            return nc.tensor.matmul(out_, lhsT, rhs, start=start, stop=stop)

        def run_experts(eng, step):
            for t in range(4):
                step(t, t, 0)
            with eng.Fori(1, SLOTS // 4) as i:
                for q in range(4):
                    step(i * 4 + q, q, i * 4)
            for t in range(SLOTS, SLOTS + 3):
                step(t, t % 4, t - t % 4)

        block = ctx.enter_context(nc.Block())

        @block.sync
        def _(sp):
            sp.dma_start(ids_sb[:], ids).then_inc(s_ids, 16)
            sp.dma_start(tab[:, 0, :], pos_emb).then_inc(s_small, 16)
            sp.wait_ge(s_const, 1)
            for n in range(3):
                sp.dma_start(tab[32 * n:32 * n + 2, 1, :], type_emb).then_inc(s_small, 16)

            def chunk_ids(c):
                for n, src in ((0, pos_ids), (1, type_ids)):
                    sp.dma_start(pt_ids[:, n, :], src[:, bass.ds(c * (CH * P), CH * P)].partition_broadcast(P))\
                      .then_inc(s_pt, 16)
            chunk_ids(0)
            sp.dma_start(gb[:, 0, :], gamma.partition_broadcast(P)).then_inc(s_gb, 16)
            sp.dma_start(gb[:, 1, :], beta.partition_broadcast(P)).then_inc(s_gb, 16)
            for dst, src in ((wq_sb, wq), (wk_sb, wk), (wv_sb, wv_t)):
                sp.dma_start(dst[:, 0, :], src[0:P, :]).then_inc(s_attw, 16)
                sp.dma_start(dst[0:D2, 1, :], src[P:D, :]).then_inc(s_attw, 16)
            sp.dma_start(rt_f[:, 0, :], router_t[0:P, :]).then_inc(s_rin, 16)
            sp.dma_start(rt_f[0:D2, 1, :], router_t[P:D, :]).then_inc(s_rin, 16)
            sp.dma_start(rt_f[D2:P, 1, :], router_t[P:D, :]).then_inc(s_rin, 16)
            w1_v = w1_t.rearrange("d (e i) -> d e i", e=E)
            sp.dma_start(stage[:, :, 0, :], w1_v[0:P, :, :]).then_inc(s_w1in, 16)
            sp.dma_start(stage[0:D2, :, 1, :], w1_v[P:D, :, :]).then_inc(s_w1in, 16)
            sp.dma_start(stage[D2:P, :, 1, :], w1_v[P:D, :, :]).then_inc(s_w1in, 16)
            with sp.Fori(0, CHUNKS - 1) as i:
                sp.wait_ge(s_oh, i + 1)
                chunk_ids(i + 1)
            sp.wait_ge(s_wlo, 1)
            sp.dma_start(stage[:].rearrange("p e a i -> p (e a i)")[:, 0:E * IC * D], w2_t).then_inc(s_w2in, 16)

            sp.wait_ge(s_pads, 1)
            for e in range(E):
                sp.dma_start(sorted_rows[E * REGION + e * P:E * REGION + (e + 1) * P, :], pads[:, E + e, :].bitcast(fp16))\
                  .then_inc(s_pad, 16)
            sp.wait_ge(s_plan, 1)
            for e in range(E):
                at = nc.sync.value_load(base_i[0:1, e:e + 1], min_val=0, max_val=E * REGION)
                sp.dma_start(sorted_rows[bass.ds(at, P), :], pads[:, e, :].bitcast(fp16)).then_inc(s_pad, 16)
            sp.wait_ge(s_pad, 2 * E * 16)
            for n in range(2):
                sp.wait_ge(s_scat[n], 16 * TOP * CH * CHUNKS // 2)
            with sp.Fori(0, SLOTS // 4) as i:
                for q in range(4):
                    at = nc.sync.value_load(row_i[0:1, bass.ds(i * 4 + q, 1)], min_val=0,
                                            max_val=E * REGION + REST - P)
                    sp.wait_ge(s_xft, i * 4 + (q + 1))
                    sp.wait_ge(s_to, i * 4 + (q + 1))
                    sp.dma_start(xin[q][:], sorted_rows[bass.ds(at, P), :]).then_inc(s_xin[q], 16)
            for q in range(4):
                sp.wait_ge(s_ysc[q], 16 * SLOTS // 4)
            y_v = y_rows[0:TOP * TOKENS, :].rearrange("(b p k) d -> p b (k d)", p=P, k=TOP)
            for g in range(TILES // 4):
                if g >= 4:
                    sp.wait_ge(s_out[g % 4], 16)
                sp.dma_start(back[g % 4].rearrange("p b k d -> p b (k d)"), y_v[:, 4 * g:4 * g + 4, :])\
                  .then_inc(s_back[g % 4], 16)
            for g in range(4):
                sp.wait_ge(s_out[g], 32)

        @block.gpsimd
        def _(pool):
            gp = nc.gpsimd
            links = Steps(pool, s_gc)
            gp.memset(tab[:, 1, :], 0.0).then_inc(s_const, 1)
            pool.wait_ge(s_ids, 16)

            def words(c):
                if c >= 2:
                    pool.wait_ge(s_word[c % 2], 16 * CH * (c // 2))
                for t in range(c * CH, (c + 1) * CH):
                    gp.indirect_dma_start(word[:, t, :], None, word_emb,
                                          bass.IndirectOffsetOnAxis(ids_sb[:, t:t + 1], 0))\
                      .then_inc(s_word[c % 2], 16)
            words(0)
            links.did(gp.memset(ident[:], 0.0))
            links.did(gp.memset(ident16[:], 0.0))
            links.did(gp.memset(before[:], 1.0))
            links.did(gp.memset(upto[:], 1.0))
            links.did(gp.memset(ones_b[:], 1.0))
            links.did(gp.memset(ones_f[:], 1.0))
            links.did(gp.memset(mean_w[:], 1.0 / P))
            links.did(gp.memset(marks[:], 0.0))
            links.wait()
            for m in (ident, ident16):
                links.did(gp.affine_select(out=m[:], in_=m[:], compare_op=ALU.not_equal, fill=1.0, base=0,
                                           pattern=[[-1, P]], channel_multiplier=1))
            links.did(gp.affine_select(out=before[:], in_=before[:], compare_op=ALU.is_gt, fill=0.0, base=0,
                                       pattern=[[1, P]], channel_multiplier=-1))
            links.did(gp.affine_select(out=upto[:], in_=upto[:], compare_op=ALU.is_ge, fill=0.0, base=0,
                                       pattern=[[1, E], [-1, E]], channel_multiplier=0))
            links.did(gp.iota(part_i[:, 0:1], [[0, 1]], base=0, channel_multiplier=1))
            for dst, pat, mult in ((iota_e[:], [[1, E]], 0), (token2[:], [[2 * P, TILES]], 2),
                                   (base[:], [[REGION, E]], 0), (tile_no[:], [[1, SLOTS]], 0)):
                links.did(gp.iota(dst, pat, base=0, channel_multiplier=mult,
                                  allow_small_or_imprecise_dtypes=True))
            links.wait()
            gp.nop().then_inc(s_const, 1)
            for c in range(1, CHUNKS):
                words(c)
            pool.wait_ge(s_rv, CHUNKS)
            links.did(gp.memset(pads, 0.0))
            links.wait()
            links.did(gp.iota(pads[:, :, D + 1], [[TOP * P, PADS]], base=TOP * TOKENS, channel_multiplier=TOP,
                              allow_small_or_imprecise_dtypes=True))
            links.wait()
            gp.nop().then_inc(s_pads, 1)
            with pool.Fori(0, CHUNKS // 2) as i:
                for n in range(2):
                    pool.wait_ge(s_slot, i * 2 + (n + 1))
                    alone(pool)
                    for k in range(TOP):
                        for t in range(CH):
                            gp.indirect_dma_start(sorted_rows, bass.IndirectOffsetOnAxis(slot[n][:, k, t:t + 1], 0),
                                                  rows[n][:, t, :], None).then_inc(s_scat[n], 16)
            with pool.Fori(0, SLOTS // 4) as i:
                for q in range(4):
                    pool.wait_ge(s_ysb, i * 4 + (q + 1 + LEAD))
                    alone(pool)
                    gp.indirect_dma_start(y_rows, bass.IndirectOffsetOnAxis(y_to[q][:], 0),
                                          y_sb[q][:], None).then_inc(s_ysc[q], 16)

        @block.tensor
        def _(pe):
            pe.wait_ge(s_const, 2)
            pe.wait_ge(s_attw, 6 * 16)
            for m, (lo, n) in enumerate(((0, P), (P, D2))):
                last = mm(bank[7][0:n, m * D:(m + 1) * D], wq_sb[:, 0, lo:lo + n], wk_sb[:, 0, :], True, False)
                last = mm(bank[7][0:n, m * D:(m + 1) * D], wq_sb[0:D2, 1, lo:lo + n], wk_sb[0:D2, 1, :], False, True)
            last.then_inc(s_wqk, 1)
            pe.wait_ge(s_tab, 1)

            with pe.Fori(0, CHUNKS) as c:
                pe.wait_ge(s_oh, c + 1)
                for q in range(CH // 2):
                    pe.wait_ge(s_embadd, c * 4 + (q + 1))
                    for u in range(2):
                        dst = bank[q % 2][:, u * D:(u + 1) * D]
                        t = slice((2 * q + u) * P, (2 * q + u + 1) * P)
                        for n in range(3):
                            mm(dst, onehot[:, 0, t], tab_p[n][:, 0, :], n == 0, False)
                        last = mm(dst, onehot[:, 1, t], type_p[:], False, True)
                    last.then_inc(s_emb, 1)
                pe.wait_ge(s_rv, c + 1)
                mm(bank[2][:, 0:CH], mean_w[:], rowvar[:], True, True).then_inc(s_bv, 1)

            for n in range(3):
                pe.wait_ge(s_sqs, n + 1)
                mm(bank[3][:, n:n + 1], ones_f[:], sqs[:, n:n + 1], True, True).then_inc(s_sq, 1)

            xt, g, v, s, pT, o = bank[0], bank[1], bank[2], bank[4], bank[5], bank[6]
            for x in (s_xt, s_g, s_v, s_s, s_pt_, s_o):
                pe.sem_inc(x, LEAD)

            def transpose_xn(j, par):
                pe.wait_ge(s_xn, j + 1)
                pe.wait_ge(s_xtsb, j + LEAD)
                for u in range(2):
                    nc.tensor.transpose(xt[:, u * P:(u + 1) * P], xn[par][:, u, 0:P], ident[:])
                    last = nc.tensor.transpose(xt[0:D2, (2 + u) * P:(3 + u) * P], xn[par][:, u, P:D], ident[:])
                last.then_inc(s_xt, 1)

            def project(j, par):
                pe.wait_ge(s_xtsb, j + 1 + LEAD)
                pe.wait_ge(s_gsb, j + LEAD)
                for m, (lo, n) in enumerate(((0, P), (P, D2))):
                    dst = g[0:n, m * 2 * P:(m + 1) * 2 * P]
                    mm(dst, wqk[:, 0, lo:lo + n], xnT[par][:, 0, :], True, False)
                    last = mm(dst, wqk[0:D2, 1, lo:lo + n], xnT[par][0:D2, 1, :], False, True)
                last.then_inc(s_g, 1)
                pe.wait_ge(s_vsb, j + LEAD)
                for u in range(2):
                    dst = v[:, u * D:(u + 1) * D]
                    mm(dst, xnT[par][:, 0, u * P:(u + 1) * P], wv_sb[:, 0, :], True, False)
                    last = mm(dst, xnT[par][0:D2, 1, u * P:(u + 1) * P], wv_sb[0:D2, 1, :], False, True)
                last.then_inc(s_v, 1)

            def scores(j, par):
                pe.wait_ge(s_gsb, j + 1 + LEAD)
                pe.wait_ge(s_p, j + LEAD)
                for u in range(2):
                    dst, c = s[:, u * P:(u + 1) * P], slice(u * P, (u + 1) * P)
                    mm(dst, gT[par][:, 0, c], xnT[par][:, 0, c], True, False)
                    last = mm(dst, gT[par][0:D2, 1, c], xnT[par][0:D2, 1, c], False, True)
                last.then_inc(s_s, 1)

            def transpose_p(j, par):
                pe.wait_ge(s_p, j + 1 + LEAD)
                pe.wait_ge(s_ptsb, j + LEAD)
                for u in range(2):
                    last = nc.tensor.transpose(pT[:, u * P:(u + 1) * P], pr[par][:, u, :], ident[:])
                last.then_inc(s_pt_, 1)

            def attend(j, par):
                pe.wait_ge(s_ptsb, j + 1 + LEAD)
                pe.wait_ge(s_vsb, j + 1 + LEAD)
                pe.wait_ge(s_res, j + LEAD)
                for u in range(2):
                    last = mm(o[:, u * D:(u + 1) * D], prT[par][:, u, :], v_sb[par][:, u, :], True, True)
                last.then_inc(s_o, 1)

            pe.wait_ge(s_wqk_sb, 1)
            transpose_xn(0, 0)
            project(0, 0)
            transpose_xn(1, 1)

            def attention(j, par):
                fixed = isinstance(j, int)
                if not fixed or j < PAIRS:
                    scores(j, par)
                if not fixed or j > 0:
                    attend(j - 1, 1 - par)
                if not fixed or j + 1 < PAIRS:
                    project(j + 1, 1 - par)
                if not fixed or j < PAIRS:
                    transpose_p(j, par)
                if not fixed or j + 2 < PAIRS:
                    transpose_xn(j + 2, par)
            attention(0, 0)
            with pe.Fori(0, PAIRS // 2 - 2) as i:
                attention(i * 2 + 1, 1)
                attention(i * 2 + 2, 0)
            for j in range(PAIRS - 3, PAIRS + 1):
                attention(j, j % 2)

            pe.wait_ge(s_wlo, 3)
            x2t = bank[0][:].bitcast(fp16)
            with pe.Fori(0, CHUNKS // 2) as i:
                for n in range(2):
                    pe.wait_ge(s_rows, i * 2 + (n + 1))
                    for q in range(CH // 2):
                        pe.wait_ge(s_x2tsb, i * 8 + (n * 4 + q + 1))
                        for u in range(2):
                            for k in range(3):
                                at = (3 * u + k) * P
                                last = nc.tensor.transpose(x2t[:, at:at + P],
                                                           rows[n][:, 2 * q + u, k * P:(k + 1) * P], ident16[:])
                        last.then_inc(s_x2t, 1)
                    for t in range(CH):
                        if t % 2 == 0:
                            pe.wait_ge(s_x2tsb, i * 8 + (n * 4 + t // 2 + 2))
                        for k, (a, b) in enumerate(((0, 0), (1, 0), (0, 1), (2, 2), (2, 3))):
                            last = mm(bank[1][:, t * E:(t + 1) * E], x2T[:, t, a, :], rt[:, b, :], k == 0, k == 4)
                    last.then_inc(s_lg, 1)
                    pe.wait_ge(s_mk, i * 2 + (n + 1))
                    mm(bank[2][:, 0:(CH + 1) * E], before[:], marks[:].rearrange("p t e -> p (t e)"), True, False)
                    for t in range(CH):
                        more = CH - t
                        last = mm(bank[2][:, (t + 1) * E:(CH + 1) * E], ones_b[:],
                                  marks[:, t:t + 1, :].to_broadcast([P, more, E]), False, t == CH - 1)
                    last.then_inc(s_rk, 1)

            xt_b = bank[0][:].bitcast(fp16)
            h_b, ht_b, y_b = [bank[1], bank[2]], [bank[3], bank[4]], [bank[5], bank[6]]
            for x in (s_xft,):
                pe.sem_inc(x, 4)
            for x in (s_h1, s_ht, s_y):
                pe.sem_inc(x, LEAD)
            w1_f = w1[:].rearrange("p e a i -> p (e a i)")
            w2_f = w2[:].rearrange("p e c a d -> p (e c a d)")

            def experts(t, q, r):
                fixed = isinstance(t, int)
                if not fixed or 1 <= t <= SLOTS:
                    e = nc.tensor.value_load(e_i[0:1, bass.ds(t - 1, 1)], min_val=0, max_val=E - 1)
                    pe.wait_ge(s_xftsb, t + LEAD)
                    pe.wait_ge(s_hs, t - 1 + LEAD - 1)
                    for k, (a, b) in enumerate(((0, 0), (1, 0), (0, 1), (2, 2), (2, 3))):
                        last = mm(h_b[(q - 1) % 2][:], xT[(q - 1) % 2][:, a, :],
                                  w1_f[:, bass.ds(e * (4 * I) + b * I, I)], k == 0, k == 4)
                    last.then_inc(s_h1, 1)
                if not fixed or t < SLOTS:
                    pe.wait_ge(s_xin[q], r * 4 + 16)
                    pe.wait_ge(s_xftsb, t + LEAD)
                    for k in range(3):
                        last = nc.tensor.transpose(xt_b[:, k * P:(k + 1) * P], xin[q][:, k * P:(k + 1) * P], ident16[:])
                    last.then_inc(s_xft, 1)
                if not fixed or 3 <= t:
                    e = nc.tensor.value_load(e_i[0:1, bass.ds(t - 3, 1)], min_val=0, max_val=E - 1)
                    par = (q - 3) % 2
                    pe.wait_ge(s_lo, t - 3 + 1 + LEAD)
                    pe.wait_ge(s_ysb, t - 5 + 1 + LEAD)
                    for c in range(IC):
                        at = e * (IC * 2 * D) + c * 2 * D
                        mm(y_b[par][:, 0:2 * D], hT[par][:, 0, c, :], w2_f[:, bass.ds(at, 2 * D)], c == 0, False)
                        last = mm(y_b[par][:, 0:D], hT[par][:, 1, c, :], w2_f[:, bass.ds(at, D)], False, c == IC - 1)
                    last.then_inc(s_y, 1)
                if not fixed or 1 <= t <= SLOTS:
                    par = (q - 1) % 2
                    pe.wait_ge(s_hs, t + LEAD)
                    pe.wait_ge(s_lo, t - 1 + LEAD - 1)
                    for c in range(IC):
                        last = nc.tensor.transpose(ht_b[par][:, c * P:(c + 1) * P],
                                                   hs[par][:, c * P:(c + 1) * P], ident[:])
                    last.then_inc(s_ht, 1)
            pe.wait_ge(s_plan, 1)
            run_experts(pe, experts)
            mm(bank[7][:, 0:TILES * E], ones_f[:], probs[:].rearrange("p t e -> p (t e)"), True, True)\
                .then_inc(s_imp, 1)

        @block.vector
        def _(dve):
            ve = nc.vector
            links = Steps(dve, s_vc)
            did, wait = links.did, links.wait

            def newton(dst, var, n, eps):
                v, y, t = nv[:, 0:n], ny[:, 0:n], nt[:, 0:n]
                did(ve.tensor_scalar(v, var, eps, None, ALU.add)); wait()
                did(ve.tensor_scalar(y.bitcast(i32), v.bitcast(i32), -0.5, float(0x5F3759DF), ALU.mult, ALU.add)); wait()
                for k in range(3):
                    did(ve.tensor_tensor(t, y, y, ALU.mult)); wait()
                    did(ve.scalar_tensor_tensor(out=t, in0=t, scalar=-0.5, in1=v, op0=ALU.mult, op1=ALU.mult)); wait()
                    did(ve.scalar_tensor_tensor(out=dst if k == 2 else y, in0=t, scalar=1.5, in1=y,
                                                op0=ALU.add, op1=ALU.mult)); wait()

            dve.wait_ge(s_const, 2)
            dve.wait_ge(s_small, 64)
            did(ve.tensor_copy(tab_p[0][:], tab[:])); wait()
            did(ve.tensor_tensor(tab_r[:], tab[:], tab_p[0][:], ALU.subtract)); wait()
            did(ve.tensor_copy(tab_p[1][:], tab_r[:])); wait()
            did(ve.tensor_tensor(tab_r[:], tab_r[:], tab_p[1][:], ALU.subtract)); wait()
            did(ve.tensor_copy(tab_p[2][:], tab_r[:]))
            did(ve.memset(type_p[:], 0.0)); wait()
            for n in range(3):
                did(ve.tensor_copy(type_p[32 * n:32 * n + 2, :], tab_p[n][32 * n:32 * n + 2, 1, :]))
            did(ve.tensor_scalar(part_i[:, 1:2], part_i[:, 0:1], 31, None, ALU.bitwise_and)); wait()
            did(ve.tensor_copy(part[:], part_i[:])); wait()
            ve.nop().then_inc(s_tab, 1)
            dve.wait_ge(s_wqk, 1)
            did(ve.tensor_copy(wqk[:, 0, :], bank[7][:, 0:D]))
            ve.tensor_copy(wqk[0:D2, 1, :], bank[7][0:D2, D:2 * D]).then_inc(s_wqk_sb, 1)
            dve.wait_ge(s_gb, 32)

            dve.sem_inc(s_embadd, 2)
            with dve.Fori(0, CHUNKS // 2) as i:
                links.round(i, 2 * (6 * CH + CH // 2 + 3 * NL + 5))
                for n in range(2):
                    c = i * 2 + n
                    dve.wait_ge(s_pt, i * 64 + (n + 1) * 32)
                    did(ve.tensor_scalar(onehot[:, 0, :], pt_ids[:, 0, :], part[:, 0:1], None, ALU.is_equal))
                    did(ve.tensor_scalar(onehot[:, 1, :], pt_ids[:, 1, :], part[:, 1:2], None, ALU.is_equal))
                    wait()
                    ve.nop().then_inc(s_oh, 1)
                    tiles = bass.ds(c * CH, CH)
                    dve.wait_ge(s_word[n], (i + 1) * (16 * CH))
                    for q in range(CH // 2):
                        two = bass.ds(c * CH + 2 * q, 2)
                        dve.wait_ge(s_emb, i * 8 + (n * 4 + q + 1))
                        did(ve.tensor_tensor(word[:, two, :], word[:, two, :],
                                             bank[q % 2][:, 0:2 * D].rearrange("p (u d) -> p u d", u=2), ALU.add))
                        wait()
                        ve.nop().then_inc(s_embadd, 1)
                        for u in range(2):
                            did(ve.bn_stats(st[:, 2 * q + u, :], word[:, c * CH + (2 * q + u), :]))
                    wait()
                    alone(dve)
                    for t in range(CH):
                        did(ve.bn_aggr(mv[:, t, :], st[:, t, :]))
                    wait()
                    newton(rstd1[:], mv[:, :, 1], CH, 1e-12)
                    for t in range(CH):
                        did(ve.scalar_tensor_tensor(out=word[:, c * CH + t, :], in0=word[:, c * CH + t, :],
                                                    scalar=mv[:, t, 0:1], in1=gb[:, 0, :],
                                                    op0=ALU.subtract, op1=ALU.mult))
                    wait()
                    for t in range(CH):
                        did(ve.scalar_tensor_tensor(out=h[:, c * CH + t, :], in0=word[:, c * CH + t, :],
                                                    scalar=rstd1[:, t:t + 1], in1=gb[:, 1, :],
                                                    op0=ALU.mult, op1=ALU.add))
                    wait()
                    alone(dve)
                    for t in range(CH):
                        did(ve.bn_stats(st[:, t, :], h[:, c * CH + t, :]))
                    wait()
                    alone(dve)
                    for t in range(CH):
                        did(ve.bn_aggr(mv[:, t, :], st[:, t, :]))
                    wait()
                    newton(rstd1[:], mv[:, :, 1], CH, 1e-5)
                    did(ve.tensor_tensor(nt[:], rstd1[:], rstd1[:], ALU.mult)); wait()
                    ve.tensor_tensor(rowvar[:], nt[:], mv[:, :, 1], ALU.mult).then_inc(s_rv, 1)
                    did(ve.tensor_copy(mean1[:, tiles], mv[:, :, 0]))
                    dve.wait_ge(s_bv, i * 2 + (n + 1))
                    newton(rowvar[:], bank[2][:, 0:CH], CH, 1e-5)
                    did(ve.tensor_tensor(coef1[:, tiles], rstd1[:], rowvar[:], ALU.mult)); wait()
            links.end(CHUNKS // 2)

            u0, sh = scale_i, 23
            sc = scale[:].bitcast(i32)

            def exponent(dst, src, mul, add):
                did(ve.tensor_scalar(dst, src, mul, add, ALU.mult, ALU.add)); wait()
                did(ve.tensor_scalar(dst, dst, sh, None, ALU.arith_shift_left)); wait()

            def scales(n):
                dve.wait_ge(s_sq, n + 1)
                u = u0[:, n, 0:1]
                did(ve.tensor_copy(sqs[:, n:n + 1], bank[3][:, n:n + 1])); wait()
                did(ve.tensor_scalar(u, sqs[:, n:n + 1].bitcast(i32), 24, None, ALU.logical_shift_right)); wait()
                return u

            def low(dst, src, hi, by):
                return ve.scalar_tensor_tensor(out=dst, in0=src, scalar=by, in1=hi, op0=ALU.mult, op1=ALU.subtract)

            def summed(n, cols):
                dve.wait_ge(s_ac, (16, 32, 33)[n])
                ve.reduce_sum(sqs[:, n:n + 1], sq[:, n, 0:cols], axis=AX).then_inc(s_sqs, 1)

            summed(0, 16)
            u = scales(0)
            exponent(sc[:, 0:1], u, -1.0, 202.0)
            exponent(sc[:, 1:2], u, 1.0, 52.0)
            exponent(sc[:, 4:5], u, -1.0, 198.0)
            exponent(sc[:, 5:6], u, 1.0, 56.0)
            ve.nop().then_inc(s_scale, 1)
            dve.wait_ge(s_whi, 1)
            for e in range(E):
                for k in range(2):
                    did(low(w1[:, e, 2 * k + 1, :], stage[:, e, k, :], w1[:, e, 2 * k, :], scale[:, 0:1]))
            wait()
            ve.nop().then_inc(s_wlo, 1)
            summed(1, 16)
            u = scales(1)
            exponent(sc[:, 2:3], u, -1.0, 202.0)
            exponent(sc[:, 3:4], u, 1.0, 52.0)
            did(ve.tensor_tensor(scale[:, 6:7], scale[:, 3:4], scale[:, 5:6], ALU.mult)); wait()
            ve.nop().then_inc(s_scale, 1)
            dve.wait_ge(s_whi, 2)
            w2_s = stage[:].rearrange("p e a i -> p (e a i)")[:, 0:E * IC * D].rearrange("p (e c d) -> p e c d", e=E, c=IC)
            for e in range(E):
                did(low(w2[:, e, :, 1, :], w2_s[:, e], w2[:, e, :, 0, :], scale[:, 2:3]))
            wait()
            ve.nop().then_inc(s_wlo, 1)
            summed(2, 1)
            u = scales(2)
            exponent(sqs[:, 0:1].bitcast(i32), u, -1.0, 202.0)
            exponent(sc[:, 7:8], u, 1.0, 52.0)
            for k in range(2):
                did(ve.tensor_scalar(rt[:, 2 * k, :], rt_f[:, k, :], sqs[:, 0:1], None, ALU.mult))
            wait()
            for k in range(2):
                did(low(rt[:, 2 * k + 1, :], rt_f[:, k, :], rt[:, 2 * k, :], sqs[:, 0:1]))
            wait()
            ve.nop().then_inc(s_wlo, 1)

            for x in (s_vsb, s_res):
                dve.sem_inc(x, LEAD)

            def normalise(j, par):
                dve.wait_ge(s_xt, j + 1)
                for u in range(2):
                    did(ve.tensor_scalar(xn[par][:, u, :], h[:, j * 2 + u, :], mean1[:, bass.ds(j * 2 + u, 1)],
                                         coef1[:, bass.ds(j * 2 + u, 1)], ALU.subtract, ALU.mult))
                wait()
                ve.nop().then_inc(s_xn, 1)

            def keep_v(j, par):
                dve.wait_ge(s_v, j + 1 + LEAD)
                dve.wait_ge(s_o, j + 1)
                ve.tensor_copy(v_sb[par][:], bank[2][:, 0:2 * D].rearrange("p (u d) -> p u d", u=2)).then_inc(s_vsb, 1)

            def residual(j, par):
                dve.wait_ge(s_p, j + 1 + LEAD)
                did(ve.reciprocal(rinv[par][:], rsum[par][:])); wait()
                dve.wait_ge(s_o, j + 1 + LEAD)
                for u in range(2):
                    did(ve.scalar_tensor_tensor(out=h[:, j * 2 + u, :], in0=bank[6][:, u * D:(u + 1) * D],
                                                scalar=rinv[par][:, u:u + 1], in1=h[:, j * 2 + u, :],
                                                op0=ALU.mult, op1=ALU.add))
                wait()
                ve.nop().then_inc(s_res, 1)
                for u in range(2):
                    did(ve.bn_stats(st2[par][:, u, :], h[:, j * 2 + u, :]))
                wait()
                alone(dve)
                for u in range(2):
                    did(ve.bn_aggr(mvp[:, u, :], st2[par][:, u, :]))
                wait()
                did(ve.tensor_copy(mv2[:, bass.ds(j * 2, 2), :], mvp[:]))

            def attention(j, par):
                fixed = isinstance(j, int)
                if not fixed or j < PAIRS:
                    dve.wait_ge(s_s, j + 1 + LEAD)
                    ve.tensor_reduce(nmax[par][:], bank[4][:, 0:2 * P].rearrange("p (u k) -> p u k", u=2),
                                     axis=AX, op=ALU.max, negate=True).then_inc(s_max, 1)
                if not fixed or j + 1 < PAIRS:
                    keep_v(j + 1, 1 - par)
                if not fixed or j + 3 < PAIRS:
                    normalise(j + 3, 1 - par)
                if not fixed or j > 0:
                    residual(j - 1, 1 - par)
            for j in range(3):
                normalise(j, j % 2)
                if j == 0:
                    keep_v(0, 0)
            attention(0, 0)
            with dve.Fori(0, PAIRS // 2 - 2) as i:
                links.round(i, 2 * (2 + 1 + 7))
                attention(i * 2 + 1, 1)
                attention(i * 2 + 2, 0)
            links.end(PAIRS // 2 - 2)
            for j in range(PAIRS - 3, PAIRS + 1):
                attention(j, j % 2)
            wait()

            with dve.Fori(0, CHUNKS // 2) as i:
                links.round(i, 2 * (NL + 3 * CH + 22))
                for n in range(2):
                    c = i * 2 + n
                    tiles = bass.ds(c * CH, CH)
                    newton(rstd1[:], mv2[:, tiles, 1], CH, 1e-5)
                    for t in range(CH):
                        did(ve.tensor_scalar(x2[:, t, :], h[:, c * CH + t, :], mv2[:, c * CH + t, 0:1],
                                             rstd1[:, t:t + 1], ALU.subtract, ALU.mult))
                    dve.wait_ge(s_scat[n], i * (16 * TOP * CH))
                    wait()
                    r = rows[n]
                    segs = ((0, P, 0, P), (P, D, 2 * P, 2 * P + D2))
                    for a, b, lo, hi in segs:
                        did(ve.tensor_copy(r[:, :, lo:hi], x2[:, :, a:b]))
                    wait()
                    for a, b, lo, hi in segs:
                        did(ve.tensor_tensor(r[:, :, lo + b - a:hi + b - a], x2[:, :, a:b], r[:, :, lo:hi], ALU.subtract))
                    wait()
                    ve.nop().then_inc(s_rows, 1)
                    dve.wait_ge(s_lg, i * 2 + (n + 1))
                    lgp = bank[1][:, 0:CH * E].rearrange("p (t e) -> p t e", t=CH)
                    did(ve.tensor_reduce(lmax[:], lgp, axis=AX, op=ALU.max)); wait()
                    did(ve.tensor_tensor(lg[:], lgp, lmax[:].unsqueeze(2).to_broadcast([P, CH, E]), ALU.subtract)); wait()
                    ve.nop().then_inc(s_lgx, 1)
                    dve.wait_ge(s_ex, i * 2 + (n + 1))
                    did(ve.reduce_sum(esum[:], lg[:], axis=AX)); wait()
                    did(ve.reciprocal(lmax[:], esum[:])); wait()
                    did(ve.tensor_tensor(lg[:], lg[:], lmax[:].unsqueeze(2).to_broadcast([P, CH, E]), ALU.mult))
                    wait()
                    did(ve.tensor_copy(probs[:, tiles, :], lg[:]))
                    for t in range(CH):
                        did(ve.max(top8[:, t, :], lg[:, t, :]))
                    wait()
                    alone(dve)
                    for t in range(CH):
                        did(ve.max_index(idx8[:, t, :], top8[:, t, :], lg[:, t, :]))
                    wait()
                    did(ve.tensor_copy(idxf[:], idx8[:, :, 0:TOP]))
                    wait()
                    for k in range(TOP):
                        did(ve.tensor_tensor(picked[:, k, tiles, :], iota_e[:].unsqueeze(1).to_broadcast([P, CH, E]),
                                             idxf[:, :, k:k + 1].to_broadcast([P, CH, E]), ALU.is_equal))
                    meta = r[:].bitcast(fp32)
                    did(ve.tensor_copy(meta[:, :, D], idxf[:, :, 0]))
                    did(ve.tensor_copy(meta[:, :, D + 1], token2[:, tiles]))
                    did(ve.tensor_copy(top_p[:, :, tiles].rearrange("p k t -> p t k"), top8[:, :, 0:TOP]))
                    wait()
                    did(ve.tensor_tensor(marks[:, 0:CH, :], picked[:, 0, tiles, :], picked[:, 1, tiles, :], ALU.add))
                    wait()
                    ve.nop().then_inc(s_mk, 1)
                    dve.wait_ge(s_rk, i * 2 + (n + 1))
                    rk = bank[2][:, 0:(CH + 1) * E].rearrange("p (t e) -> p t e", e=E)
                    did(ve.tensor_tensor(place[:], rk[:, 0:CH, :], base[:].unsqueeze(1).to_broadcast([P, CH, E]), ALU.add))
                    wait()
                    for k in range(TOP):
                        did(ve.tensor_tensor(place_k[:, k, :, :], place[:], picked[:, k, tiles, :], ALU.mult))
                    did(ve.tensor_tensor(base[:], base[:], rk[:, CH, :], ALU.add))
                    wait()
                    did(ve.reduce_sum(slot_f[:], place_k[:], axis=AX)); wait()
                    ve.tensor_copy(slot[n][:], slot_f[:]).then_inc(s_slot, 1)
            links.end(CHUNKS // 2)

            wait()
            did(ve.tensor_copy(base_i[:], base[:]))
            did(ve.tensor_scalar(cnt[:], iota_e[:], float(-REGION), float(P - 1), ALU.mult, ALU.add)); wait()
            did(ve.tensor_tensor(cnt_i[:], base[:], cnt[:], ALU.add)); wait()
            did(ve.tensor_scalar(cnt_i[:], cnt_i[:], 7, None, ALU.logical_shift_right)); wait()
            did(ve.tensor_copy(tiles_e[:], cnt_i[:])); wait()
            did(ve.tensor_tensor(upto[:], upto[:], tiles_e[:].unsqueeze(1).to_broadcast([P, E, E]), ALU.mult))
            did(ve.tensor_scalar(jump[:], tiles_e[:], float(-P), float(REGION), ALU.mult, ALU.add)); wait()
            did(ve.reduce_sum(last_e[:], upto[:], axis=AX)); wait()
            did(ve.tensor_tensor(passed[:], tile_no[:].unsqueeze(2).to_broadcast([P, SLOTS, E]),
                                 last_e[:].unsqueeze(1).to_broadcast([P, SLOTS, E]), ALU.is_ge)); wait()
            did(ve.reduce_sum(e_f[:], passed[:], axis=AX)); wait()
            did(ve.tensor_scalar(e_f[:], e_f[:], float(E - 1), None, ALU.min))
            did(ve.tensor_tensor(passed[:], passed[:], jump[:].unsqueeze(1).to_broadcast([P, SLOTS, E]), ALU.mult)); wait()
            did(ve.tensor_copy(e_i[:], e_f[:]))
            did(ve.reduce_sum(row_f[:], passed[:], axis=AX)); wait()
            did(ve.scalar_tensor_tensor(out=row_i[:], in0=tile_no[:], scalar=float(P), in1=row_f[:],
                                        op0=ALU.mult, op1=ALU.add)); wait()
            ve.nop().then_inc(s_plan, 1)

            dve.sem_inc(s_lo, LEAD)
            dve.sem_inc(s_ysb, LEAD)
            dve.sem_inc(s_to, 4)

            def experts(t, q, r):
                fixed = isinstance(t, int)
                if not fixed or t >= 3:
                    m = (q - 3) % 4
                    dve.wait_ge(s_y, t - 3 + 1 + LEAD)
                    dve.wait_ge(s_ylo, t - 3 + 1)
                    k = r - (4 if q < 3 else 0)
                    dve.wait_ge(s_ysc[m], k * 4)
                    ve.scalar_tensor_tensor(out=y_sb[m][:], in0=bank[5 + m % 2][:, 0:D], scalar=scale[:, 6:7],
                                            in1=y_lo[m % 2][:], op0=ALU.mult, op1=ALU.add).then_inc(s_ysb, 1)
                if not fixed or t < SLOTS:
                    dve.wait_ge(s_xin[q], r * 4 + 16)
                    dve.wait_ge(s_ysc[q], r * 4)
                    meta = xin[q][:].bitcast(fp32)
                    ve.tensor_scalar(y_to[q][:], meta[:, D:D + 1], e_f[:, bass.ds(t, 1)], meta[:, D + 1:D + 2],
                                     ALU.not_equal, ALU.add).then_inc(s_to, 1)
                if not fixed or 1 <= t <= SLOTS:
                    par = (q - 1) % 2
                    dve.wait_ge(s_hi, t)
                    ve.scalar_tensor_tensor(out=hT[par][:, 1, :, :], in0=bank[3 + par][:].rearrange("p (c k) -> p c k", c=IC),
                                            scalar=scale[:, 4:5], in1=hT[par][:, 0, :, :],
                                            op0=ALU.mult, op1=ALU.subtract).then_inc(s_lo, 1)
            run_experts(dve, experts)

            dve.wait_ge(s_imp, 1)
            did(ve.tensor_reduce(imp[:], bank[7][:, 0:TILES * E].rearrange("p (t e) -> p e t", e=E),
                                 axis=AX, op=ALU.add)); wait()
            did(ve.tensor_scalar(imp[:], imp[:], -1.0, 1.0 - 0.9, ALU.add, ALU.mult)); wait()
            did(ve.tensor_scalar(imp[:], imp[:], 1.0, 0.01, ALU.add, ALU.add)); wait()
            for k in range(TOP):
                did(ve.tensor_tensor(bal[:, k], picked[:, k], imp[:].unsqueeze(1).to_broadcast([P, TILES, E]), ALU.mult))
            wait()
            did(ve.reduce_sum(wgt[:], bal[:], axis=AX)); wait()
            did(ve.reciprocal(wgt[:], wgt[:])); wait()
            did(ve.tensor_tensor(wgt[:], wgt[:], top_p[:], ALU.mult)); wait()
            did(ve.tensor_tensor(wsum[:], wgt[:, 0, :], wgt[:, 1, :], ALU.add)); wait()
            did(ve.reciprocal(wsum[:], wsum[:])); wait()
            did(ve.tensor_tensor(wgt[:], wgt[:], wsum[:].unsqueeze(1).to_broadcast([P, TOP, TILES]), ALU.mult)); wait()
            for g in range(TILES // 4):
                dve.wait_ge(s_back[g % 4], 16 * (g // 4 + 1))
                for k in range(TOP):
                    for u in range(4):
                        t = 4 * g + u
                        did(ve.scalar_tensor_tensor(out=h[:, t, :], in0=back[g % 4][:, u, k, :],
                                                    scalar=wgt[:, k, t:t + 1], in1=h[:, t, :],
                                                    op0=ALU.mult, op1=ALU.add))
                    wait()
                ve.nop().then_inc(s_fin, 1)

        @block.scalar
        def _(act):
            ac = nc.scalar

            def square_room(n):
                if n >= 2:
                    act.wait_ge(s_ac, n - 1)

            act.wait_ge(s_w1in, 48)
            for e in range(E):
                for k in range(2):
                    n = 2 * e + k
                    square_room(n)
                    ac.activation(hs[n % 2][:], stage[:, e, k, :], ACT.Square,
                                  accum_out=sq[:, 0, n:n + 1]).then_inc(s_ac, 1)
            act.wait_ge(s_scale, 1)
            for e in range(E):
                for k in range(2):
                    last = ac.activation(w1[:, e, 2 * k, :], stage[:, e, k, :], ACT.Copy, scale=scale[:, 0:1])
            last.then_inc(s_whi, 1)
            act.wait_ge(s_w2in, 16)
            w2_s = stage[:].rearrange("p e a i -> p (e a i)")[:, 0:E * IC * D].rearrange("p (e c d) -> p e c d", e=E, c=IC)
            for e in range(E):
                for k in range(2):
                    square_room(16 + 2 * e + k)
                    ac.activation(hs[k][:, 0:2 * D].rearrange("p (c d) -> p c d", c=2),
                                  w2_s[:, e, 2 * k:2 * k + 2], ACT.Square,
                                  accum_out=sq[:, 1, 2 * e + k:2 * e + k + 1]).then_inc(s_ac, 1)
            act.wait_ge(s_rin, 48)
            square_room(32)
            ac.activation(hs[0][:, 0:2 * E], rt_f[:].rearrange("p a e -> p (a e)"), ACT.Square,
                          accum_out=sq[:, 2, 0:1]).then_inc(s_ac, 1)
            act.wait_ge(s_scale, 2)
            for e in range(E):
                last = ac.activation(w2[:, e, :, 0, :], w2_s[:, e], ACT.Copy, scale=scale[:, 2:3])
            last.then_inc(s_whi, 1)

            for x in (s_xtsb, s_gsb, s_p, s_ptsb):
                act.sem_inc(x, LEAD)

            def keep_xnT(j, par):
                act.wait_ge(s_xt, j + 1 + LEAD)
                act.wait_ge(s_s, j + 1)
                ac.copy(xnT[par][:, 0, :], bank[0][:, 0:2 * P])
                ac.copy(xnT[par][0:D2, 1, :], bank[0][0:D2, 2 * P:4 * P]).then_inc(s_xtsb, 1)

            def keep_g(j, par):
                act.wait_ge(s_g, j + 1 + LEAD)
                act.wait_ge(s_s, j + 1)
                ac.copy(gT[par][:, 0, :], bank[1][:, 0:2 * P])
                ac.copy(gT[par][0:D2, 1, :], bank[1][0:D2, 2 * P:4 * P]).then_inc(s_gsb, 1)

            keep_xnT(0, 0)
            keep_g(0, 0)
            keep_xnT(1, 1)

            def attention(j, par):
                fixed = isinstance(j, int)
                if not fixed or j < PAIRS:
                    act.wait_ge(s_max, j + 1)
                    act.wait_ge(s_pt_, j + 1)
                    for u in range(2):
                        last = ac.activation(pr[par][:, u, :], bank[4][:, u * P:(u + 1) * P], ACT.Exp,
                                             bias=nmax[par][:, u:u + 1], accum_out=rsum[par][:, u:u + 1])
                    last.then_inc(s_p, 1)
                if not fixed or j + 1 < PAIRS:
                    keep_g(j + 1, 1 - par)
                if not fixed or j < PAIRS:
                    act.wait_ge(s_pt_, j + 1 + LEAD)
                    act.wait_ge(s_o, j + 1)
                    ac.copy(prT[par][:].rearrange("p u k -> p (u k)"), bank[5][:, 0:2 * P]).then_inc(s_ptsb, 1)
                if not fixed or j + 2 < PAIRS:
                    keep_xnT(j + 2, par)
            attention(0, 0)
            with act.Fori(0, PAIRS // 2 - 2) as i:
                attention(i * 2 + 1, 1)
                attention(i * 2 + 2, 0)
            for j in range(PAIRS - 3, PAIRS):
                attention(j, j % 2)

            act.sem_inc(s_x2tsb, 1)
            x2t = bank[0][:].bitcast(fp16)
            with act.Fori(0, CHUNKS // 2) as i:
                for n in range(2):
                    for q in range(CH // 2):
                        act.wait_ge(s_x2t, i * 8 + (n * 4 + q + 1))
                        ac.copy(x2T[:, 2 * q:2 * q + 2, :, :].rearrange("p u k t -> p (u k t)"), x2t[:, 0:6 * P])\
                          .then_inc(s_x2tsb, 1)
                    act.wait_ge(s_lgx, i * 2 + (n + 1))
                    ac.activation(lg[:], lg[:], ACT.Exp, scale=scale[:, 7:8]).then_inc(s_ex, 1)

            for x in (s_xftsb, s_hs):
                act.sem_inc(x, LEAD)

            def experts(t, q, r):
                fixed = isinstance(t, int)
                if not fixed or 1 <= t <= SLOTS:
                    par = (q - 1) % 2
                    act.wait_ge(s_h1, t + LEAD)
                    act.wait_ge(s_ht, t - 1 + LEAD - 1)
                    ac.activation(hs[par][:], bank[1 + par][:], ACT.Silu, scale=scale[:, 1:2]).then_inc(s_hs, 1)
                if not fixed or t < SLOTS:
                    act.wait_ge(s_xft, t + 1 + 4)
                    act.wait_ge(s_h1, t + 1)
                    ac.copy(xT[q % 2][:].rearrange("p k t -> p (k t)"), bank[0][:].bitcast(fp16)[:, 0:3 * P])\
                      .then_inc(s_xftsb, 1)
                if not fixed or t >= 3:
                    par = (q - 3) % 2
                    act.wait_ge(s_y, t - 3 + 1 + LEAD)
                    act.wait_ge(s_ysb, t - 5 + 1 + LEAD)
                    ac.activation(y_lo[par][:], bank[5 + par][:, D:2 * D], ACT.Copy, scale=scale[:, 6:7]).then_inc(s_ylo, 1)
                if not fixed or 1 <= t <= SLOTS:
                    par = (q - 1) % 2
                    act.wait_ge(s_ht, t + LEAD)
                    act.wait_ge(s_y, t)
                    ac.activation(hT[par][:, 0, :, :].rearrange("p c k -> p (c k)"), bank[3 + par][:], ACT.Copy,
                                  scale=scale[:, 4:5]).then_inc(s_hi, 1)
            run_experts(act, experts)
            out_v = out.rearrange("b p d -> p b d")
            for g in range(TILES // 4):
                act.wait_ge(s_fin, g + 1)
                act.dma_start(out_v[:, 4 * g:4 * g + 4, :], h[:, 4 * g:4 * g + 4, :]).then_inc(s_out[g % 4], 16)
            for g in range(4):
                act.wait_ge(s_out[g], 32)


def kernel(x, mask_BS_i1_0, pos_BS, L0_tok_word_emb, L0_tok_pos_emb, L0_tok_type_emb, L0_tok_gamma,
           L0_tok_beta, L0_attn_Wk, L0_attn_Wq, L0_attn_Wv, L0_ffn_router_w, L0_ffn_w1, L0_ffn_w2):
    import numpy as np
    import concourse.bacc as bacc
    from concourse.bass_utils import run_bass_kernel_spmd

    B, S = x.shape
    E, I, D = L0_ffn_w1.shape
    w2 = np.asarray(L0_ffn_w2).reshape(E, D, I // 128, 128)
    arrays = {
        "ids": np.asarray(x).T,
        "pos_ids": np.asarray(pos_BS).reshape(1, B * S),
        "type_ids": np.asarray(mask_BS_i1_0).reshape(1, B * S),
        "word_emb": np.asarray(L0_tok_word_emb),
        "pos_emb": np.asarray(L0_tok_pos_emb),
        "type_emb": np.asarray(L0_tok_type_emb),
        "gamma": np.asarray(L0_tok_gamma).reshape(1, D),
        "beta": np.asarray(L0_tok_beta).reshape(1, D),
        "wq": np.asarray(L0_attn_Wq),
        "wk": np.asarray(L0_attn_Wk),
        "wv_t": np.asarray(L0_attn_Wv).T,
        "router_t": np.asarray(L0_ffn_router_w).T,
        "w1_t": np.asarray(L0_ffn_w1).transpose(2, 0, 1).reshape(D, E * I),
        "w2_t": w2.transpose(3, 0, 2, 1).reshape(128, E * (I // 128) * D),
    }
    arrays = {k: np.ascontiguousarray(v) for k, v in arrays.items()}
    nc = bacc.Bacc("TRN2", target_bir_lowering=False, num_devices=1)
    args = [nc.dram_tensor(k, v.shape, mybir.dt.from_np(v.dtype), kind="ExternalInput").ap()
            for k, v in arrays.items()]
    out = nc.dram_tensor("out", (B, S, D), mybir.dt.float32, kind="ExternalOutput").ap()
    tower_kernel(nc, *args, out)
    r = run_bass_kernel_spmd(nc, [arrays], core_ids=[0])
    return r.results[0]["out"]
```

```python
import concourse.bass as bass
from concourse import mybir
from contextlib import ExitStack


def tower_kernel(nc, ids, pt_rows, word_emb, pos_emb, type_emb, gamma, beta,
                 wq, wk, wv_t, router_t, w1_t, w2_t, out):
    fp32, fp16, bf16, i32, u32 = (mybir.dt.float32, mybir.dt.float16, mybir.dt.bfloat16,
                                  mybir.dt.int32, mybir.dt.uint32)
    ALU = mybir.AluOpType
    ACT = mybir.ActivationFunctionType
    AX = mybir.AxisListType.X

    P = 128
    D = word_emb.shape[1]
    D2 = D - P
    TILES = ids.shape[1]
    TOKENS = TILES * P
    E = router_t.shape[1]
    I = w1_t.shape[1] // E
    IC = I // P
    TOP = 2
    CH = 4
    CHUNKS = TILES // CH
    PAIRS = TILES // 2
    XC = 2 * D
    ROW = XC + 4
    REGION = TOKENS + P
    SLOTS = (TOP * TOKENS + E * (P - 1)) // P
    SLOTS = SLOTS + (-SLOTS) % 4
    REST = E * P
    PADS = 2 * E
    TRASH = PADS * TOP * P
    LEAD = 2

    ctx = ExitStack()
    with ctx:
        def sb(name, shape, dt=fp32):
            return ctx.enter_context(nc.sbuf_tensor(name, shape, dt))

        def sem(name):
            return ctx.enter_context(nc.semaphore(name))

        sorted_rows = nc.dram_tensor("sorted_rows", (E * REGION + REST, ROW), fp16, kind="Internal").ap()
        y_rows = nc.dram_tensor("y_rows", (TOP * TOKENS + TRASH, D), fp32, kind="Internal").ap()

        stage = sb("stage", [P, E, 2, I])
        carved = [0]

        def carve(shape, dt=fp32):
            n = 1
            for x in shape:
                n *= x
            words = n if dt == fp32 else n // 2
            at, carved[0] = carved[0], carved[0] + words
            ap = stage[:].rearrange("p e a i -> p (e a i)")[:, at:at + words]
            ap = ap if dt == fp32 else ap.bitcast(dt)
            names = " ".join("abc"[:len(shape)])
            return ap.rearrange(f"p ({names}) -> p {names}", **dict(zip("abc", shape))) if len(shape) > 1 else ap

        ident = sb("ident", [P, P])
        ident16 = sb("ident16", [P, P], fp16)
        before = sb("before", [P, P], bf16)
        ones_b = sb("ones_b", [P, P], bf16)
        mean_w = sb("mean_w", [P, P])
        ones_f = sb("ones_f", [P, P])
        part = sb("part", [P, 2])
        part_i = sb("part_i", [P, 2], i32)
        iota_e = sb("iota_e", [P, E])
        token2 = sb("token2", [P, TILES])
        base = sb("base", [P, E])
        upto = sb("upto", [P, E, E])
        tile_no = sb("tile_no", [P, SLOTS])
        ids_sb = sb("ids_sb", [P, TILES], i32)
        gb = sb("gb", [P, 2, D])
        tab = sb("tab", [P, 2, D])
        tab_p = [sb(f"tab_p{n}", [P, 2, D], bf16) for n in range(3)]
        type_p = sb("type_p", [P, D], bf16)
        pt_ids = [sb(f"pt_ids{n}", [P, 2, CH * P], i32) for n in range(2)]
        onehot = sb("onehot", [P, 2, CH * P], bf16)
        h = sb("h", [P, TILES, D])
        word = sb("word", [P, TILES, D])
        st_w = sb("st_w", [P, CH, 6])
        mv_w = sb("mv_w", [P, CH, 2])
        st_h = sb("st_h", [P, CH, 6])
        mv_h = sb("mv_h", [P, CH, 2])
        eps = sb("eps", [P, 2])
        root_ln = sb("root_ln", [P, 4, CH])
        root_0 = sb("root_0", [P, 4, CH])
        root_t = sb("root_t", [P, 4, CH])
        root = sb("root", [P, 4, CH])
        batch_var = sb("batch_var", [P, CH])
        rowvar = sb("rowvar", [P, CH])
        coef1 = sb("coef1", [P, TILES])
        shift1 = sb("shift1", [P, TILES])
        shift2 = sb("shift2", [P, CH])
        mv2 = sb("mv2", [P, TILES, 2])
        wq_sb = sb("wq_sb", [P, 2, D])
        wk_sb = sb("wk_sb", [P, 2, D])
        wv_sb = sb("wv_sb", [P, 2, D])
        wqk = sb("wqk", [P, 2, D])
        xn = [sb(f"xn{n}", [P, 2, D]) for n in range(2)]
        xnT = [sb(f"xnT{n}", [P, 2, 2 * P]) for n in range(2)]
        gT = [sb(f"gT{n}", [P, 2, 2 * P]) for n in range(2)]
        v_sb = [sb(f"v_sb{n}", [P, 2, D]) for n in range(2)]
        tab_r = v_sb[0]
        pr = [sb(f"pr{n}", [P, 2, P]) for n in range(2)]
        prT = [sb(f"prT{n}", [P, 2, P]) for n in range(2)]
        nmax = [sb(f"nmax{n}", [P, 2]) for n in range(2)]
        rsum = [sb(f"rsum{n}", [P, 2]) for n in range(2)]
        rinv = [sb(f"rinv{n}", [P, 2]) for n in range(2)]
        st2 = [sb(f"st2{n}", [P, 2, 6]) for n in range(2)]
        x2 = sb("x2", [P, CH, D])
        rows = [sb(f"rows{n}", [P, CH, ROW], fp16) for n in range(4)]
        x2T = sb("x2T", [P, CH, 3, P], fp16)
        rt_f = sb("rt_f", [P, 2, E])
        rt = sb("rt", [P, 4, E], fp16)
        lmax = sb("lmax", [P, CH])
        lg = sb("lg", [P, CH, E])
        esum = sb("esum", [P, CH])
        probs = sb("probs", [P, TILES, E])
        top8 = sb("top8", [P, CH, 8])
        idx8 = sb("idx8", [P, CH, 8], u32)
        idxf = sb("idxf", [P, CH, TOP])
        picked = sb("picked", [P, TOP, TILES, E])
        top_p = sb("top_p", [P, TOP, TILES])
        marks = sb("marks", [P, CH + 1, E], bf16)
        place = sb("place", [P, CH, E])
        place_k = sb("place_k", [P, TOP, CH, E])
        slot_f = sb("slot_f", [P, TOP, CH])
        slot = [sb(f"slot{n}", [P, TOP, CH], i32) for n in range(2)]
        w1 = sb("w1", [P, E, 4, I], fp16)
        w2 = sb("w2", [P, E, IC, 2, D], fp16)
        sq = sb("sq", [P, 3, 16])
        sqs = sb("sqs", [P, 7])
        scale_i = sb("scale_i", [P, 4, 2], i32)
        scale = sb("scale", [P, 8])
        cnt = sb("cnt", [P, E])
        cnt_i = sb("cnt_i", [P, E], i32)
        tiles_e = sb("tiles_e", [P, E])
        jump = sb("jump", [P, E])
        last_e = sb("last_e", [P, E])
        e_f = sb("e_f", [P, SLOTS])
        row_f = sb("row_f", [P, SLOTS])
        e_i = sb("e_i", [P, SLOTS], i32)
        row_i = sb("row_i", [P, SLOTS], i32)
        base_i = sb("base_i", [P, E], i32)
        xin = [carve((ROW,), fp16) for n in range(4)]
        xT = [carve((3, P), fp16) for n in range(2)]
        hs = [carve((I,)) for n in range(2)]
        hT = [carve((2, IC, P), fp16) for n in range(2)]
        y_lo = [carve((D,)) for n in range(2)]
        y_sb = [carve((D,)) for n in range(4)]
        y_to = [sb(f"y_to{n}", [P, 1], i32) for n in range(4)]
        imp = sb("imp", [P, E])
        bal = sb("bal", [P, TOP, TILES, E])
        wgt = sb("wgt", [P, TOP, TILES])
        wsum = sb("wsum", [P, TILES])
        junk = [bal[:].rearrange("p k t e -> p (k t e)").bitcast(bf16)[:, n * I:(n + 1) * I] for n in range(2)]
        word_f = word[:].rearrange("p t d -> p (t d)")
        n_pads = PADS * ROW // 2
        pads = word_f[:, 0:n_pads].rearrange("p (n r) -> p n r", n=PADS)
        passed = word_f[:, n_pads:n_pads + SLOTS * E].rearrange("p (t e) -> p t e", e=E)
        back = [word[:, 8 * n:8 * n + 8, :].rearrange("p (b k) d -> p b k d", k=2) for n in range(4)]

        STEPS = range(-8, PAIRS + 6)

        def chunk(k):
            return 0 <= k < CHUNKS

        def pair(j):
            return 0 <= j < PAIRS

        SUM_AT = {0: 1, 12: 2}

        AT_RANKS, AT_BATCH = CH * E, (2 * CH + 1) * E
        bank = [ctx.enter_context(nc.psum_tensor(f"bank{n}", [P, 512], fp32)) for n in range(8)]

        s_ids, s_small, s_attw, s_gb = sem("ids_in"), sem("small_in"), sem("attn_w_in"), sem("gb_in")
        s_w1in, s_w2in, s_rin = sem("w1_in"), sem("w2_in"), sem("router_in")
        s_word = [sem(f"words_in{n}") for n in range(2)]
        s_pt = [sem(f"pt_ids_in{n}") for n in range(2)]
        s_const = sem("const_ready")
        s_vc, s_ac, s_gc = sem("vector_step"), sem("squares_done"), sem("gpsimd_step")
        s_ac2 = sem("scalar_step")
        s_alone = sem("waits_alone")
        s_tab = sem("tables_ready")
        s_wqk, s_wqk_sb = sem("wqk_done"), sem("wqk_ready")
        s_oh, s_emb, s_embadd = sem("onehot_ready"), sem("emb_done"), sem("emb_added")
        s_wv, s_hv, s_coef = sem("word_variances_ready"), sem("h_variances_ready"), sem("coefs_ready")
        s_wg, s_hg, s_bg = sem("word_guesses_ready"), sem("h_guesses_ready"), sem("batch_guesses_ready")
        s_rowvar, s_bv = sem("rowvar_ready"), sem("batch_var_done")
        s_r2v, s_r2 = sem("second_variances_ready"), sem("second_guesses_ready")
        s_r2c, s_x2 = sem("second_coefs_ready"), sem("x2_ready")
        s_eps = sem("eps_ready")
        s_xn, s_xt, s_xtsb = sem("xn_ready"), sem("xnT_done"), sem("xnT_ready")
        s_g, s_gsb, s_v, s_vsb = sem("g_done"), sem("g_ready"), sem("v_done"), sem("v_ready")
        s_s, s_max, s_p = sem("scores_done"), sem("max_ready"), sem("p_ready")
        s_pt_, s_ptsb, s_o, s_res = sem("pT_done"), sem("pT_ready"), sem("o_done"), sem("residual_added")
        s_rows, s_x2t, s_x2tsb, s_lg = sem("rows_ready"), sem("x2T_done"), sem("x2T_ready"), sem("logits_done")
        s_lgx, s_ex, s_mk, s_rk = sem("logits_shifted"), sem("exp_ready"), sem("marks_ready"), sem("ranks_done")
        s_slot = sem("slots_ready")
        s_scat = [sem(f"scattered{n}") for n in range(4)]
        s_sq, s_sqs, s_scale = sem("squares_ready"), sem("squares_summed"), sem("scale_ready")
        s_whi, s_wlo = sem("w_high_ready"), sem("w_low_ready")
        s_plan, s_pads, s_pad = sem("plan_ready"), sem("padding_ready"), sem("padding_written")
        s_xin = [sem(f"x_in{n}") for n in range(4)]
        s_xft, s_xftsb, s_h1, s_hs = sem("xT_done"), sem("xT_ready"), sem("h_done"), sem("silu_ready")
        s_ht, s_hi, s_lo = sem("hT_done"), sem("hT_high_ready"), sem("hT_low_ready")
        s_y, s_ylo, s_ysb, s_to = sem("y_done"), sem("y_low_ready"), sem("y_ready"), sem("y_place_ready")
        s_ysc = [sem(f"y_scattered{n}") for n in range(4)]
        s_imp, s_wgt = sem("importance_done"), sem("weights_ready")
        s_back = [sem(f"y_back{n}") for n in range(4)]
        s_fin = sem("result_ready")
        s_out = [sem(f"result_out{n}") for n in range(4)]

        class Steps:

            def __init__(self, eng, s):
                self.eng, self.s, self.n = eng, s, 0

            def did(self, ins):
                self.n += 1
                ins.then_inc(self.s, 1)
                return self.n

            def wait(self, link=None):
                self.eng.wait_ge(self.s, self.n if link is None else link)


        def alone(eng):
            eng.sem_inc(s_alone, 1)

        def need(eng, s, n):
            if n > 0:
                eng.wait_ge(s, n)

        def mm(out_, lhsT, rhs, start, stop):
            return nc.tensor.matmul(out_, lhsT, rhs, start=start, stop=stop)

        def run_experts(eng, step):
            for t in range(4):
                step(t, t, 0)
            with eng.Fori(1, SLOTS // 4) as i:
                for q in range(4):
                    step(i * 4 + q, q, i * 4)
            for t in range(SLOTS, SLOTS + 3):
                step(t, t % 4, t - t % 4)

        block = ctx.enter_context(nc.Block())

        @block.sync
        def _(sp):
            sp.dma_start(ids_sb[:], ids).then_inc(s_ids, 16)
            sp.dma_start(tab[:, 0, :], pos_emb).then_inc(s_small, 16)
            sp.wait_ge(s_const, 1)
            for n in range(3):
                sp.dma_start(tab[32 * n:32 * n + 2, 1, :], type_emb).then_inc(s_small, 16)

            def chunk_ids(k):
                need(sp, s_oh, k - 1)
                sp.dma_start(pt_ids[k % 2][:], pt_rows[:, k, :, :].partition_broadcast(P)).then_inc(s_pt[k % 2], 16)
            chunk_ids(0)
            chunk_ids(1)
            sp.dma_start(gb[:, 0, :], gamma.partition_broadcast(P)).then_inc(s_gb, 16)
            sp.dma_start(gb[:, 1, :], beta.partition_broadcast(P)).then_inc(s_gb, 16)
            for dst, src in ((wq_sb, wq), (wk_sb, wk), (wv_sb, wv_t)):
                sp.dma_start(dst[:, 0, :], src[0:P, :]).then_inc(s_attw, 16)
                sp.dma_start(dst[0:D2, 1, :], src[P:D, :]).then_inc(s_attw, 16)
            sp.dma_start(rt_f[:, 0, :], router_t[0:P, :]).then_inc(s_rin, 16)
            sp.dma_start(rt_f[0:D2, 1, :], router_t[P:D, :]).then_inc(s_rin, 16)
            sp.dma_start(rt_f[D2:P, 1, :], router_t[P:D, :]).then_inc(s_rin, 16)
            w1_v = w1_t.rearrange("d (e i) -> d e i", e=E)
            sp.dma_start(stage[:, :, 0, :], w1_v[0:P, :, :]).then_inc(s_w1in, 16)
            sp.dma_start(stage[0:D2, :, 1, :], w1_v[P:D, :, :]).then_inc(s_w1in, 16)
            sp.dma_start(stage[D2:P, :, 1, :], w1_v[P:D, :, :]).then_inc(s_w1in, 16)
            for k in range(2, CHUNKS):
                chunk_ids(k)
            sp.wait_ge(s_wlo, 2 + 4)
            sp.dma_start(stage[:].rearrange("p e a i -> p (e a i)")[:, 0:E * IC * D], w2_t).then_inc(s_w2in, 16)

            sp.wait_ge(s_pads, 1)
            for e in range(E):
                sp.dma_start(sorted_rows[E * REGION + e * P:E * REGION + (e + 1) * P, :], pads[:, E + e, :].bitcast(fp16))\
                  .then_inc(s_pad, 16)
            sp.wait_ge(s_plan, 1)
            for e in range(E):
                at = nc.sync.value_load(base_i[0:1, e:e + 1], min_val=0, max_val=E * REGION)
                sp.dma_start(sorted_rows[bass.ds(at, P), :], pads[:, e, :].bitcast(fp16)).then_inc(s_pad, 16)
            sp.wait_ge(s_pad, 2 * E * 16)
            for n in range(4):
                sp.wait_ge(s_scat[n], 16 * TOP * CH * (CHUNKS // 4))
            with sp.Fori(0, SLOTS // 4) as i:
                for q in range(4):
                    at = nc.sync.value_load(row_i[0:1, bass.ds(i * 4 + q, 1)], min_val=0,
                                            max_val=E * REGION + REST - P)
                    sp.wait_ge(s_xft, i * 4 + (q + 1))
                    sp.wait_ge(s_to, i * 4 + (q + 1))
                    sp.dma_start(xin[q][:], sorted_rows[bass.ds(at, P), :]).then_inc(s_xin[q], 16)
            for q in range(4):
                sp.wait_ge(s_ysc[q], 16 * SLOTS // 4)
            y_v = y_rows[0:TOP * TOKENS, :].rearrange("(b p k) d -> p b (k d)", p=P, k=TOP)
            for g in range(TILES // 4):
                if g >= 4:
                    sp.wait_ge(s_out[g % 4], 16)
                sp.dma_start(back[g % 4].rearrange("p b k d -> p b (k d)"), y_v[:, 4 * g:4 * g + 4, :])\
                  .then_inc(s_back[g % 4], 16)
            for g in range(4):
                sp.wait_ge(s_out[g], 32)

        @block.gpsimd
        def _(pool):
            gp = nc.gpsimd
            links = Steps(pool, s_gc)
            gp.memset(tab[:, 1, :], 0.0).then_inc(s_const, 1)
            gp.memset(eps[:, 0:1], 1e-12).then_inc(s_eps, 1)
            gp.memset(eps[:, 1:2], 1e-5).then_inc(s_eps, 1)
            links.did(gp.memset(ident[:], 0.0))
            links.did(gp.memset(ident16[:], 0.0))
            links.did(gp.memset(before[:], 1.0))
            links.did(gp.memset(upto[:], 1.0))
            links.did(gp.memset(ones_b[:], 1.0))
            links.did(gp.memset(ones_f[:], 1.0))
            links.did(gp.memset(mean_w[:], 1.0 / P))
            links.did(gp.memset(marks[:], 0.0))
            links.wait()
            for m in (ident, ident16):
                links.did(gp.affine_select(out=m[:], in_=m[:], compare_op=ALU.not_equal, fill=1.0, base=0,
                                           pattern=[[-1, P]], channel_multiplier=1))
            links.did(gp.affine_select(out=before[:], in_=before[:], compare_op=ALU.is_gt, fill=0.0, base=0,
                                       pattern=[[1, P]], channel_multiplier=-1))
            links.did(gp.affine_select(out=upto[:], in_=upto[:], compare_op=ALU.is_ge, fill=0.0, base=0,
                                       pattern=[[1, E], [-1, E]], channel_multiplier=0))
            links.did(gp.iota(part_i[:, 0:1], [[0, 1]], base=0, channel_multiplier=1))
            for dst, pat, mult in ((iota_e[:], [[1, E]], 0), (token2[:], [[2 * P, TILES]], 2),
                                   (base[:], [[REGION, E]], 0), (tile_no[:], [[1, SLOTS]], 0)):
                links.did(gp.iota(dst, pat, base=0, channel_multiplier=mult,
                                  allow_small_or_imprecise_dtypes=True))
            links.wait()
            gp.nop().then_inc(s_const, 1)
            pool.wait_ge(s_ids, 16)

            def words(c):
                need(pool, s_word[c % 2], 16 * CH * (c // 2))
                for t in range(c * CH, (c + 1) * CH):
                    gp.indirect_dma_start(word[:, t, :], None, word_emb,
                                          bass.IndirectOffsetOnAxis(ids_sb[:, t:t + 1], 0))\
                      .then_inc(s_word[c % 2], 16)
            words(0)
            words(1)
            for c in range(2, CHUNKS):
                words(c)
            for r in range(CHUNKS):
                n = r % 4
                if r == CHUNKS - 4:
                    pool.wait_ge(s_rowvar, CHUNKS)
                    links.did(gp.memset(pads, 0.0))
                    links.wait()
                    links.did(gp.iota(pads[:, :, D + 1], [[TOP * P, PADS]], base=TOP * TOKENS, channel_multiplier=TOP,
                                      allow_small_or_imprecise_dtypes=True))
                    links.wait()
                    gp.nop().then_inc(s_pads, 1)
                pool.wait_ge(s_slot, r + 1)
                for k in range(TOP):
                    for t in range(CH):
                        gp.indirect_dma_start(sorted_rows, bass.IndirectOffsetOnAxis(slot[r % 2][:, k, t:t + 1], 0),
                                              rows[n][:, t, :], None).then_inc(s_scat[n], 16)
            with pool.Fori(0, SLOTS // 4) as i:
                for q in range(4):
                    pool.wait_ge(s_ysb, i * 4 + (q + 1 + LEAD))
                    alone(pool)
                    gp.indirect_dma_start(y_rows, bass.IndirectOffsetOnAxis(y_to[q][:], 0),
                                          y_sb[q][:], None).then_inc(s_ysc[q], 16)

        @block.tensor
        def _(pe):
            pe.wait_ge(s_const, 2)
            pe.wait_ge(s_tab, 1)

            xt, g, v, s, o, emb, x2t_b, small = [bank[n] for n in (0, 1, 2, 3, 4, 5, 6, 7)]

            def multiply_wq_wk():
                pe.wait_ge(s_attw, 6 * 16)
                for m, (lo, n) in enumerate(((0, P), (P, D2))):
                    mm(g[0:n, m * D:(m + 1) * D], wq_sb[:, 0, lo:lo + n], wk_sb[:, 0, :], True, False)
                    last = mm(g[0:n, m * D:(m + 1) * D], wq_sb[0:D2, 1, lo:lo + n], wk_sb[0:D2, 1, :], False, True)
                last.then_inc(s_wqk, 1)

            def embed(k, q):
                if q == 0:
                    pe.wait_ge(s_oh, k + 1)
                need(pe, s_embadd, 2 * k + q)
                for u in range(2):
                    dst = emb[:, u * D:(u + 1) * D]
                    t = slice((2 * q + u) * P, (2 * q + u + 1) * P)
                    for n in range(3):
                        mm(dst, onehot[:, 0, t], tab_p[n][:, 0, :], n == 0, False)
                    last = mm(dst, onehot[:, 1, t], type_p[:], False, True)
                last.then_inc(s_emb, 1)

            def batch_mean(k):
                pe.wait_ge(s_rowvar, k + 1)
                need(pe, s_lgx, k - 5 + 1)
                mm(small[:, AT_BATCH:AT_BATCH + CH], mean_w[:], rowvar[:], True, True).then_inc(s_bv, 1)

            def transpose_xn(j):
                par = j % 2
                pe.wait_ge(s_xn, j + 1)
                need(pe, s_xtsb, j)
                for u in range(2):
                    nc.tensor.transpose(xt[:, u * P:(u + 1) * P], xn[par][:, u, 0:P], ident[:])
                    last = nc.tensor.transpose(xt[0:D2, (2 + u) * P:(3 + u) * P], xn[par][:, u, P:D], ident[:])
                last.then_inc(s_xt, 1)

            def project(j):
                par = j % 2
                if j == 0:
                    pe.wait_ge(s_wqk_sb, 1)
                pe.wait_ge(s_xtsb, j + 1)
                need(pe, s_gsb, j)
                for m, (lo, n) in enumerate(((0, P), (P, D2))):
                    dst = g[0:n, m * 2 * P:(m + 1) * 2 * P]
                    mm(dst, wqk[:, 0, lo:lo + n], xnT[par][:, 0, :], True, False)
                    last = mm(dst, wqk[0:D2, 1, lo:lo + n], xnT[par][0:D2, 1, :], False, True)
                last.then_inc(s_g, 1)
                need(pe, s_vsb, j)
                for u in range(2):
                    dst = v[:, u * D:(u + 1) * D]
                    mm(dst, xnT[par][:, 0, u * P:(u + 1) * P], wv_sb[:, 0, :], True, False)
                    last = mm(dst, xnT[par][0:D2, 1, u * P:(u + 1) * P], wv_sb[0:D2, 1, :], False, True)
                last.then_inc(s_v, 1)

            def scores(j):
                par = j % 2
                pe.wait_ge(s_gsb, j + 1)
                need(pe, s_ptsb, j)
                for u in range(2):
                    dst, c = s[:, u * P:(u + 1) * P], slice(u * P, (u + 1) * P)
                    mm(dst, gT[par][:, 0, c], xnT[par][:, 0, c], True, False)
                    last = mm(dst, gT[par][0:D2, 1, c], xnT[par][0:D2, 1, c], False, True)
                last.then_inc(s_s, 1)

            def transpose_p(j):
                pe.wait_ge(s_p, j + 1)
                for u in range(2):
                    last = nc.tensor.transpose(s[:, (2 + u) * P:(3 + u) * P], pr[j % 2][:, u, :], ident[:])
                last.then_inc(s_pt_, 1)

            def attend(j):
                par = j % 2
                need(pe, s_res, j)
                if j in SUM_AT:
                    n = SUM_AT[j]
                    pe.wait_ge(s_sqs, n + 1)
                    mm(o[:, 2 * D:2 * D + 1], ones_f[:], sqs[:, n:n + 1], True, True)
                pe.wait_ge(s_ptsb, j + 1)
                pe.wait_ge(s_vsb, j + 1)
                for u in range(2):
                    last = mm(o[:, u * D:(u + 1) * D], prT[par][:, u, :], v_sb[par][:, u, :], True, True)
                last.then_inc(s_o, 1)

            x2t = x2t_b[:].bitcast(fp16)

            def transpose_rows(r, q):
                pe.wait_ge(s_rows, r + 1)
                need(pe, s_x2tsb, 2 * r + q)
                for u in range(2):
                    for k in range(3):
                        at = (3 * u + k) * P
                        last = nc.tensor.transpose(x2t[:, at:at + P],
                                                   rows[r % 4][:, 2 * q + u, k * P:(k + 1) * P], ident16[:])
                last.then_inc(s_x2t, 1)

            def logits(r):
                need(pe, s_slot, r)
                need(pe, s_bg, min(r + 5, CHUNKS))
                for t in range(CH):
                    pe.wait_ge(s_x2tsb, 2 * r + t // 2 + 1)
                    for k, (a, b) in enumerate(((0, 0), (1, 0), (0, 1), (2, 2), (2, 3))):
                        last = mm(small[:, t * E:(t + 1) * E], x2T[:, t, a, :], rt[:, b, :], k == 0, k == 4)
                last.then_inc(s_lg, 1)

            def ranks(r):
                pe.wait_ge(s_mk, r + 1)
                need(pe, s_bg, min(r + 6, CHUNKS))
                at = AT_RANKS
                mm(small[:, at:at + (CH + 1) * E], before[:], marks[:].rearrange("p t e -> p (t e)"), True, False)
                for t in range(CH):
                    last = mm(small[:, at + (t + 1) * E:at + (CH + 1) * E], ones_b[:],
                              marks[:, t:t + 1, :].to_broadcast([P, CH - t, E]), False, t == CH - 1)
                last.then_inc(s_rk, 1)

            pe.wait_ge(s_sqs, 1)
            mm(o[:, 2 * D:2 * D + 1], ones_f[:], sqs[:, 0:1], True, True).then_inc(s_sq, 1)
            for j in STEPS:
                c = j // 2
                if j == -3:
                    multiply_wq_wk()
                if pair(j):
                    scores(j)
                if pair(j - 1):
                    attend(j - 1)
                if j % 2 == 0:
                    if chunk(c + 4):
                        embed(c + 4, 0)
                    if pair(j + 1):
                        project(j + 1)
                    if chunk(c - 2):
                        transpose_rows(c - 2, 0)
                    if pair(j):
                        transpose_p(j)
                    if chunk(c - 2):
                        transpose_rows(c - 2, 1)
                    if pair(j + 2):
                        transpose_xn(j + 2)
                    if chunk(c + 2):
                        batch_mean(c + 2)
                else:
                    if chunk(c - 3):
                        ranks(c - 3)
                    if pair(j + 1):
                        project(j + 1)
                    if chunk(c + 4):
                        embed(c + 4, 1)
                    if chunk(c - 2):
                        logits(c - 2)
                    if pair(j):
                        transpose_p(j)
                    if pair(j + 2):
                        transpose_xn(j + 2)

            xt_b = bank[0][:].bitcast(fp16)
            h_b, ht_b, y_b = [bank[1], bank[2]], [bank[3], bank[4]], [bank[5], bank[6]]
            for x in (s_xft,):
                pe.sem_inc(x, 4)
            for x in (s_h1, s_ht, s_y):
                pe.sem_inc(x, LEAD)
            w1_f = w1[:].rearrange("p e a i -> p (e a i)")
            w2_f = w2[:].rearrange("p e c a d -> p (e c a d)")

            def load_experts(at, n):
                return nc.values_load_multi_w_load_instructions(
                    e_i[0:1, bass.ds(at, n)], engines=(mybir.EngineType.PE,), min_val=0, max_val=E - 1,
                    skip_runtime_bounds_check_because="the plan keeps it below E")[1]

            def experts(t, q, r):
                fixed = isinstance(t, int)
                if fixed and t == 0:
                    loaded[0] = (None,) * 4 + tuple(load_experts(0, 4))
                if fixed and t == SLOTS:
                    loaded[0] = tuple(load_experts(SLOTS - 4, 4)) + (None,) * 4
                if not fixed and q == 0:
                    loaded[0] = tuple(load_experts(r - 4, 8))
                if not fixed or 1 <= t <= SLOTS:
                    e = loaded[0][4 + q - 1]
                    pe.wait_ge(s_xftsb, t + LEAD)
                    pe.wait_ge(s_hs, t - 1 + LEAD - 1)
                    for k, (a, b) in enumerate(((0, 0), (1, 0), (0, 1), (2, 2), (2, 3))):
                        last = mm(h_b[(q - 1) % 2][:], xT[(q - 1) % 2][:, a, :],
                                  w1_f[:, bass.ds(e * (4 * I) + b * I, I)], k == 0, k == 4)
                    last.then_inc(s_h1, 1)
                if not fixed or t < SLOTS:
                    pe.wait_ge(s_xin[q], r * 4 + 16)
                    pe.wait_ge(s_xftsb, t + LEAD)
                    for k in range(3):
                        last = nc.tensor.transpose(xt_b[:, k * P:(k + 1) * P], xin[q][:, k * P:(k + 1) * P], ident16[:])
                    last.then_inc(s_xft, 1)
                if not fixed or 3 <= t:
                    e = loaded[0][4 + q - 3]
                    par = (q - 3) % 2
                    pe.wait_ge(s_lo, t - 3 + 1 + LEAD)
                    pe.wait_ge(s_ysb, t - 5 + 1 + LEAD)
                    for c in range(IC):
                        at = e * (IC * 2 * D) + c * 2 * D
                        mm(y_b[par][:, 0:2 * D], hT[par][:, 0, c, :], w2_f[:, bass.ds(at, 2 * D)], c == 0, False)
                        last = mm(y_b[par][:, 0:D], hT[par][:, 1, c, :], w2_f[:, bass.ds(at, D)], False, c == IC - 1)
                    last.then_inc(s_y, 1)
                if not fixed or 1 <= t <= SLOTS:
                    par = (q - 1) % 2
                    pe.wait_ge(s_hs, t + LEAD)
                    pe.wait_ge(s_lo, t - 1 + LEAD - 1)
                    for c in range(IC):
                        last = nc.tensor.transpose(ht_b[par][:, c * P:(c + 1) * P],
                                                   hs[par][:, c * P:(c + 1) * P], ident[:])
                    last.then_inc(s_ht, 1)
            pe.wait_ge(s_plan, 1)
            pe.wait_ge(s_wlo, 2 + 8)
            loaded = [None]
            run_experts(pe, experts)
            mm(bank[7][:, 0:TILES * E], ones_f[:], probs[:].rearrange("p t e -> p (t e)"), True, True)\
                .then_inc(s_imp, 1)

        @block.vector
        def _(dve):
            ve = nc.vector
            links = Steps(dve, s_vc)
            did, wait = links.did, links.wait

            def refine(n, var, eps_value):
                y, t = root_0[:, n, :], root_t[:, n, :]
                did(ve.scalar_tensor_tensor(out=t, in0=y, scalar=-0.5, in1=y, op0=ALU.mult, op1=ALU.mult)); wait()
                did(ve.scalar_tensor_tensor(out=t, in0=var, scalar=eps_value, in1=t, op0=ALU.add, op1=ALU.mult)); wait()
                return did(ve.scalar_tensor_tensor(out=root[:, n, :], in0=t, scalar=1.5, in1=y,
                                                   op0=ALU.add, op1=ALU.mult))

            dve.wait_ge(s_const, 2)
            dve.wait_ge(s_small, 64)
            did(ve.tensor_copy(tab_p[0][:], tab[:])); wait()
            did(ve.tensor_tensor(tab_r[:], tab[:], tab_p[0][:], ALU.subtract)); wait()
            did(ve.tensor_copy(tab_p[1][:], tab_r[:])); wait()
            did(ve.tensor_tensor(tab_r[:], tab_r[:], tab_p[1][:], ALU.subtract)); wait()
            did(ve.tensor_copy(tab_p[2][:], tab_r[:]))
            did(ve.memset(type_p[:], 0.0)); wait()
            for n in range(3):
                did(ve.tensor_copy(type_p[32 * n:32 * n + 2, :], tab_p[n][32 * n:32 * n + 2, 1, :]))
            did(ve.tensor_scalar(part_i[:, 1:2], part_i[:, 0:1], 31, None, ALU.bitwise_and)); wait()
            did(ve.tensor_copy(part[:], part_i[:])); wait()
            ve.nop().then_inc(s_tab, 1)
            dve.wait_ge(s_gb, 32)

            u0, sh = scale_i, 23
            sc = scale[:].bitcast(i32)

            def exponent(dst, src, mul, add):
                did(ve.tensor_scalar(dst, src, mul, add, ALU.mult, ALU.add)); wait()
                did(ve.tensor_scalar(dst, dst, sh, None, ALU.arith_shift_left)); wait()

            def exponent_of(n):
                u = u0[:, n, 0:1]
                did(ve.tensor_copy(sqs[:, 3 + n:4 + n], bank[4][:, 2 * D:2 * D + 1])); wait()
                did(ve.tensor_scalar(u, sqs[:, 3 + n:4 + n].bitcast(i32), 24, None, ALU.logical_shift_right)); wait()
                return u

            def low(dst, src, hi, by):
                return ve.scalar_tensor_tensor(out=dst, in0=src, scalar=by, in1=hi, op0=ALU.mult, op1=ALU.subtract)

            def sum_squares(n, squares, cols):
                dve.wait_ge(s_ac, squares)
                ve.reduce_sum(sqs[:, n:n + 1], sq[:, n, 0:cols], axis=AX).then_inc(s_sqs, 1)

            def w1_scales():
                u = exponent_of(1)
                exponent(sc[:, 0:1], u, -1.0, 202.0)
                exponent(sc[:, 1:2], u, 1.0, 52.0)
                exponent(sc[:, 4:5], u, -1.0, 198.0)
                exponent(sc[:, 5:6], u, 1.0, 56.0)
                ve.nop().then_inc(s_scale, 1)

            def w2_scales():
                u = exponent_of(2)
                exponent(sc[:, 2:3], u, -1.0, 202.0)
                exponent(sc[:, 3:4], u, 1.0, 52.0)
                did(ve.tensor_tensor(scale[:, 6:7], scale[:, 3:4], scale[:, 5:6], ALU.mult)); wait()
                ve.nop().then_inc(s_scale, 1)

            def keep_wqk():
                dve.wait_ge(s_wqk, 1)
                did(ve.tensor_copy(wqk[:, 0, :], bank[1][:, 0:D]))
                did(ve.tensor_copy(wqk[0:D2, 1, :], bank[1][0:D2, D:2 * D])); wait()
                ve.nop().then_inc(s_wqk_sb, 1)

            w2_s = stage[:].rearrange("p e a i -> p (e a i)")[:, 0:E * IC * D].rearrange("p (e c d) -> p e c d", e=E, c=IC)

            def weights(j, part):
                if j == 0 and part == 0:
                    sum_squares(1, 17, 16)
                if 3 <= j < 7:
                    if part == 0:
                        dve.wait_ge(s_whi, j - 2)
                    n = 4 * (j - 3) + part
                    e, k = n // 2, n % 2
                    done = did(low(w1[:, e, 2 * k + 1, :], stage[:, e, k, :], w1[:, e, 2 * k, :], scale[:, 0:1]))
                    if part == 3:
                        wait(done)
                        ve.nop().then_inc(s_wlo, 1)
                if j == 12 and part == 0:
                    sum_squares(2, 33, 16)
                if 15 <= j < 19 and part % 2 == 0:
                    if part == 0:
                        dve.wait_ge(s_whi, 4 + j - 14)
                    e = 2 * (j - 15) + part // 2
                    done = did(low(w2[:, e, :, 1, :], w2_s[:, e], w2[:, e, :, 0, :], scale[:, 2:3]))
                    if part == 2:
                        wait(done)
                        ve.nop().then_inc(s_wlo, 1)

            sum_squares(0, 1, 1)
            dve.wait_ge(s_sq, 1)
            u = exponent_of(0)
            exponent(sqs[:, 6:7].bitcast(i32), u, -1.0, 202.0)
            exponent(sc[:, 7:8], u, 1.0, 52.0)
            for k in range(2):
                did(ve.tensor_scalar(rt[:, 2 * k, :], rt_f[:, k, :], sqs[:, 6:7], None, ALU.mult))
            wait()
            for k in range(2):
                did(low(rt[:, 2 * k + 1, :], rt_f[:, k, :], rt[:, 2 * k, :], sqs[:, 6:7]))
            wait()
            ve.nop().then_inc(s_wlo, 2)

            def one_hots(k):
                need(dve, s_emb, 2 * k)
                dve.wait_ge(s_pt[k % 2], 16 * (k // 2 + 1))
                did(ve.tensor_scalar(onehot[:, 0, :], pt_ids[k % 2][:, 0, :], part[:, 0:1], None, ALU.is_equal))
                ve.tensor_scalar(onehot[:, 1, :], pt_ids[k % 2][:, 1, :], part[:, 1:2], None, ALU.is_equal)\
                    .then_inc(s_oh, 1)

            def add_words(k, q):
                t = CH * k + 2 * q
                dve.wait_ge(s_word[k % 2], 16 * CH * (k // 2 + 1))
                dve.wait_ge(s_emb, 2 * k + q + 1)
                ve.tensor_tensor(word[:, t:t + 2, :], word[:, t:t + 2, :],
                                 bank[5][:, 0:2 * D].rearrange("p (u d) -> p u d", u=2), ALU.add).then_inc(s_embadd, 1)
                return 2 * k + q + 1

            def word_stats(k, q, added):
                dve.wait_ge(s_embadd, added)
                for u in range(2):
                    last = did(ve.bn_stats(st_w[:, 2 * q + u, :], word[:, CH * k + 2 * q + u, :]))
                return last

            def aggregate(mv, st, done, ready):
                wait(done)
                for t in range(CH):
                    last = did(ve.bn_aggr(mv[:, t, :], st[:, t, :]))
                wait(last)
                ve.nop().then_inc(ready, 1)

            def gamma_part(k):
                dve.wait_ge(s_wg, k + 1)
                refine(0, mv_w[:, :, 1], 1e-12)
                for t in range(CH):
                    last = did(ve.scalar_tensor_tensor(out=word[:, CH * k + t, :], in0=word[:, CH * k + t, :],
                                                       scalar=mv_w[:, t, 0:1], in1=gb[:, 0, :],
                                                       op0=ALU.subtract, op1=ALU.mult))
                return last

            def beta_part(k, done):
                wait(done)
                for t in range(CH):
                    last = did(ve.scalar_tensor_tensor(out=h[:, CH * k + t, :], in0=word[:, CH * k + t, :],
                                                       scalar=root[:, 0, t:t + 1], in1=gb[:, 1, :],
                                                       op0=ALU.mult, op1=ALU.add))
                return last

            def h_stats(k, done):
                wait(done)
                for t in range(CH):
                    last = did(ve.bn_stats(st_h[:, t, :], h[:, CH * k + t, :]))
                return last

            def row_variance(k):
                dve.wait_ge(s_hg, k + 1)
                wait(refine(1, mv_h[:, :, 1], 1e-5))
                did(ve.tensor_tensor(root_t[:, 1, :], root[:, 1, :], root[:, 1, :], ALU.mult)); wait()
                ve.tensor_tensor(rowvar[:], root_t[:, 1, :], mv_h[:, :, 1], ALU.mult).then_inc(s_rowvar, 1)

            def coefs(k):
                tiles = slice(CH * k, CH * (k + 1))
                dve.wait_ge(s_bg, k + 1)
                wait(refine(2, batch_var[:], 1e-5))
                did(ve.tensor_tensor(coef1[:, tiles], root[:, 1, :], root[:, 2, :], ALU.mult)); wait()
                ve.scalar_tensor_tensor(out=shift1[:, tiles], in0=mv_h[:, :, 0], scalar=-1.0, in1=coef1[:, tiles],
                                        op0=ALU.mult, op1=ALU.mult).then_inc(s_coef, 1)

            def row_max(j):
                dve.wait_ge(s_s, j + 1)
                need(dve, s_p, j - 1)
                ve.tensor_reduce(nmax[j % 2][:], bank[3][:, 0:2 * P].rearrange("p (u k) -> p u k", u=2),
                                 axis=AX, op=ALU.max, negate=True).then_inc(s_max, 1)

            def residual(j):
                par = j % 2
                dve.wait_ge(s_p, j + 1)
                r = did(ve.reciprocal(rinv[par][:], rsum[par][:]))
                dve.wait_ge(s_o, j + 1)
                if j in SUM_AT:
                    (w1_scales if SUM_AT[j] == 1 else w2_scales)()
                wait(r)
                for u in range(2):
                    last = did(ve.scalar_tensor_tensor(out=h[:, 2 * j + u, :], in0=bank[4][:, u * D:(u + 1) * D],
                                                       scalar=rinv[par][:, u:u + 1], in1=h[:, 2 * j + u, :],
                                                       op0=ALU.mult, op1=ALU.add))
                wait(last)
                ve.nop().then_inc(s_res, 1)

            def residual_stats(j):
                for u in range(2):
                    last = did(ve.bn_stats(st2[j % 2][:, u, :], h[:, 2 * j + u, :]))
                return last

            def residual_aggr(j, done):
                wait(done)
                for u in range(2):
                    last = did(ve.bn_aggr(mv2[:, 2 * j + u, :], st2[j % 2][:, u, :]))
                if j % 2:
                    wait(last)
                    ve.nop().then_inc(s_r2v, 1)

            def second_coefs(r):
                m = mv2[:, CH * r:CH * (r + 1), :]
                dve.wait_ge(s_r2, r + 1)
                wait(refine(3, m[:, :, 1], 1e-5))
                ve.scalar_tensor_tensor(out=shift2[:], in0=m[:, :, 0], scalar=-1.0, in1=root[:, 3, :],
                                        op0=ALU.mult, op1=ALU.mult).then_inc(s_r2c, 1)

            segs = ((0, P, 0, P), (P, D, 2 * P, 2 * P + D2))

            def row_parts(r):
                row = rows[r % 4]
                dve.wait_ge(s_x2, r + 1)
                need(dve, s_scat[r % 4], 16 * TOP * CH * (r // 4))
                for a, b, lo, hi in segs:
                    last = did(ve.tensor_copy(row[:, :, lo:hi], x2[:, :, a:b]))
                wait(last)
                for a, b, lo, hi in segs:
                    last = did(ve.tensor_tensor(row[:, :, lo + b - a:hi + b - a], x2[:, :, a:b], row[:, :, lo:hi],
                                                ALU.subtract))
                wait(last)
                ve.nop().then_inc(s_rows, 1)

            def shift_logits(r):
                dve.wait_ge(s_lg, r + 1)
                lgp = bank[7][:, 0:CH * E].rearrange("p (t e) -> p t e", t=CH)
                did(ve.tensor_reduce(lmax[:], lgp, axis=AX, op=ALU.max)); wait()
                ve.tensor_tensor(lg[:], lgp, lmax[:].unsqueeze(2).to_broadcast([P, CH, E]), ALU.subtract)\
                    .then_inc(s_lgx, 1)

            def choose(r):
                tiles = slice(CH * r, CH * (r + 1))
                dve.wait_ge(s_ex, r + 1)
                did(ve.reduce_sum(esum[:], lg[:], axis=AX)); wait()
                did(ve.reciprocal(lmax[:], esum[:])); wait()
                did(ve.tensor_tensor(probs[:, tiles, :], lg[:], lmax[:].unsqueeze(2).to_broadcast([P, CH, E]), ALU.mult))
                wait()
                for t in range(CH):
                    last = did(ve.max(top8[:, t, :], probs[:, CH * r + t, :]))
                wait(last)
                for t in range(CH):
                    last = did(ve.max_index(idx8[:, t, :], top8[:, t, :], probs[:, CH * r + t, :]))
                wait(last)
                did(ve.tensor_copy(idxf[:], idx8[:, :, 0:TOP])); wait()
                for k in range(TOP):
                    last = did(ve.tensor_tensor(picked[:, k, tiles, :], iota_e[:].unsqueeze(1).to_broadcast([P, CH, E]),
                                                idxf[:, :, k:k + 1].to_broadcast([P, CH, E]), ALU.is_equal))
                meta = rows[r % 4][:].bitcast(fp32)
                did(ve.tensor_copy(meta[:, :, D], idxf[:, :, 0]))
                did(ve.tensor_copy(meta[:, :, D + 1], token2[:, tiles]))
                did(ve.tensor_copy(top_p[:, :, tiles].rearrange("p k t -> p t k"), top8[:, :, 0:TOP]))
                wait(last)
                ve.tensor_tensor(marks[:, 0:CH, :], picked[:, 0, tiles, :], picked[:, 1, tiles, :], ALU.add)\
                    .then_inc(s_mk, 1)

            def find_places(r):
                tiles = slice(CH * r, CH * (r + 1))
                dve.wait_ge(s_rk, r + 1)
                rk = bank[7][:, CH * E:(2 * CH + 1) * E].rearrange("p (t e) -> p t e", e=E)
                did(ve.tensor_tensor(place[:], rk[:, 0:CH, :], base[:].unsqueeze(1).to_broadcast([P, CH, E]), ALU.add))
                wait()
                for k in range(TOP):
                    last = did(ve.tensor_tensor(place_k[:, k, :, :], place[:], picked[:, k, tiles, :], ALU.mult))
                did(ve.tensor_tensor(base[:], base[:], rk[:, CH, :], ALU.add))
                wait(last)
                did(ve.reduce_sum(slot_f[:], place_k[:], axis=AX)); wait()
                need(dve, s_scat[(r - 2) % 4], 16 * TOP * CH * ((r - 2) // 4 + 1))
                ve.tensor_copy(slot[r % 2][:], slot_f[:]).then_inc(s_slot, 1)

            one_hots(0)
            for j in STEPS:
                c = j // 2
                if j == -3:
                    keep_wqk()
                if pair(j - 1):
                    residual(j - 1)
                    residual_aggr(j - 1, residual_stats(j - 1))
                weights(j, 0)
                if j % 2 == 0:
                    if chunk(c + 2):
                        row_variance(c + 2)
                    if chunk(c + 3):
                        gamma_end = gamma_part(c + 3)
                    if chunk(c - 3):
                        choose(c - 3)
                    weights(j, 1)
                    if chunk(c + 4):
                        word_stats(c + 4, 0, add_words(c + 4, 0))
                    weights(j, 2)
                    if pair(j + 1):
                        row_max(j + 1)
                else:
                    if chunk(c - 1):
                        second_coefs(c - 1)
                    if chunk(c + 3):
                        done = h_stats(c + 3, beta_part(c + 3, gamma_end))
                    if chunk(c - 3):
                        find_places(c - 3)
                    if chunk(c + 2):
                        coefs(c + 2)
                    if chunk(c + 3):
                        need(dve, s_coef, c + 3)
                        aggregate(mv_h, st_h, done, s_hv)
                    weights(j, 1)
                    if chunk(c - 2):
                        shift_logits(c - 2)
                    if chunk(c + 4):
                        aggregate(mv_w, st_w, word_stats(c + 4, 1, add_words(c + 4, 1)), s_wv)
                    if chunk(c + 5):
                        one_hots(c + 5)
                    weights(j, 2)
                    if pair(j + 1):
                        row_max(j + 1)
                    if chunk(c - 1):
                        row_parts(c - 1)
                weights(j, 3)

            wait()
            did(ve.tensor_copy(base_i[:], base[:]))
            did(ve.tensor_scalar(cnt[:], iota_e[:], float(-REGION), float(P - 1), ALU.mult, ALU.add)); wait()
            did(ve.tensor_tensor(cnt_i[:], base[:], cnt[:], ALU.add)); wait()
            did(ve.tensor_scalar(cnt_i[:], cnt_i[:], 7, None, ALU.logical_shift_right)); wait()
            did(ve.tensor_copy(tiles_e[:], cnt_i[:])); wait()
            did(ve.tensor_tensor(upto[:], upto[:], tiles_e[:].unsqueeze(1).to_broadcast([P, E, E]), ALU.mult))
            did(ve.tensor_scalar(jump[:], tiles_e[:], float(-P), float(REGION), ALU.mult, ALU.add)); wait()
            did(ve.reduce_sum(last_e[:], upto[:], axis=AX)); wait()
            did(ve.tensor_tensor(passed, tile_no[:].unsqueeze(2).to_broadcast([P, SLOTS, E]),
                                 last_e[:].unsqueeze(1).to_broadcast([P, SLOTS, E]), ALU.is_ge)); wait()
            did(ve.reduce_sum(e_f[:], passed, axis=AX)); wait()
            did(ve.tensor_scalar(e_f[:], e_f[:], float(E - 1), None, ALU.min))
            did(ve.tensor_tensor(passed, passed, jump[:].unsqueeze(1).to_broadcast([P, SLOTS, E]), ALU.mult)); wait()
            did(ve.tensor_copy(e_i[:], e_f[:]))
            did(ve.reduce_sum(row_f[:], passed, axis=AX)); wait()
            did(ve.scalar_tensor_tensor(out=row_i[:], in0=tile_no[:], scalar=float(P), in1=row_f[:],
                                        op0=ALU.mult, op1=ALU.add)); wait()
            ve.nop().then_inc(s_plan, 1)

            dve.sem_inc(s_lo, LEAD)
            dve.sem_inc(s_ysb, LEAD)
            dve.sem_inc(s_to, 4)

            def experts(t, q, r):
                fixed = isinstance(t, int)
                if not fixed or t >= 3:
                    m = (q - 3) % 4
                    dve.wait_ge(s_y, t - 3 + 1 + LEAD)
                    dve.wait_ge(s_ylo, t - 3 + 1)
                    ve.scalar_tensor_tensor(out=y_sb[m][:], in0=bank[5 + m % 2][:, 0:D], scalar=scale[:, 6:7],
                                            in1=y_lo[m % 2][:], op0=ALU.mult, op1=ALU.add).then_inc(s_ysb, 1)
                if not fixed or t < SLOTS:
                    dve.wait_ge(s_xin[q], r * 4 + 16)
                    dve.wait_ge(s_ysc[q], r * 4)
                    meta = xin[q][:].bitcast(fp32)
                    ve.tensor_scalar(y_to[q][:], meta[:, D:D + 1], e_f[:, bass.ds(t, 1)], meta[:, D + 1:D + 2],
                                     ALU.not_equal, ALU.add).then_inc(s_to, 1)
                if not fixed or 1 <= t <= SLOTS:
                    par = (q - 1) % 2
                    dve.wait_ge(s_hi, t)
                    ve.scalar_tensor_tensor(out=hT[par][:, 1, :, :], in0=bank[3 + par][:].rearrange("p (c k) -> p c k", c=IC),
                                            scalar=scale[:, 4:5], in1=hT[par][:, 0, :, :],
                                            op0=ALU.mult, op1=ALU.subtract).then_inc(s_lo, 1)
            run_experts(dve, experts)

            dve.wait_ge(s_imp, 1)
            did(ve.tensor_reduce(imp[:], bank[7][:, 0:TILES * E].rearrange("p (t e) -> p e t", e=E),
                                 axis=AX, op=ALU.add)); wait()
            did(ve.tensor_scalar(imp[:], imp[:], -1.0, 1.0 - 0.9, ALU.add, ALU.mult)); wait()
            did(ve.tensor_scalar(imp[:], imp[:], 1.0, 0.01, ALU.add, ALU.add)); wait()
            for k in range(TOP):
                did(ve.tensor_tensor(bal[:, k], picked[:, k], imp[:].unsqueeze(1).to_broadcast([P, TILES, E]), ALU.mult))
            wait()
            did(ve.reduce_sum(wgt[:], bal[:], axis=AX)); wait()
            did(ve.reciprocal(wgt[:], wgt[:])); wait()
            did(ve.tensor_tensor(wgt[:], wgt[:], top_p[:], ALU.mult)); wait()
            did(ve.tensor_tensor(wsum[:], wgt[:, 0, :], wgt[:, 1, :], ALU.add)); wait()
            did(ve.reciprocal(wsum[:], wsum[:])); wait()
            did(ve.tensor_tensor(wgt[:], wgt[:], wsum[:].unsqueeze(1).to_broadcast([P, TOP, TILES]), ALU.mult)); wait()
            for g in range(TILES // 4):
                dve.wait_ge(s_back[g % 4], 16 * (g // 4 + 1))
                for k in range(TOP):
                    for u in range(4):
                        t = 4 * g + u
                        did(ve.scalar_tensor_tensor(out=h[:, t, :], in0=back[g % 4][:, u, k, :],
                                                    scalar=wgt[:, k, t:t + 1], in1=h[:, t, :],
                                                    op0=ALU.mult, op1=ALU.add))
                    wait()
                ve.nop().then_inc(s_fin, 1)

        @block.scalar
        def _(act):
            ac = nc.scalar

            links = Steps(act, s_ac2)

            def square_room(n):
                if n >= 2:
                    act.wait_ge(s_ac, n - 1)

            def guess(n, var, eps_col, done):
                links.did(ac.activation(root_ln[:, n, :], var, ACT.Ln, bias=eps[:, eps_col:eps_col + 1])); links.wait()
                ac.activation(root_0[:, n, :], root_ln[:, n, :], ACT.Exp, scale=-0.5).then_inc(done, 1)

            def embedding_guess(k):
                act.wait_ge(s_wv, k + 1)
                guess(0, mv_w[:, :, 1], 0, s_wg)

            def first_guess(k):
                act.wait_ge(s_hv, k + 1)
                guess(1, mv_h[:, :, 1], 1, s_hg)

            def batch_guess(k):
                act.wait_ge(s_bv, k + 1)
                links.did(ac.copy(batch_var[:], bank[7][:, AT_BATCH:AT_BATCH + CH])); links.wait()
                guess(2, batch_var[:], 1, s_bg)

            def second_guess(r):
                act.wait_ge(s_r2v, r + 1)
                guess(3, mv2[:, CH * r:CH * (r + 1), 1], 1, s_r2)

            def normalise(j):
                act.wait_ge(s_coef, j // 2 + 1)
                need(act, s_xt, j - 1)
                for u in range(2):
                    t = 2 * j + u
                    last = ac.activation(xn[j % 2][:, u, :], h[:, t, :], ACT.Identity, scale=coef1[:, t:t + 1],
                                         bias=shift1[:, t:t + 1])
                last.then_inc(s_xn, 1)

            def keep_xnT(j):
                act.wait_ge(s_xt, j + 1)
                need(act, s_s, j - 1)
                need(act, s_v, j - 1)
                ac.copy(xnT[j % 2][:, 0, :], bank[0][:, 0:2 * P])
                ac.copy(xnT[j % 2][0:D2, 1, :], bank[0][0:D2, 2 * P:4 * P]).then_inc(s_xtsb, 1)

            def keep_g(j):
                act.wait_ge(s_g, j + 1)
                need(act, s_s, j - 1)
                ac.copy(gT[j % 2][:, 0, :], bank[1][:, 0:2 * P])
                ac.copy(gT[j % 2][0:D2, 1, :], bank[1][0:D2, 2 * P:4 * P]).then_inc(s_gsb, 1)

            def keep_v(j):
                act.wait_ge(s_v, j + 1)
                need(act, s_o, j - 1)
                ac.copy(v_sb[j % 2][:].rearrange("p u d -> p (u d)"), bank[2][:, 0:2 * D]).then_inc(s_vsb, 1)

            def softmax(j):
                par = j % 2
                act.wait_ge(s_max, j + 1)
                need(act, s_pt_, j - 1)
                need(act, s_res, j - 1)
                for u in range(2):
                    last = ac.activation(pr[par][:, u, :], bank[3][:, u * P:(u + 1) * P], ACT.Exp,
                                         bias=nmax[par][:, u:u + 1], accum_out=rsum[par][:, u:u + 1])
                last.then_inc(s_p, 1)

            def keep_pT(j):
                act.wait_ge(s_pt_, j + 1)
                need(act, s_o, j - 1)
                ac.copy(prT[j % 2][:].rearrange("p u k -> p (u k)"), bank[3][:, 2 * P:4 * P]).then_inc(s_ptsb, 1)

            def second_norm(r):
                act.wait_ge(s_r2c, r + 1)
                need(act, s_rows, r)
                for t in range(CH):
                    last = ac.activation(x2[:, t, :], h[:, CH * r + t, :], ACT.Identity, scale=root[:, 3, t:t + 1],
                                         bias=shift2[:, t:t + 1])
                last.then_inc(s_x2, 1)

            def keep_x2T(r, q):
                need(act, s_lg, r)
                act.wait_ge(s_x2t, 2 * r + q + 1)
                ac.copy(x2T[:, 2 * q:2 * q + 2, :, :].rearrange("p u k t -> p (u k t)"),
                        bank[6][:].bitcast(fp16)[:, 0:6 * P]).then_inc(s_x2tsb, 1)

            def exp_logits(r):
                act.wait_ge(s_lgx, r + 1)
                ac.activation(lg[:], lg[:], ACT.Exp, scale=scale[:, 7:8]).then_inc(s_ex, 1)

            w2_s = stage[:].rearrange("p e a i -> p (e a i)")[:, 0:E * IC * D].rearrange("p (e c d) -> p e c d", e=E, c=IC)

            def square_w1(n):
                square_room(1 + n)
                ac.activation(junk[(1 + n) % 2], stage[:, n // 2, n % 2, :], ACT.Square,
                              accum_out=sq[:, 1, n:n + 1]).then_inc(s_ac, 1)

            def square_w2(n):
                square_room(17 + n)
                ac.activation(junk[(17 + n) % 2][:, 0:2 * D].rearrange("p (c d) -> p c d", c=2),
                              w2_s[:, n // 2, 2 * (n % 2):2 * (n % 2) + 2], ACT.Square,
                              accum_out=sq[:, 2, n:n + 1]).then_inc(s_ac, 1)

            def weights(j):
                if -4 <= j < 0:
                    act.wait_ge(s_w1in, 48)
                    for n in range(4 * (j + 4), 4 * (j + 5)):
                        square_w1(n)
                if 2 <= j < 6:
                    act.wait_ge(s_scale, 1)
                    for n in range(4 * (j - 2), 4 * (j - 1)):
                        e, k = n // 2, n % 2
                        last = ac.activation(w1[:, e, 2 * k, :], stage[:, e, k, :], ACT.Copy, scale=scale[:, 0:1])
                    last.then_inc(s_whi, 1)
                if 8 <= j < 12:
                    act.wait_ge(s_w2in, 16)
                    for n in range(4 * (j - 8), 4 * (j - 7)):
                        square_w2(n)
                if 14 <= j < 18:
                    act.wait_ge(s_scale, 2)
                    for e in range(2 * (j - 14), 2 * (j - 13)):
                        last = ac.activation(w2[:, e, :, 0, :], w2_s[:, e], ACT.Copy, scale=scale[:, 2:3])
                    last.then_inc(s_whi, 1)

            nc.scalar.preload_act_table_set("natural_log_exp_and_others")
            act.wait_ge(s_eps, 2)
            act.wait_ge(s_rin, 48)
            ac.activation(junk[0][:, 0:2 * E], rt_f[:].rearrange("p a e -> p (a e)"), ACT.Square,
                          accum_out=sq[:, 0, 0:1]).then_inc(s_ac, 1)
            for j in STEPS:
                c = j // 2
                if pair(j):
                    softmax(j)
                if j % 2 == 0:
                    if chunk(c + 3):
                        embedding_guess(c + 3)
                    if chunk(c + 2):
                        first_guess(c + 2)
                    if chunk(c - 3):
                        exp_logits(c - 3)
                if pair(j + 1):
                    keep_g(j + 1)
                    keep_v(j + 1)
                if pair(j + 2):
                    normalise(j + 2)
                if j % 2 == 0:
                    if chunk(c - 2):
                        keep_x2T(c - 2, 0)
                if pair(j):
                    keep_pT(j)
                if j % 2 == 0 and chunk(c - 2):
                    keep_x2T(c - 2, 1)
                if pair(j + 2):
                    keep_xnT(j + 2)
                if j % 2 == 0 and chunk(c + 2):
                    batch_guess(c + 2)
                if chunk(c - 1):
                    if j % 2 == 0:
                        second_guess(c - 1)
                    else:
                        second_norm(c - 1)
                weights(j)

            for x in (s_xftsb, s_hs):
                act.sem_inc(x, LEAD)

            def experts(t, q, r):
                fixed = isinstance(t, int)
                if not fixed or 1 <= t <= SLOTS:
                    par = (q - 1) % 2
                    act.wait_ge(s_h1, t + LEAD)
                    act.wait_ge(s_ht, t - 1 + LEAD - 1)
                    ac.activation(hs[par][:], bank[1 + par][:], ACT.Silu, scale=scale[:, 1:2]).then_inc(s_hs, 1)
                if not fixed or t < SLOTS:
                    act.wait_ge(s_xft, t + 1 + 4)
                    act.wait_ge(s_h1, t + 1)
                    ac.copy(xT[q % 2][:].rearrange("p k t -> p (k t)"), bank[0][:].bitcast(fp16)[:, 0:3 * P])\
                      .then_inc(s_xftsb, 1)
                if not fixed or t >= 3:
                    par = (q - 3) % 2
                    act.wait_ge(s_y, t - 3 + 1 + LEAD)
                    act.wait_ge(s_ysb, t - 5 + 1 + LEAD)
                    ac.activation(y_lo[par][:], bank[5 + par][:, D:2 * D], ACT.Copy, scale=scale[:, 6:7]).then_inc(s_ylo, 1)
                if not fixed or 1 <= t <= SLOTS:
                    par = (q - 1) % 2
                    act.wait_ge(s_ht, t + LEAD)
                    act.wait_ge(s_y, t)
                    ac.activation(hT[par][:, 0, :, :].rearrange("p c k -> p (c k)"), bank[3 + par][:], ACT.Copy,
                                  scale=scale[:, 4:5]).then_inc(s_hi, 1)
            run_experts(act, experts)
            out_v = out.rearrange("b p d -> p b d")
            for g in range(TILES // 4):
                act.wait_ge(s_fin, g + 1)
                act.dma_start(out_v[:, 4 * g:4 * g + 4, :], h[:, 4 * g:4 * g + 4, :]).then_inc(s_out[g % 4], 16)
            for g in range(4):
                act.wait_ge(s_out[g], 32)


def kernel(x, mask_BS_i1_0, pos_BS, L0_tok_word_emb, L0_tok_pos_emb, L0_tok_type_emb, L0_tok_gamma,
           L0_tok_beta, L0_attn_Wk, L0_attn_Wq, L0_attn_Wv, L0_ffn_router_w, L0_ffn_w1, L0_ffn_w2):
    import numpy as np
    import concourse.bacc as bacc
    from concourse.bass_utils import run_bass_kernel_spmd

    B, S = x.shape
    E, I, D = L0_ffn_w1.shape
    w2 = np.asarray(L0_ffn_w2).reshape(E, D, I // 128, 128)
    arrays = {
        "ids": np.asarray(x).T,
        "pt_rows": np.stack([np.asarray(pos_BS).reshape(1, B // 4, 4 * S),
                             np.asarray(mask_BS_i1_0).reshape(1, B // 4, 4 * S)], axis=2),
        "word_emb": np.asarray(L0_tok_word_emb),
        "pos_emb": np.asarray(L0_tok_pos_emb),
        "type_emb": np.asarray(L0_tok_type_emb),
        "gamma": np.asarray(L0_tok_gamma).reshape(1, D),
        "beta": np.asarray(L0_tok_beta).reshape(1, D),
        "wq": np.asarray(L0_attn_Wq),
        "wk": np.asarray(L0_attn_Wk),
        "wv_t": np.asarray(L0_attn_Wv).T,
        "router_t": np.asarray(L0_ffn_router_w).T,
        "w1_t": np.asarray(L0_ffn_w1).transpose(2, 0, 1).reshape(D, E * I),
        "w2_t": w2.transpose(3, 0, 2, 1).reshape(128, E * (I // 128) * D),
    }
    arrays = {k: np.ascontiguousarray(v) for k, v in arrays.items()}
    nc = bacc.Bacc("TRN2", target_bir_lowering=False, num_devices=1)
    args = [nc.dram_tensor(k, v.shape, mybir.dt.from_np(v.dtype), kind="ExternalInput").ap()
            for k, v in arrays.items()]
    out = nc.dram_tensor("out", (B, S, D), mybir.dt.float32, kind="ExternalOutput").ap()
    tower_kernel(nc, *args, out)
    r = run_bass_kernel_spmd(nc, [arrays], core_ids=[0])
    return r.results[0]["out"]
```

```python
import concourse.bass as bass
from concourse import mybir
from contextlib import ExitStack


def tower_kernel(nc, ids, pt_rows, word_emb, pos_emb, type_emb, gamma, beta,
                 wq, wk, wv_t, router_t, w1_t, w2_t, out):
    fp32, fp16, bf16, i32, u32 = (mybir.dt.float32, mybir.dt.float16, mybir.dt.bfloat16,
                                  mybir.dt.int32, mybir.dt.uint32)
    ALU = mybir.AluOpType
    ACT = mybir.ActivationFunctionType
    AX = mybir.AxisListType.X

    P = 128
    D = word_emb.shape[1]
    D2 = D - P
    TILES = ids.shape[1]
    TOKENS = TILES * P
    E = router_t.shape[1]
    I = w1_t.shape[1] // E
    IC = I // P
    TOP = 2
    CH = 4
    CHUNKS = TILES // CH
    PAIRS = TILES // 2
    XC = 2 * D
    ROW = XC + 4
    REGION = TOKENS + P
    SLOTS = (TOP * TOKENS + E * (P - 1)) // P
    SLOTS = SLOTS + (-SLOTS) % 4
    REST = E * P
    PADS = 2 * E
    TRASH = PADS * TOP * P
    LEAD = 2

    ctx = ExitStack()
    with ctx:
        def sb(name, shape, dt=fp32):
            return ctx.enter_context(nc.sbuf_tensor(name, shape, dt))

        def sem(name):
            return ctx.enter_context(nc.semaphore(name))

        sorted_rows = nc.dram_tensor("sorted_rows", (E * REGION + REST, ROW), fp16, kind="Internal").ap()
        y_rows = nc.dram_tensor("y_rows", (TOP * TOKENS + TRASH, D), fp32, kind="Internal").ap()

        stage = sb("stage", [P, E, 2, I])
        w2_words = E * IC * D
        carved = [w2_words]

        def carve(shape, dt=fp32):
            n = 1
            for x in shape:
                n *= x
            words = n if dt == fp32 else n // 2
            at, carved[0] = carved[0], carved[0] + words
            ap = stage[:].rearrange("p e a i -> p (e a i)")[:, at:at + words]
            ap = ap if dt == fp32 else ap.bitcast(dt)
            names = " ".join("abc"[:len(shape)])
            return ap.rearrange(f"p ({names}) -> p {names}", **dict(zip("abc", shape))) if len(shape) > 1 else ap

        ident = sb("ident", [P, P])
        ident16 = sb("ident16", [P, P], fp16)
        before = sb("before", [P, P], bf16)
        ones_b = sb("ones_b", [P, P], bf16)
        mean_w = sb("mean_w", [P, P])
        ones_f = sb("ones_f", [P, P])
        part = sb("part", [P, 2])
        part_i = sb("part_i", [P, 2], i32)
        iota_e = sb("iota_e", [P, E])
        token2 = sb("token2", [P, TILES])
        base = sb("base", [P, E])
        upto = sb("upto", [P, E, E])
        tile_no = sb("tile_no", [P, SLOTS])
        ids_sb = sb("ids_sb", [P, TILES], i32)
        gb = sb("gb", [P, 2, D])
        tab = sb("tab", [P, 2, D])
        tab_p = [sb(f"tab_p{n}", [P, 2, D], bf16) for n in range(3)]
        type_p = sb("type_p", [P, D], bf16)
        pt_ids = [sb(f"pt_ids{n}", [P, 2, CH * P], i32) for n in range(2)]
        onehot = sb("onehot", [P, 2, CH * P], bf16)
        h = sb("h", [P, TILES, D])
        word = sb("word", [P, TILES, D])
        st_w = sb("st_w", [P, CH, 6])
        mv_w = sb("mv_w", [P, CH, 2])
        st_h = sb("st_h", [P, CH, 6])
        mv_h = sb("mv_h", [P, CH, 2])
        eps = sb("eps", [P, 2])
        root_ln = sb("root_ln", [P, 4, CH])
        root_0 = sb("root_0", [P, 4, CH])
        root_t = sb("root_t", [P, 4, CH])
        root = sb("root", [P, 4, CH])
        batch_var = sb("batch_var", [P, CH])
        rowvar = sb("rowvar", [P, CH])
        var_eps = sb("var_eps", [P, CH])
        coef1 = sb("coef1", [P, TILES])
        shift1 = sb("shift1", [P, TILES])
        shift2 = sb("shift2", [P, CH])
        mv2 = sb("mv2", [P, TILES, 2])
        wq_sb = sb("wq_sb", [P, 2, D])
        wk_sb = sb("wk_sb", [P, 2, D])
        wv_sb = sb("wv_sb", [P, 2, D])
        wqk = sb("wqk", [P, 2, D])
        xn = [sb(f"xn{n}", [P, 2, D]) for n in range(2)]
        xnT = [sb(f"xnT{n}", [P, 2, 2 * P]) for n in range(2)]
        gT = [sb(f"gT{n}", [P, 2, 2 * P]) for n in range(2)]
        v_sb = [sb(f"v_sb{n}", [P, 2, D]) for n in range(2)]
        tab_r = v_sb[0]
        pr = [sb(f"pr{n}", [P, 2, P]) for n in range(2)]
        prT = [sb(f"prT{n}", [P, 2, P]) for n in range(2)]
        nmax = [sb(f"nmax{n}", [P, 2]) for n in range(2)]
        rsum = [sb(f"rsum{n}", [P, 2]) for n in range(2)]
        rinv = [sb(f"rinv{n}", [P, 2]) for n in range(2)]
        st2 = [sb(f"st2{n}", [P, 2, 6]) for n in range(2)]
        x2 = sb("x2", [P, CH, D])
        rows = [sb(f"rows{n}", [P, CH, ROW], fp16) for n in range(4)]
        x2T = sb("x2T", [P, CH, 3, P], fp16)
        rt_f = sb("rt_f", [P, 2, E])
        rt = sb("rt", [P, 4, E], fp16)
        lmax = sb("lmax", [P, CH])
        lg = sb("lg", [P, CH, E])
        esum = sb("esum", [P, CH])
        probs = sb("probs", [P, TILES, E])
        top8 = sb("top8", [P, CH, 8])
        idx8 = sb("idx8", [P, CH, 8], u32)
        idxf = sb("idxf", [P, CH, TOP])
        picked = sb("picked", [P, TOP, TILES, E])
        top_p = sb("top_p", [P, TOP, TILES])
        marks = sb("marks", [P, CH + 1, E], bf16)
        place = sb("place", [P, CH, E])
        place_k = sb("place_k", [P, TOP, CH, E])
        slot_f = sb("slot_f", [P, TOP, CH])
        slot = [sb(f"slot{n}", [P, TOP, CH], i32) for n in range(2)]
        w1 = sb("w1", [P, E, 4, I], fp16)
        w2 = sb("w2", [P, E, IC, 2, D], fp16)
        sq = sb("sq", [P, 3, 16])
        sqs = sb("sqs", [P, 7])
        scale_i = sb("scale_i", [P, 4, 2], i32)
        scale = sb("scale", [P, 8])
        cnt = sb("cnt", [P, E])
        cnt_i = sb("cnt_i", [P, E], i32)
        tiles_e = sb("tiles_e", [P, E])
        jump = sb("jump", [P, E])
        last_e = sb("last_e", [P, E])
        e_f = sb("e_f", [P, SLOTS])
        row_f = sb("row_f", [P, SLOTS])
        e_i = sb("e_i", [P, SLOTS], i32)
        row_i = sb("row_i", [P, SLOTS], i32)
        base_i = sb("base_i", [P, E], i32)
        xin = [carve((ROW,), fp16) for n in range(4)]
        xT = [carve((3, P), fp16) for n in range(2)]
        carved[0] = 0
        hs = [carve((I,)) for n in range(2)]
        hT = [carve((2, IC, P), fp16) for n in range(2)]
        y_lo = [carve((D,)) for n in range(2)]
        y_sb = [carve((D,)) for n in range(4)]
        y_to = [sb(f"y_to{n}", [P, 1], i32) for n in range(4)]
        imp = sb("imp", [P, E])
        bal = sb("bal", [P, TOP, TILES, E])
        wgt = sb("wgt", [P, TOP, TILES])
        wsum = sb("wsum", [P, TILES])
        junk = [bal[:].rearrange("p k t e -> p (k t e)").bitcast(bf16)[:, n * I:(n + 1) * I] for n in range(2)]
        word_f = word[:].rearrange("p t d -> p (t d)")
        n_pads = PADS * ROW // 2
        pads = word_f[:, 0:n_pads].rearrange("p (n r) -> p n r", n=PADS)
        passed = word_f[:, n_pads:n_pads + SLOTS * E].rearrange("p (t e) -> p t e", e=E)
        BACK = 2
        backs = TILES // (TOP * BACK)
        back = [word[:, TOP * BACK * n:TOP * BACK * (n + 1), :].rearrange("p (b k) d -> p b k d", k=TOP)
                for n in range(backs)]

        STEPS = range(-8, PAIRS + 5)

        def chunk(k):
            return 0 <= k < CHUNKS

        def pair(j):
            return 0 <= j < PAIRS

        def late(r):
            return CHUNKS - 3 <= r < CHUNKS

        def early(r):
            return 0 <= r < CHUNKS - 3

        W1_HIGH, W2_SQUARES, W2_SUM = 2, (12, 13, 14, 17), 18
        ROUTER_SUM = -2

        AT_RANKS, AT_BATCH = CH * E, (2 * CH + 1) * E
        bank = [ctx.enter_context(nc.psum_tensor(f"bank{n}", [P, 512], fp32)) for n in range(8)]

        s_ids, s_small, s_attw, s_gb = sem("ids_in"), sem("small_in"), sem("attn_w_in"), sem("gb_in")
        s_w1in, s_w2in, s_rin = sem("w1_in"), sem("w2_in"), sem("router_in")
        s_word = [sem(f"words_in{n}") for n in range(4)]
        s_pt = [sem(f"pt_ids_in{n}") for n in range(2)]
        s_const = sem("const_ready")
        s_vc, s_ac, s_gc = sem("vector_step"), sem("squares_done"), sem("gpsimd_step")
        s_ac2 = sem("scalar_step")
        s_alone = sem("waits_alone")
        s_tab = sem("tables_ready")
        s_wqk, s_wqk_sb = sem("wqk_done"), sem("wqk_ready")
        s_oh, s_emb, s_embadd = sem("onehot_ready"), sem("emb_done"), sem("emb_added")
        s_wv, s_hv, s_coef = sem("word_variances_ready"), sem("h_variances_ready"), sem("coefs_ready")
        s_wg, s_hg, s_bg = sem("word_guesses_ready"), sem("h_guesses_ready"), sem("batch_guesses_ready")
        s_rowvar, s_bv = sem("rowvar_ready"), sem("batch_var_done")
        s_r2v, s_r2 = sem("second_variances_ready"), sem("second_guesses_ready")
        s_r2c, s_x2 = sem("second_coefs_ready"), sem("x2_ready")
        s_eps = sem("eps_ready")
        s_xn, s_xt, s_xtsb = sem("xn_ready"), sem("xnT_done"), sem("xnT_ready")
        s_g, s_gsb, s_v, s_vsb = sem("g_done"), sem("g_ready"), sem("v_done"), sem("v_ready")
        s_s, s_max, s_p = sem("scores_done"), sem("max_ready"), sem("p_ready")
        s_pt_, s_ptsb, s_o, s_res = sem("pT_done"), sem("pT_ready"), sem("o_done"), sem("residual_added")
        s_rows, s_x2t, s_x2tsb, s_lg = sem("rows_ready"), sem("x2T_done"), sem("x2T_ready"), sem("logits_done")
        s_lgx, s_ex, s_mk, s_rk = sem("logits_shifted"), sem("exp_ready"), sem("marks_ready"), sem("ranks_done")
        s_slot = sem("slots_ready")
        s_scat = [sem(f"scattered{n}") for n in range(4)]
        s_sq, s_sqs, s_scale = sem("squares_ready"), sem("squares_summed"), sem("scale_ready")
        s_whi, s_wlo = sem("w_high_ready"), sem("w_low_ready")
        s_base, s_plan, s_pads, s_pad = sem("bases_ready"), sem("plan_ready"), sem("padding_ready"), sem("padding_written")
        s_xin = [sem(f"x_in{n}") for n in range(4)]
        s_xft, s_xftsb, s_h1, s_hs = sem("xT_done"), sem("xT_ready"), sem("h_done"), sem("silu_ready")
        s_ht, s_hi, s_lo = sem("hT_done"), sem("hT_high_ready"), sem("hT_low_ready")
        s_y, s_ylo, s_ysb, s_to = sem("y_done"), sem("y_low_ready"), sem("y_ready"), sem("y_place_ready")
        s_ysc = [sem(f"y_scattered{n}") for n in range(4)]
        s_imp, s_wgt = sem("importance_done"), sem("weights_ready")
        s_back = [sem(f"y_back{n}") for n in range(backs)]
        s_fin = sem("result_ready")
        s_out = [sem(f"result_out{n}") for n in range(4)]

        class Steps:

            def __init__(self, eng, s):
                self.eng, self.s, self.n = eng, s, 0

            def did(self, ins):
                self.n += 1
                ins.then_inc(self.s, 1)
                return self.n

            def wait(self, link=None):
                self.eng.wait_ge(self.s, self.n if link is None else link)


        def alone(eng):
            eng.sem_inc(s_alone, 1)

        def need(eng, s, n):
            if n > 0:
                eng.wait_ge(s, n)

        def mm(out_, lhsT, rhs, start, stop):
            return nc.tensor.matmul(out_, lhsT, rhs, start=start, stop=stop)

        def run_experts(eng, step):
            for t in range(4):
                step(t, t, 0)
            with eng.Fori(1, SLOTS // 4) as i:
                for q in range(4):
                    step(i * 4 + q, q, i * 4)
            for t in range(SLOTS, SLOTS + 3):
                step(t, t % 4, t - t % 4)

        block = ctx.enter_context(nc.Block())

        @block.sync
        def _(sp):
            sp.dma_start(ids_sb[:], ids).then_inc(s_ids, 16)
            sp.dma_start(tab[:, 0, :], pos_emb).then_inc(s_small, 16)
            sp.wait_ge(s_const, 1)
            for n in range(3):
                sp.dma_start(tab[32 * n:32 * n + 2, 1, :], type_emb).then_inc(s_small, 16)

            def chunk_ids(k):
                need(sp, s_oh, k - 1)
                sp.dma_start(pt_ids[k % 2][:], pt_rows[:, k, :, :].partition_broadcast(P)).then_inc(s_pt[k % 2], 16)
            chunk_ids(0)
            chunk_ids(1)
            sp.dma_start(gb[:, 0, :], gamma.partition_broadcast(P)).then_inc(s_gb, 16)
            sp.dma_start(gb[:, 1, :], beta.partition_broadcast(P)).then_inc(s_gb, 16)
            for dst, src in ((wq_sb, wq), (wk_sb, wk), (wv_sb, wv_t)):
                sp.dma_start(dst[:, 0, :], src[0:P, :]).then_inc(s_attw, 16)
                sp.dma_start(dst[0:D2, 1, :], src[P:D, :]).then_inc(s_attw, 16)
            sp.dma_start(rt_f[:, 0, :], router_t[0:P, :]).then_inc(s_rin, 16)
            sp.dma_start(rt_f[0:D2, 1, :], router_t[P:D, :]).then_inc(s_rin, 16)
            sp.dma_start(rt_f[D2:P, 1, :], router_t[P:D, :]).then_inc(s_rin, 16)
            w1_v = w1_t.rearrange("d (e i) -> d e i", e=E)
            for e in range(0, E, 2):
                sp.dma_start(stage[:, e:e + 2, 0, :], w1_v[0:P, e:e + 2, :]).then_inc(s_w1in, 16)
                sp.dma_start(stage[0:D2, e:e + 2, 1, :], w1_v[P:D, e:e + 2, :]).then_inc(s_w1in, 16)
                sp.dma_start(stage[D2:P, e:e + 2, 1, :], w1_v[P:D, e:e + 2, :]).then_inc(s_w1in, 16)
            for k in range(2, CHUNKS):
                chunk_ids(k)
            sp.wait_ge(s_wlo, 2)
            sp.dma_start(stage[:].rearrange("p e a i -> p (e a i)")[:, 0:E * IC * D], w2_t).then_inc(s_w2in, 16)

            sp.wait_ge(s_pads, 1)
            for e in range(E):
                sp.dma_start(sorted_rows[E * REGION + e * P:E * REGION + (e + 1) * P, :], pads[:, E + e, :].bitcast(fp16))\
                  .then_inc(s_pad, 16)
            sp.wait_ge(s_base, 1)
            for e in range(E):
                at = nc.sync.value_load(base_i[0:1, e:e + 1], min_val=0, max_val=E * REGION)
                sp.dma_start(sorted_rows[bass.ds(at, P), :], pads[:, e, :].bitcast(fp16)).then_inc(s_pad, 16)
            sp.wait_ge(s_pad, 2 * E * 16)
            sp.wait_ge(s_plan, 1)
            for n in range(4):
                sp.wait_ge(s_scat[n], 16 * TOP * CH * (CHUNKS // 4))
            with sp.Fori(0, SLOTS // 4) as i:
                for q in range(4):
                    at = nc.sync.value_load(row_i[0:1, bass.ds(i * 4 + q, 1)], min_val=0,
                                            max_val=E * REGION + REST - P)
                    sp.wait_ge(s_xft, i * 4 + (q + 1))
                    sp.wait_ge(s_to, i * 4 + (q + 1))
                    sp.dma_start(xin[q][:], sorted_rows[bass.ds(at, P), :]).then_inc(s_xin[q], 16)
            for q in range(4):
                sp.wait_ge(s_ysc[q], 16 * SLOTS // 4)
            y_v = y_rows[0:TOP * TOKENS, :].rearrange("(b p k) d -> p b (k d)", p=P, k=TOP)
            for g in range(TILES // BACK):
                need(sp, s_fin, g - backs + 1)
                sp.dma_start(back[g % backs].rearrange("p b k d -> p b (k d)"), y_v[:, BACK * g:BACK * (g + 1), :])\
                  .then_inc(s_back[g % backs], 16)
            for g in range(4):
                sp.wait_ge(s_out[g], 16 * TILES // BACK // 4)

        @block.gpsimd
        def _(pool):
            gp = nc.gpsimd
            links = Steps(pool, s_gc)
            gp.memset(tab[:, 1, :], 0.0).then_inc(s_const, 1)
            gp.memset(eps[:, 0:1], 1e-12).then_inc(s_eps, 1)
            gp.memset(eps[:, 1:2], 1e-5).then_inc(s_eps, 1)
            links.did(gp.memset(ident[:], 0.0))
            links.did(gp.memset(ident16[:], 0.0))
            links.did(gp.memset(before[:], 1.0))
            links.did(gp.memset(upto[:], 1.0))
            links.did(gp.memset(ones_b[:], 1.0))
            links.did(gp.memset(ones_f[:], 1.0))
            links.did(gp.memset(mean_w[:], 1.0 / P))
            links.did(gp.memset(marks[:], 0.0))
            links.wait()
            for m in (ident, ident16):
                links.did(gp.affine_select(out=m[:], in_=m[:], compare_op=ALU.not_equal, fill=1.0, base=0,
                                           pattern=[[-1, P]], channel_multiplier=1))
            links.did(gp.affine_select(out=before[:], in_=before[:], compare_op=ALU.is_gt, fill=0.0, base=0,
                                       pattern=[[1, P]], channel_multiplier=-1))
            links.did(gp.affine_select(out=upto[:], in_=upto[:], compare_op=ALU.is_ge, fill=0.0, base=0,
                                       pattern=[[1, E], [-1, E]], channel_multiplier=0))
            links.did(gp.iota(part_i[:, 0:1], [[0, 1]], base=0, channel_multiplier=1))
            for dst, pat, mult in ((iota_e[:], [[1, E]], 0), (token2[:], [[2 * P, TILES]], 2),
                                   (base[:], [[REGION, E]], 0), (tile_no[:], [[1, SLOTS]], 0)):
                links.did(gp.iota(dst, pat, base=0, channel_multiplier=mult,
                                  allow_small_or_imprecise_dtypes=True))
            links.wait()
            gp.nop().then_inc(s_const, 1)
            pool.wait_ge(s_ids, 16)

            def words(c):
                need(pool, s_word[c % 4], 16 * CH * (c // 4))
                for t in range(c * CH, (c + 1) * CH):
                    gp.indirect_dma_start(word[:, t, :], None, word_emb,
                                          bass.IndirectOffsetOnAxis(ids_sb[:, t:t + 1], 0))\
                      .then_inc(s_word[c % 4], 16)
            words(0)
            words(1)
            for c in range(2, CHUNKS):
                words(c)
            for r in range(CHUNKS):
                n = r % 4
                if r == CHUNKS - 5:
                    pool.wait_ge(s_rowvar, CHUNKS)
                    links.did(gp.memset(pads, 0.0))
                    links.wait()
                    links.did(gp.iota(pads[:, :, D + 1], [[TOP * P, PADS]], base=TOP * TOKENS, channel_multiplier=TOP,
                                      allow_small_or_imprecise_dtypes=True))
                    links.wait()
                    gp.nop().then_inc(s_pads, 1)
                pool.wait_ge(s_slot, r + 1)
                for k in range(TOP):
                    for t in range(CH):
                        gp.indirect_dma_start(sorted_rows, bass.IndirectOffsetOnAxis(slot[r % 2][:, k, t:t + 1], 0),
                                              rows[n][:, t, :], None).then_inc(s_scat[n], 16)
            with pool.Fori(0, SLOTS // 4) as i:
                for q in range(4):
                    pool.wait_ge(s_ysb, i * 4 + (q + 1 + LEAD))
                    alone(pool)
                    gp.indirect_dma_start(y_rows, bass.IndirectOffsetOnAxis(y_to[q][:], 0),
                                          y_sb[q][:], None).then_inc(s_ysc[q], 16)

        @block.tensor
        def _(pe):
            pe.wait_ge(s_const, 2)
            pe.wait_ge(s_tab, 1)

            xt, g, v, s, o, emb, x2t_b, small = [bank[n] for n in (0, 1, 2, 3, 4, 5, 6, 7)]

            def multiply_wq_wk():
                pe.wait_ge(s_attw, 6 * 16)
                for m, (lo, n) in enumerate(((0, P), (P, D2))):
                    mm(g[0:n, m * D:(m + 1) * D], wq_sb[:, 0, lo:lo + n], wk_sb[:, 0, :], True, False)
                    last = mm(g[0:n, m * D:(m + 1) * D], wq_sb[0:D2, 1, lo:lo + n], wk_sb[0:D2, 1, :], False, True)
                last.then_inc(s_wqk, 1)

            def embed(k, q):
                if q == 0:
                    pe.wait_ge(s_oh, k + 1)
                need(pe, s_embadd, 2 * k + q)
                for u in range(2):
                    dst = emb[:, u * D:(u + 1) * D]
                    t = slice((2 * q + u) * P, (2 * q + u + 1) * P)
                    for n in range(3):
                        mm(dst, onehot[:, 0, t], tab_p[n][:, 0, :], n == 0, False)
                    last = mm(dst, onehot[:, 1, t], type_p[:], False, True)
                last.then_inc(s_emb, 1)

            def batch_mean(k):
                pe.wait_ge(s_rowvar, k + 1)
                need(pe, s_lgx, k - 5 + 1)
                mm(small[:, AT_BATCH:AT_BATCH + CH], mean_w[:], rowvar[:], True, True).then_inc(s_bv, 1)

            def transpose_xn(j):
                par = j % 2
                pe.wait_ge(s_xn, j + 1)
                need(pe, s_xtsb, j)
                for u in range(2):
                    nc.tensor.transpose(xt[:, u * P:(u + 1) * P], xn[par][:, u, 0:P], ident[:])
                    last = nc.tensor.transpose(xt[0:D2, (2 + u) * P:(3 + u) * P], xn[par][:, u, P:D], ident[:])
                last.then_inc(s_xt, 1)

            def project(j):
                par = j % 2
                if j == 0:
                    pe.wait_ge(s_wqk_sb, 1)
                pe.wait_ge(s_xtsb, j + 1)
                need(pe, s_gsb, j)
                for m, (lo, n) in enumerate(((0, P), (P, D2))):
                    dst = g[0:n, m * 2 * P:(m + 1) * 2 * P]
                    mm(dst, wqk[:, 0, lo:lo + n], xnT[par][:, 0, :], True, False)
                    last = mm(dst, wqk[0:D2, 1, lo:lo + n], xnT[par][0:D2, 1, :], False, True)
                last.then_inc(s_g, 1)
                need(pe, s_vsb, j)
                for u in range(2):
                    dst = v[:, u * D:(u + 1) * D]
                    mm(dst, xnT[par][:, 0, u * P:(u + 1) * P], wv_sb[:, 0, :], True, False)
                    last = mm(dst, xnT[par][0:D2, 1, u * P:(u + 1) * P], wv_sb[0:D2, 1, :], False, True)
                last.then_inc(s_v, 1)

            def scores(j):
                par = j % 2
                pe.wait_ge(s_gsb, j + 1)
                need(pe, s_ptsb, j)
                for u in range(2):
                    dst, c = s[:, u * P:(u + 1) * P], slice(u * P, (u + 1) * P)
                    mm(dst, gT[par][:, 0, c], xnT[par][:, 0, c], True, False)
                    last = mm(dst, gT[par][0:D2, 1, c], xnT[par][0:D2, 1, c], False, True)
                last.then_inc(s_s, 1)

            def transpose_p(j):
                pe.wait_ge(s_p, j + 1)
                for u in range(2):
                    last = nc.tensor.transpose(s[:, (2 + u) * P:(3 + u) * P], pr[j % 2][:, u, :], ident[:])
                last.then_inc(s_pt_, 1)

            def attend(j):
                par = j % 2
                need(pe, s_res, j)
                if j == 0:
                    pe.wait_ge(s_sqs, 2)
                    mm(o[:, 2 * D:2 * D + 1], ones_f[:], sqs[:, 1:2], True, True)
                pe.wait_ge(s_ptsb, j + 1)
                pe.wait_ge(s_vsb, j + 1)
                for u in range(2):
                    last = mm(o[:, u * D:(u + 1) * D], prT[par][:, u, :], v_sb[par][:, u, :], True, True)
                last.then_inc(s_o, 1)

            x2t = x2t_b[:].bitcast(fp16)

            def transpose_rows(r, q):
                pe.wait_ge(s_rows, r + 1)
                need(pe, s_x2tsb, 2 * r + q)
                for u in range(2):
                    for k in range(3):
                        at = (3 * u + k) * P
                        last = nc.tensor.transpose(x2t[:, at:at + P],
                                                   rows[r % 4][:, 2 * q + u, k * P:(k + 1) * P], ident16[:])
                last.then_inc(s_x2t, 1)

            def logits(r):
                need(pe, s_slot, r)
                need(pe, s_bg, min(r + 5, CHUNKS))
                for t in range(CH):
                    pe.wait_ge(s_x2tsb, 2 * r + t // 2 + 1)
                    for k, (a, b) in enumerate(((0, 0), (1, 0), (0, 1), (2, 2), (2, 3))):
                        last = mm(small[:, t * E:(t + 1) * E], x2T[:, t, a, :], rt[:, b, :], k == 0, k == 4)
                last.then_inc(s_lg, 1)

            def ranks(r):
                pe.wait_ge(s_mk, r + 1)
                need(pe, s_bg, min(r + 6, CHUNKS))
                at = AT_RANKS
                mm(small[:, at:at + (CH + 1) * E], before[:], marks[:].rearrange("p t e -> p (t e)"), True, False)
                for t in range(CH):
                    last = mm(small[:, at + (t + 1) * E:at + (CH + 1) * E], ones_b[:],
                              marks[:, t:t + 1, :].to_broadcast([P, CH - t, E]), False, t == CH - 1)
                last.then_inc(s_rk, 1)

            for j in STEPS:
                c = j // 2
                if j == -3:
                    multiply_wq_wk()
                if j == ROUTER_SUM:
                    pe.wait_ge(s_sqs, 1)
                    mm(o[:, 2 * D:2 * D + 1], ones_f[:], sqs[:, 0:1], True, True).then_inc(s_sq, 1)
                if j == W2_SUM:
                    pe.wait_ge(s_sqs, 3)
                    need(pe, s_res, PAIRS)
                    mm(o[:, 2 * D:2 * D + 1], ones_f[:], sqs[:, 2:3], True, True).then_inc(s_sq, 1)
                if pair(j):
                    scores(j)
                if pair(j - 1):
                    attend(j - 1)
                if j % 2 == 0:
                    if late(c - 3):
                        ranks(c - 3)
                    if chunk(c + 4):
                        embed(c + 4, 0)
                    if pair(j + 1):
                        project(j + 1)
                    if chunk(c - 2):
                        transpose_rows(c - 2, 0)
                    if pair(j):
                        transpose_p(j)
                    if chunk(c - 2):
                        transpose_rows(c - 2, 1)
                    if pair(j + 2):
                        transpose_xn(j + 2)
                    if chunk(c + 2):
                        batch_mean(c + 2)
                else:
                    if early(c - 3):
                        ranks(c - 3)
                    if chunk(c + 4):
                        embed(c + 4, 1)
                    if pair(j + 1):
                        project(j + 1)
                    if chunk(c - 2):
                        logits(c - 2)
                    if pair(j):
                        transpose_p(j)
                    if pair(j + 2):
                        transpose_xn(j + 2)

            pe.wait_ge(s_slot, CHUNKS)
            mm(bank[7][:, 0:TILES * E], ones_f[:], probs[:].rearrange("p t e -> p (t e)"), True, True)\
                .then_inc(s_imp, 1)

            xt_b = bank[0][:].bitcast(fp16)
            h_b, ht_b, y_b = [bank[1], bank[2]], [bank[3], bank[4]], [bank[5], bank[6]]
            for x in (s_xft,):
                pe.sem_inc(x, 4)
            for x in (s_h1, s_ht, s_y):
                pe.sem_inc(x, LEAD)
            w1_f = w1[:].rearrange("p e a i -> p (e a i)")
            w2_f = w2[:].rearrange("p e c a d -> p (e c a d)")

            def load_experts(at, n):
                return nc.values_load_multi_w_load_instructions(
                    e_i[0:1, bass.ds(at, n)], engines=(mybir.EngineType.PE,), min_val=0, max_val=E - 1,
                    skip_runtime_bounds_check_because="the plan keeps it below E")[1]

            def experts(t, q, r):
                fixed = isinstance(t, int)
                if not fixed or 2 <= t <= SLOTS + 1:
                    par = (q - 2) % 2
                    pe.wait_ge(s_hs, t - 2 + 1 + LEAD)
                    pe.wait_ge(s_lo, t - 2 + LEAD - 1)
                    for c in range(IC):
                        last = nc.tensor.transpose(ht_b[par][:, c * P:(c + 1) * P],
                                                   hs[par][:, c * P:(c + 1) * P], ident[:])
                    last.then_inc(s_ht, 1)
                if fixed and t == 0:
                    loaded[0] = (None,) * 4 + tuple(load_experts(0, 4))
                if fixed and t == SLOTS:
                    loaded[0] = tuple(load_experts(SLOTS - 4, 4)) + (None,) * 4
                if not fixed and q == 0:
                    loaded[0] = tuple(load_experts(r - 4, 8))
                if not fixed or 1 <= t <= SLOTS:
                    e = loaded[0][4 + q - 1]
                    pe.wait_ge(s_xftsb, t + LEAD)
                    pe.wait_ge(s_hs, t - 1 + LEAD - 1)
                    for k, (a, b) in enumerate(((0, 0), (1, 0), (0, 1), (2, 2), (2, 3))):
                        last = mm(h_b[(q - 1) % 2][:], xT[(q - 1) % 2][:, a, :],
                                  w1_f[:, bass.ds(e * (4 * I) + b * I, I)], k == 0, k == 4)
                    last.then_inc(s_h1, 1)
                if not fixed or t < SLOTS:
                    pe.wait_ge(s_xin[q], r * 4 + 16)
                    pe.wait_ge(s_xftsb, t + LEAD)
                    for k in range(3):
                        last = nc.tensor.transpose(xt_b[:, k * P:(k + 1) * P], xin[q][:, k * P:(k + 1) * P], ident16[:])
                    last.then_inc(s_xft, 1)
                if not fixed or 3 <= t:
                    e = loaded[0][4 + q - 3]
                    par = (q - 3) % 2
                    if fixed and t == 3:
                        pe.wait_ge(s_wlo, 3)
                    pe.wait_ge(s_lo, t - 3 + 1 + LEAD)
                    pe.wait_ge(s_ysb, t - 5 + 1 + LEAD)
                    for c in range(IC):
                        at = e * (IC * 2 * D) + c * 2 * D
                        mm(y_b[par][:, 0:2 * D], hT[par][:, 0, c, :], w2_f[:, bass.ds(at, 2 * D)], c == 0, False)
                        last = mm(y_b[par][:, 0:D], hT[par][:, 1, c, :], w2_f[:, bass.ds(at, D)], False, c == IC - 1)
                    last.then_inc(s_y, 1)
            pe.wait_ge(s_plan, 1)
            pe.wait_ge(s_wlo, 2)
            loaded = [None]
            run_experts(pe, experts)
        @block.vector
        def _(dve):
            ve = nc.vector
            links = Steps(dve, s_vc)
            did, wait = links.did, links.wait


            def newton(n, link, var, eps_value, done):
                y, t = root_0[:, n, :], root_t[:, n, :]
                if link == 0:
                    return did(ve.scalar_tensor_tensor(out=t, in0=y, scalar=-0.5, in1=y, op0=ALU.mult, op1=ALU.mult))
                wait(done)
                if link == 1:
                    return did(ve.scalar_tensor_tensor(out=t, in0=var, scalar=eps_value, in1=t, op0=ALU.add, op1=ALU.mult))
                return did(ve.scalar_tensor_tensor(out=root[:, n, :], in0=t, scalar=1.5, in1=y, op0=ALU.add, op1=ALU.mult))

            dve.wait_ge(s_const, 2)
            dve.wait_ge(s_small, 64)
            did(ve.tensor_copy(tab_p[0][:], tab[:])); wait()
            did(ve.tensor_tensor(tab_r[:], tab[:], tab_p[0][:], ALU.subtract)); wait()
            did(ve.tensor_copy(tab_p[1][:], tab_r[:])); wait()
            did(ve.tensor_tensor(tab_r[:], tab_r[:], tab_p[1][:], ALU.subtract)); wait()
            did(ve.tensor_copy(tab_p[2][:], tab_r[:]))
            did(ve.memset(type_p[:], 0.0)); wait()
            for n in range(3):
                did(ve.tensor_copy(type_p[32 * n:32 * n + 2, :], tab_p[n][32 * n:32 * n + 2, 1, :]))
            did(ve.tensor_scalar(part_i[:, 1:2], part_i[:, 0:1], 31, None, ALU.bitwise_and)); wait()
            did(ve.tensor_copy(part[:], part_i[:])); wait()
            ve.nop().then_inc(s_tab, 1)
            dve.wait_ge(s_gb, 32)

            u0, sh = scale_i, 23
            sc = scale[:].bitcast(i32)

            def exponent(dst, src, mul, add):
                did(ve.tensor_scalar(dst, src, mul, add, ALU.mult, ALU.add)); wait()
                did(ve.tensor_scalar(dst, dst, sh, None, ALU.arith_shift_left)); wait()

            def exponent_of(n):
                u = u0[:, n, 0:1]
                did(ve.tensor_copy(sqs[:, 3 + n:4 + n], bank[4][:, 2 * D:2 * D + 1])); wait()
                did(ve.tensor_scalar(u, sqs[:, 3 + n:4 + n].bitcast(i32), 24, None, ALU.logical_shift_right)); wait()
                return u

            def low(dst, src, hi, by):
                return ve.scalar_tensor_tensor(out=dst, in0=src, scalar=by, in1=hi, op0=ALU.mult, op1=ALU.subtract)

            def sum_squares(n, squares, cols):
                dve.wait_ge(s_ac, squares)
                ve.reduce_sum(sqs[:, n:n + 1], sq[:, n, 0:cols], axis=AX).then_inc(s_sqs, 1)

            def w1_scales():
                u = exponent_of(1)
                exponent(sc[:, 0:1], u, -1.0, 202.0)
                exponent(sc[:, 1:2], u, 1.0, 52.0)
                exponent(sc[:, 4:5], u, -1.0, 198.0)
                exponent(sc[:, 5:6], u, 1.0, 56.0)
                ve.nop().then_inc(s_scale, 1)

            def w2_scales():
                u = exponent_of(2)
                exponent(sc[:, 2:3], u, -1.0, 202.0)
                exponent(sc[:, 3:4], u, 1.0, 52.0)
                did(ve.tensor_tensor(scale[:, 6:7], scale[:, 3:4], scale[:, 5:6], ALU.mult)); wait()
                ve.nop().then_inc(s_scale, 1)

            def keep_wqk():
                dve.wait_ge(s_wqk, 1)
                did(ve.tensor_copy(wqk[:, 0, :], bank[1][:, 0:D]))
                did(ve.tensor_copy(wqk[0:D2, 1, :], bank[1][0:D2, D:2 * D])); wait()
                ve.nop().then_inc(s_wqk_sb, 1)

            w2_s = stage[:].rearrange("p e a i -> p (e a i)")[:, 0:E * IC * D].rearrange("p (e c d) -> p e c d", e=E, c=IC)

            def weights(j, part):
                if j == 0 and part == 0:
                    sum_squares(1, 17, 16)
                if W1_HIGH < j <= W1_HIGH + 8 and part % 2 == 0:
                    if part == 0:
                        dve.wait_ge(s_whi, j - W1_HIGH)
                    n = 2 * (j - W1_HIGH - 1) + part // 2
                    e, k = n // 2, n % 2
                    done = did(low(w1[:, e, 2 * k + 1, :], stage[:, e, k, :], w1[:, e, 2 * k, :], scale[:, 0:1]))
                    if n == 15:
                        wait(done)
                        ve.nop().then_inc(s_wlo, 1)
                if j == W2_SUM - 1 and part == 3:
                    sum_squares(2, 33, 16)
                if j == W2_SUM and part == 3:
                    dve.wait_ge(s_sq, 2)
                    w2_scales()

            def router_parts():
                dve.wait_ge(s_sq, 1)
                u = exponent_of(0)
                exponent(sqs[:, 6:7].bitcast(i32), u, -1.0, 202.0)
                exponent(sc[:, 7:8], u, 1.0, 52.0)
                for k in range(2):
                    did(ve.tensor_scalar(rt[:, 2 * k, :], rt_f[:, k, :], sqs[:, 6:7], None, ALU.mult))
                wait()
                for k in range(2):
                    did(low(rt[:, 2 * k + 1, :], rt_f[:, k, :], rt[:, 2 * k, :], sqs[:, 6:7]))
                wait()
                ve.nop().then_inc(s_wlo, 1)

            def one_hots(k):
                need(dve, s_emb, 2 * k)
                dve.wait_ge(s_pt[k % 2], 16 * (k // 2 + 1))
                did(ve.tensor_scalar(onehot[:, 0, :], pt_ids[k % 2][:, 0, :], part[:, 0:1], None, ALU.is_equal))
                ve.tensor_scalar(onehot[:, 1, :], pt_ids[k % 2][:, 1, :], part[:, 1:2], None, ALU.is_equal)\
                    .then_inc(s_oh, 1)

            def add_words(k, q):
                t = CH * k + 2 * q
                dve.wait_ge(s_word[k % 4], 16 * CH * (k // 4 + 1))
                dve.wait_ge(s_emb, 2 * k + q + 1)
                ve.tensor_tensor(word[:, t:t + 2, :], word[:, t:t + 2, :],
                                 bank[5][:, 0:2 * D].rearrange("p (u d) -> p u d", u=2), ALU.add).then_inc(s_embadd, 1)
                return 2 * k + q + 1

            def word_stats(k, q, added):
                dve.wait_ge(s_embadd, added)
                for u in range(2):
                    last = did(ve.bn_stats(st_w[:, 2 * q + u, :], word[:, CH * k + 2 * q + u, :]))
                return last

            def aggregate(mv, st, done, ready):
                wait(done)
                for t in range(CH):
                    last = did(ve.bn_aggr(mv[:, t, :], st[:, t, :]))
                wait(last)
                ve.nop().then_inc(ready, 1)

            def gamma_root(k, link, done=None):
                if link == 0:
                    dve.wait_ge(s_wg, k + 1)
                return newton(0, link, mv_w[:, :, 1], 1e-12, done)

            def gamma_part(k, u):
                for t in (2 * u, 2 * u + 1):
                    last = did(ve.scalar_tensor_tensor(out=word[:, CH * k + t, :], in0=word[:, CH * k + t, :],
                                                       scalar=mv_w[:, t, 0:1], in1=gb[:, 0, :],
                                                       op0=ALU.subtract, op1=ALU.mult))
                return last

            def beta_part(k, u, done):
                wait(done)
                for t in (2 * u, 2 * u + 1):
                    last = did(ve.scalar_tensor_tensor(out=h[:, CH * k + t, :], in0=word[:, CH * k + t, :],
                                                       scalar=root[:, 0, t:t + 1], in1=gb[:, 1, :],
                                                       op0=ALU.mult, op1=ALU.add))
                return last

            def h_stats(k, u, done):
                wait(done)
                for t in (2 * u, 2 * u + 1):
                    last = did(ve.bn_stats(st_h[:, t, :], h[:, CH * k + t, :]))
                return last

            def row_variance(k, link, done=None):
                if link == 0:
                    dve.wait_ge(s_hv, k + 1)
                    return did(ve.tensor_scalar(var_eps[:], mv_h[:, :, 1], 1e-5, None, ALU.add))
                wait(done)
                if link == 1:
                    return did(ve.reciprocal(root_t[:, 1, :], var_eps[:]))
                ve.tensor_tensor(rowvar[:], root_t[:, 1, :], mv_h[:, :, 1], ALU.mult).then_inc(s_rowvar, 1)

            def coefs(k, link, done=None):
                tiles = slice(CH * k, CH * (k + 1))
                y, t, both = root[:, 1, :], root_t[:, 1, :], root_t[:, 2, :]
                if link == 0:
                    dve.wait_ge(s_hg, k + 1)
                    dve.wait_ge(s_bg, k + 1)
                    did(ve.scalar_tensor_tensor(out=both, in0=batch_var[:], scalar=1e-5, in1=var_eps[:],
                                                op0=ALU.add, op1=ALU.mult))
                    return did(ve.tensor_tensor(y, root_0[:, 1, :], root_0[:, 2, :], ALU.mult))
                wait(done)
                if link == 1:
                    return did(ve.scalar_tensor_tensor(out=t, in0=y, scalar=-0.5, in1=y, op0=ALU.mult, op1=ALU.mult))
                if link == 2:
                    return did(ve.tensor_tensor(t, t, both, ALU.mult))
                if link == 3:
                    return did(ve.scalar_tensor_tensor(out=coef1[:, tiles], in0=t, scalar=1.5, in1=y,
                                                       op0=ALU.add, op1=ALU.mult))
                ve.scalar_tensor_tensor(out=shift1[:, tiles], in0=mv_h[:, :, 0], scalar=-1.0, in1=coef1[:, tiles],
                                        op0=ALU.mult, op1=ALU.mult).then_inc(s_coef, 1)

            def row_max(j):
                dve.wait_ge(s_s, j + 1)
                need(dve, s_p, j - 1)
                ve.tensor_reduce(nmax[j % 2][:], bank[3][:, 0:2 * P].rearrange("p (u k) -> p u k", u=2),
                                 axis=AX, op=ALU.max, negate=True).then_inc(s_max, 1)

            def invert(j):
                dve.wait_ge(s_p, j + 1)
                return did(ve.reciprocal(rinv[j % 2][:], rsum[j % 2][:]))

            def residual(j, done):
                par = j % 2
                dve.wait_ge(s_o, j + 1)
                if j == 0:
                    w1_scales()
                wait(done)
                for u in range(2):
                    last = did(ve.scalar_tensor_tensor(out=h[:, 2 * j + u, :], in0=bank[4][:, u * D:(u + 1) * D],
                                                       scalar=rinv[par][:, u:u + 1], in1=h[:, 2 * j + u, :],
                                                       op0=ALU.mult, op1=ALU.add))
                return last

            def residual_stats(j, done):
                wait(done)
                ve.nop().then_inc(s_res, 1)
                for u in range(2):
                    last = did(ve.bn_stats(st2[j % 2][:, u, :], h[:, 2 * j + u, :]))
                return last

            def residual_aggr(j, done):
                wait(done)
                for u in range(2):
                    last = did(ve.bn_aggr(mv2[:, 2 * j + u, :], st2[j % 2][:, u, :]))
                return last

            def residual_end(j, done):
                if j % 2:
                    wait(done)
                    ve.nop().then_inc(s_r2v, 1)

            def second_coefs(r, link, done=None):
                m = mv2[:, CH * r:CH * (r + 1), :]
                if link == 0:
                    dve.wait_ge(s_r2, r + 1)
                if link < 3:
                    return newton(3, link, m[:, :, 1], 1e-5, done)
                wait(done)
                ve.scalar_tensor_tensor(out=shift2[:], in0=m[:, :, 0], scalar=-1.0, in1=root[:, 3, :],
                                        op0=ALU.mult, op1=ALU.mult).then_inc(s_r2c, 1)

            segs = ((0, P, 0, P), (P, D, 2 * P, 2 * P + D2))

            def row_parts(r):
                row = rows[r % 4]
                dve.wait_ge(s_x2, r + 1)
                need(dve, s_scat[r % 4], 16 * TOP * CH * (r // 4))
                for a, b, lo, hi in segs:
                    last = did(ve.tensor_copy(row[:, :, lo:hi], x2[:, :, a:b]))
                wait(last)
                for a, b, lo, hi in segs:
                    last = did(ve.tensor_tensor(row[:, :, lo + b - a:hi + b - a], x2[:, :, a:b], row[:, :, lo:hi],
                                                ALU.subtract))
                wait(last)
                ve.nop().then_inc(s_rows, 1)

            def shift_logits(r, link, done=None):
                lgp = bank[7][:, 0:CH * E].rearrange("p (t e) -> p t e", t=CH)
                if link == 0:
                    dve.wait_ge(s_lg, r + 1)
                    return did(ve.tensor_reduce(lmax[:], lgp, axis=AX, op=ALU.max))
                wait(done)
                ve.tensor_tensor(lg[:], lgp, lmax[:].unsqueeze(2).to_broadcast([P, CH, E]), ALU.subtract)\
                    .then_inc(s_lgx, 1)

            def choose(r, link, done=None):
                tiles = slice(CH * r, CH * (r + 1))
                if link == 0:
                    dve.wait_ge(s_ex, r + 1)
                    return did(ve.reduce_sum(esum[:], lg[:], axis=AX))
                wait(done)
                if link == 1:
                    return did(ve.reciprocal(lmax[:], esum[:]))
                if link == 2:
                    return did(ve.tensor_tensor(probs[:, tiles, :], lg[:], lmax[:].unsqueeze(2).to_broadcast([P, CH, E]),
                                                ALU.mult))
                if link == 3:
                    for t in range(CH):
                        last = did(ve.max(top8[:, t, :], probs[:, CH * r + t, :]))
                    return last
                if link == 4:
                    for t in range(CH):
                        last = did(ve.max_index(idx8[:, t, :], top8[:, t, :], probs[:, CH * r + t, :]))
                    return last
                if link == 5:
                    return did(ve.tensor_copy(idxf[:], idx8[:, :, 0:TOP]))
                if link == 6:
                    for k in range(TOP):
                        did(ve.tensor_tensor(picked[:, k, tiles, :], iota_e[:].unsqueeze(1).to_broadcast([P, CH, E]),
                                             idxf[:, :, k:k + 1].to_broadcast([P, CH, E]), ALU.is_equal))
                    meta = rows[r % 4][:].bitcast(fp32)
                    did(ve.tensor_copy(meta[:, :, D], idxf[:, :, 0]))
                    did(ve.tensor_copy(meta[:, :, D + 1], token2[:, tiles]))
                    return did(ve.tensor_copy(top_p[:, :, tiles].rearrange("p k t -> p t k"), top8[:, :, 0:TOP]))
                ve.tensor_tensor(marks[:, 0:CH, :], picked[:, 0, tiles, :], picked[:, 1, tiles, :], ALU.add)\
                    .then_inc(s_mk, 1)

            def find_places(r, link, done=None):
                tiles = slice(CH * r, CH * (r + 1))
                rk = bank[7][:, AT_RANKS:AT_RANKS + (CH + 1) * E].rearrange("p (t e) -> p t e", e=E)
                if link == 0:
                    dve.wait_ge(s_rk, r + 1)
                    return did(ve.tensor_tensor(place[:], rk[:, 0:CH, :], base[:].unsqueeze(1).to_broadcast([P, CH, E]),
                                                ALU.add))
                wait(done)
                if link == 1:
                    for k in range(TOP):
                        did(ve.tensor_tensor(place_k[:, k, :, :], place[:], picked[:, k, tiles, :], ALU.mult))
                    return did(ve.tensor_tensor(base[:], base[:], rk[:, CH, :], ALU.add))
                if link == 2:
                    return did(ve.reduce_sum(slot_f[:], place_k[:], axis=AX))
                need(dve, s_scat[(r - 2) % 4], 16 * TOP * CH * ((r - 2) // 4 + 1))
                ve.tensor_copy(slot[r % 2][:], slot_f[:]).then_inc(s_slot, 1)

            def even_step(j, c):
                router, attn, batch, norm, embed = early(c - 3), pair(j - 1), chunk(c + 2), chunk(c + 3), chunk(c + 4)
                last_pair = j == PAIRS
                if last_pair: at_r = residual_aggr(j - 1, residual_stats(j - 1, residual(j - 1, invert(j - 1))))
                if last_pair: residual_end(j - 1, at_r)
                attn = attn and not last_pair
                if late(c - 3):
                    at_f = find_places(c - 3, 0)
                    at_f = find_places(c - 3, 1, at_f)
                    at_f = find_places(c - 3, 2, at_f)
                    find_places(c - 3, 3, at_f)
                if router: at_c = choose(c - 3, 0)
                if batch: at_v = row_variance(c + 2, 0)
                if router: at_c = choose(c - 3, 1, at_c)
                if batch: at_v = row_variance(c + 2, 1, at_v)
                if router: at_c = choose(c - 3, 2, at_c)
                if batch: row_variance(c + 2, 2, at_v)
                if norm: at_g = gamma_root(c + 3, 0)
                if router: at_c = choose(c - 3, 3, at_c)
                if norm: at_g = gamma_root(c + 3, 1, at_g)
                if router: at_c = choose(c - 3, 4, at_c)
                if norm: at_g = gamma_root(c + 3, 2, at_g)
                if router: at_c = choose(c - 3, 5, at_c)
                if attn: at_r = invert(j - 1)
                weights(j, 0)
                if router: at_c = choose(c - 3, 6, at_c)
                if attn: at_r = residual(j - 1, at_r)
                if router: choose(c - 3, 7, at_c)
                if norm: gamma_part(c + 3, 0)
                if attn: at_r = residual_stats(j - 1, at_r)
                if norm: gamma_end[0] = gamma_part(c + 3, 1)
                if attn: at_r = residual_aggr(j - 1, at_r)
                if embed: added = add_words(c + 4, 0)
                weights(j, 1)
                if attn: residual_end(j - 1, at_r)
                if embed: word_stats(c + 4, 0, added)
                weights(j, 2)
                if pair(j + 1):
                    row_max(j + 1)
                weights(j, 3)

            def odd_step(j, c):
                second, attn, batch, norm, embed = chunk(c - 1), pair(j - 1), chunk(c + 2), chunk(c + 3), chunk(c + 4)
                places, router = early(c - 3), chunk(c - 2)
                if second: at_2 = second_coefs(c - 1, 0)
                if norm: at_b0 = beta_part(c + 3, 0, gamma_end[0])
                if second: at_2 = second_coefs(c - 1, 1, at_2)
                if norm: at_b1 = beta_part(c + 3, 1, at_b0)
                if second: at_2 = second_coefs(c - 1, 2, at_2)
                if attn: at_r = invert(j - 1)
                if norm: h_stats(c + 3, 0, at_b0)
                if second: second_coefs(c - 1, 3, at_2)
                if batch: at_k = coefs(c + 2, 0)
                if norm: at_h = h_stats(c + 3, 1, at_b1)
                if batch: at_k = coefs(c + 2, 1, at_k)
                if places: at_f = find_places(c - 3, 0)
                if batch: at_k = coefs(c + 2, 2, at_k)
                if places: at_f = find_places(c - 3, 1, at_f)
                if batch: at_k = coefs(c + 2, 3, at_k)
                if places: at_f = find_places(c - 3, 2, at_f)
                if batch: coefs(c + 2, 4, at_k)
                if chunk(c + 5): one_hots(c + 5)
                if attn: at_r = residual(j - 1, at_r)
                if places: find_places(c - 3, 3, at_f)
                weights(j, 0)
                if attn: at_r = residual_stats(j - 1, at_r)
                if norm:
                    need(dve, s_coef, c + 3)
                    aggregate(mv_h, st_h, at_h, s_hv)
                if attn: at_r = residual_aggr(j - 1, at_r)
                weights(j, 1)
                if embed: added = add_words(c + 4, 1)
                if attn: residual_end(j - 1, at_r)
                if router: at_l = shift_logits(c - 2, 0)
                if embed: at_e = word_stats(c + 4, 1, added)
                if router: shift_logits(c - 2, 1, at_l)
                if pair(j + 1): row_max(j + 1)
                if embed: aggregate(mv_w, st_w, at_e, s_wv)
                weights(j, 2)
                if late(c - 2):
                    at_c = choose(c - 2, 0)
                    for link in range(1, 7):
                        at_c = choose(c - 2, link, at_c)
                    choose(c - 2, 7, at_c)
                if second:
                    row_parts(c - 1)
                weights(j, 3)

            one_hots(0)
            gamma_end = [None]
            for j in STEPS:
                if j == ROUTER_SUM - 1:
                    sum_squares(0, 1, 1)
                if j == -2:
                    keep_wqk()
                if j == ROUTER_SUM + 1:
                    router_parts()
                if j % 2 == 0:
                    even_step(j, j // 2)
                else:
                    odd_step(j, j // 2)

            wait()
            did(ve.tensor_copy(base_i[:], base[:])); wait()
            ve.nop().then_inc(s_base, 1)
            did(ve.tensor_scalar(cnt[:], iota_e[:], float(-REGION), float(P - 1), ALU.mult, ALU.add)); wait()
            did(ve.tensor_tensor(cnt_i[:], base[:], cnt[:], ALU.add)); wait()
            did(ve.tensor_scalar(cnt_i[:], cnt_i[:], 7, None, ALU.logical_shift_right)); wait()
            did(ve.tensor_copy(tiles_e[:], cnt_i[:])); wait()
            did(ve.tensor_tensor(upto[:], upto[:], tiles_e[:].unsqueeze(1).to_broadcast([P, E, E]), ALU.mult))
            did(ve.tensor_scalar(jump[:], tiles_e[:], float(-P), float(REGION), ALU.mult, ALU.add)); wait()
            did(ve.reduce_sum(last_e[:], upto[:], axis=AX)); wait()
            did(ve.tensor_tensor(passed, tile_no[:].unsqueeze(2).to_broadcast([P, SLOTS, E]),
                                 last_e[:].unsqueeze(1).to_broadcast([P, SLOTS, E]), ALU.is_ge)); wait()
            did(ve.reduce_sum(e_f[:], passed, axis=AX)); wait()
            did(ve.tensor_scalar(e_f[:], e_f[:], float(E - 1), None, ALU.min))
            did(ve.tensor_tensor(passed, passed, jump[:].unsqueeze(1).to_broadcast([P, SLOTS, E]), ALU.mult)); wait()
            did(ve.tensor_copy(e_i[:], e_f[:]))
            did(ve.reduce_sum(row_f[:], passed, axis=AX)); wait()
            did(ve.scalar_tensor_tensor(out=row_i[:], in0=tile_no[:], scalar=float(P), in1=row_f[:],
                                        op0=ALU.mult, op1=ALU.add)); wait()
            ve.nop().then_inc(s_plan, 1)
            dve.sem_inc(s_lo, LEAD)
            dve.sem_inc(s_ysb, LEAD)
            dve.sem_inc(s_to, 4)

            for e in range(E):
                dve.wait_ge(s_whi, 8 + e + 1)
                done = did(low(w2[:, e, :, 1, :], w2_s[:, e], w2[:, e, :, 0, :], scale[:, 2:3]))
            wait(done)
            ve.nop().then_inc(s_wlo, 1)

            dve.wait_ge(s_imp, 1)
            did(ve.tensor_reduce(imp[:], bank[7][:, 0:TILES * E].rearrange("p (t e) -> p e t", e=E),
                                 axis=AX, op=ALU.add)); wait()
            did(ve.tensor_scalar(imp[:], imp[:], -1.0, 1.0 - 0.9, ALU.add, ALU.mult)); wait()
            did(ve.tensor_scalar(imp[:], imp[:], 1.0, 0.01, ALU.add, ALU.add)); wait()
            for k in range(TOP):
                did(ve.tensor_tensor(bal[:, k], picked[:, k], imp[:].unsqueeze(1).to_broadcast([P, TILES, E]), ALU.mult))
            wait()
            did(ve.reduce_sum(wgt[:], bal[:], axis=AX)); wait()
            did(ve.reciprocal(wgt[:], wgt[:])); wait()
            did(ve.tensor_tensor(wgt[:], wgt[:], top_p[:], ALU.mult)); wait()
            did(ve.tensor_tensor(wsum[:], wgt[:, 0, :], wgt[:, 1, :], ALU.add)); wait()
            did(ve.reciprocal(wsum[:], wsum[:])); wait()
            did(ve.tensor_tensor(wgt[:], wgt[:], wsum[:].unsqueeze(1).to_broadcast([P, TOP, TILES]), ALU.mult)); wait()


            def experts(t, q, r):
                fixed = isinstance(t, int)
                if not fixed or t >= 3:
                    m = (q - 3) % 4
                    dve.wait_ge(s_y, t - 3 + 1 + LEAD)
                    dve.wait_ge(s_ylo, t - 3 + 1)
                    ve.scalar_tensor_tensor(out=y_sb[m][:], in0=bank[5 + m % 2][:, 0:D], scalar=scale[:, 6:7],
                                            in1=y_lo[m % 2][:], op0=ALU.mult, op1=ALU.add).then_inc(s_ysb, 1)
                if not fixed or t < SLOTS:
                    dve.wait_ge(s_xin[q], r * 4 + 16)
                    dve.wait_ge(s_ysc[q], r * 4)
                    meta = xin[q][:].bitcast(fp32)
                    ve.tensor_scalar(y_to[q][:], meta[:, D:D + 1], e_f[:, bass.ds(t, 1)], meta[:, D + 1:D + 2],
                                     ALU.not_equal, ALU.add).then_inc(s_to, 1)
                if not fixed or 1 <= t <= SLOTS:
                    par = (q - 1) % 2
                    dve.wait_ge(s_hi, t)
                    ve.scalar_tensor_tensor(out=hT[par][:, 1, :, :], in0=bank[3 + par][:].rearrange("p (c k) -> p c k", c=IC),
                                            scalar=scale[:, 4:5], in1=hT[par][:, 0, :, :],
                                            op0=ALU.mult, op1=ALU.subtract).then_inc(s_lo, 1)
            run_experts(dve, experts)

            for g in range(TILES // BACK):
                dve.wait_ge(s_back[g % backs], 16 * (g // backs + 1))
                done = [None] * BACK
                for k in range(TOP):
                    for u in range(BACK):
                        t = BACK * g + u
                        if k > 0:
                            wait(done[u])
                        done[u] = did(ve.scalar_tensor_tensor(out=h[:, t, :], in0=back[g % backs][:, u, k, :],
                                                              scalar=wgt[:, k, t:t + 1], in1=h[:, t, :],
                                                              op0=ALU.mult, op1=ALU.add))
                wait()
                ve.nop().then_inc(s_fin, 1)

        @block.scalar
        def _(act):
            ac = nc.scalar

            links = Steps(act, s_ac2)

            def square_room(n):
                if n >= 2:
                    act.wait_ge(s_ac, n - 1)

            def guess(n, var, eps_col, done):
                links.did(ac.activation(root_ln[:, n, :], var, ACT.Ln, bias=eps[:, eps_col:eps_col + 1])); links.wait()
                ac.activation(root_0[:, n, :], root_ln[:, n, :], ACT.Exp, scale=-0.5).then_inc(done, 1)

            def embedding_guess(k):
                act.wait_ge(s_wv, k + 1)
                guess(0, mv_w[:, :, 1], 0, s_wg)

            def first_guess(k):
                act.wait_ge(s_hv, k + 1)
                guess(1, mv_h[:, :, 1], 1, s_hg)

            def batch_guess(k):
                act.wait_ge(s_bv, k + 1)
                links.did(ac.copy(batch_var[:], bank[7][:, AT_BATCH:AT_BATCH + CH])); links.wait()
                guess(2, batch_var[:], 1, s_bg)

            def second_guess(r):
                act.wait_ge(s_r2v, r + 1)
                guess(3, mv2[:, CH * r:CH * (r + 1), 1], 1, s_r2)

            def normalise(j):
                act.wait_ge(s_coef, j // 2 + 1)
                need(act, s_xt, j - 1)
                for u in range(2):
                    t = 2 * j + u
                    last = ac.activation(xn[j % 2][:, u, :], h[:, t, :], ACT.Identity, scale=coef1[:, t:t + 1],
                                         bias=shift1[:, t:t + 1])
                last.then_inc(s_xn, 1)

            def keep_xnT(j):
                act.wait_ge(s_xt, j + 1)
                need(act, s_s, j - 1)
                need(act, s_v, j - 1)
                ac.copy(xnT[j % 2][:, 0, :], bank[0][:, 0:2 * P])
                ac.copy(xnT[j % 2][0:D2, 1, :], bank[0][0:D2, 2 * P:4 * P]).then_inc(s_xtsb, 1)

            def keep_g(j):
                act.wait_ge(s_g, j + 1)
                need(act, s_s, j - 1)
                ac.copy(gT[j % 2][:, 0, :], bank[1][:, 0:2 * P])
                ac.copy(gT[j % 2][0:D2, 1, :], bank[1][0:D2, 2 * P:4 * P]).then_inc(s_gsb, 1)

            def keep_v(j):
                act.wait_ge(s_v, j + 1)
                need(act, s_o, j - 1)
                ac.copy(v_sb[j % 2][:].rearrange("p u d -> p (u d)"), bank[2][:, 0:2 * D]).then_inc(s_vsb, 1)

            def softmax(j):
                par = j % 2
                act.wait_ge(s_max, j + 1)
                need(act, s_pt_, j - 1)
                need(act, s_res, j - 1)
                for u in range(2):
                    last = ac.activation(pr[par][:, u, :], bank[3][:, u * P:(u + 1) * P], ACT.Exp,
                                         bias=nmax[par][:, u:u + 1], accum_out=rsum[par][:, u:u + 1])
                last.then_inc(s_p, 1)

            def keep_pT(j):
                act.wait_ge(s_pt_, j + 1)
                need(act, s_o, j - 1)
                ac.copy(prT[j % 2][:].rearrange("p u k -> p (u k)"), bank[3][:, 2 * P:4 * P]).then_inc(s_ptsb, 1)

            def second_norm(r):
                act.wait_ge(s_r2c, r + 1)
                need(act, s_rows, r)
                for t in range(CH):
                    last = ac.activation(x2[:, t, :], h[:, CH * r + t, :], ACT.Identity, scale=root[:, 3, t:t + 1],
                                         bias=shift2[:, t:t + 1])
                last.then_inc(s_x2, 1)

            def keep_x2T(r, q):
                need(act, s_lg, r)
                act.wait_ge(s_x2t, 2 * r + q + 1)
                ac.copy(x2T[:, 2 * q:2 * q + 2, :, :].rearrange("p u k t -> p (u k t)"),
                        bank[6][:].bitcast(fp16)[:, 0:6 * P]).then_inc(s_x2tsb, 1)

            def exp_logits(r):
                act.wait_ge(s_lgx, r + 1)
                ac.activation(lg[:], lg[:], ACT.Exp, scale=scale[:, 7:8]).then_inc(s_ex, 1)

            w2_s = stage[:].rearrange("p e a i -> p (e a i)")[:, 0:E * IC * D].rearrange("p (e c d) -> p e c d", e=E, c=IC)

            def square_w1(n):
                square_room(1 + n)
                ac.activation(junk[(1 + n) % 2], stage[:, n // 2, n % 2, :], ACT.Square,
                              accum_out=sq[:, 1, n:n + 1]).then_inc(s_ac, 1)

            def square_w2(n):
                square_room(17 + n)
                ac.activation(junk[(17 + n) % 2][:, 0:2 * D].rearrange("p (c d) -> p c d", c=2),
                              w2_s[:, n // 2, 2 * (n % 2):2 * (n % 2) + 2], ACT.Square,
                              accum_out=sq[:, 2, n:n + 1]).then_inc(s_ac, 1)

            def weights(j):
                if -4 <= j < 0:
                    act.wait_ge(s_w1in, 48 * E // 2)
                    for n in range(4 * (j + 4), 4 * (j + 5)):
                        square_w1(n)
                if W1_HIGH <= j < W1_HIGH + 8:
                    act.wait_ge(s_scale, 1)
                    for k in range(2):
                        e = j - W1_HIGH
                        last = ac.activation(w1[:, e, 2 * k, :], stage[:, e, k, :], ACT.Copy, scale=scale[:, 0:1])
                    last.then_inc(s_whi, 1)
                if j in W2_SQUARES:
                    act.wait_ge(s_w2in, 16)
                    n0 = 4 * W2_SQUARES.index(j)
                    for n in range(n0, n0 + 4):
                        square_w2(n)

            nc.scalar.preload_act_table_set("natural_log_exp_and_others")
            act.wait_ge(s_eps, 2)
            act.wait_ge(s_rin, 48)
            ac.activation(junk[0][:, 0:2 * E], rt_f[:].rearrange("p a e -> p (a e)"), ACT.Square,
                          accum_out=sq[:, 0, 0:1]).then_inc(s_ac, 1)
            for j in STEPS:
                c = j // 2
                if pair(j):
                    softmax(j)
                if j % 2 == 0:
                    if chunk(c + 3):
                        embedding_guess(c + 3)
                    if chunk(c + 2):
                        first_guess(c + 2)
                    if early(c - 3):
                        exp_logits(c - 3)
                if pair(j + 1):
                    keep_g(j + 1)
                    keep_v(j + 1)
                if pair(j + 2):
                    normalise(j + 2)
                if j % 2 == 0:
                    if chunk(c - 2):
                        keep_x2T(c - 2, 0)
                if pair(j):
                    keep_pT(j)
                if j % 2 == 0 and chunk(c - 2):
                    keep_x2T(c - 2, 1)
                if pair(j + 2):
                    keep_xnT(j + 2)
                if j % 2 == 0 and chunk(c + 2):
                    batch_guess(c + 2)
                if j % 2 and late(c - 2):
                    exp_logits(c - 2)
                if chunk(c - 1):
                    if j % 2 == 0:
                        second_guess(c - 1)
                    else:
                        second_norm(c - 1)
                weights(j)

            act.wait_ge(s_scale, 2)
            for e in range(E):
                ac.activation(w2[:, e, :, 0, :], w2_s[:, e], ACT.Copy, scale=scale[:, 2:3]).then_inc(s_whi, 1)

            nc.scalar.preload_act_table_set("silu_and_others")

            for x in (s_xftsb, s_hs):
                act.sem_inc(x, LEAD)

            def experts(t, q, r):
                fixed = isinstance(t, int)
                if not fixed or 1 <= t <= SLOTS:
                    par = (q - 1) % 2
                    if fixed and t == 1:
                        act.wait_ge(s_wlo, 3)
                    act.wait_ge(s_h1, t + LEAD)
                    act.wait_ge(s_ht, t - 1 + LEAD - 1)
                    ac.activation(hs[par][:], bank[1 + par][:], ACT.Silu, scale=scale[:, 1:2]).then_inc(s_hs, 1)
                if not fixed or t < SLOTS:
                    act.wait_ge(s_xft, t + 1 + 4)
                    act.wait_ge(s_h1, t + 1)
                    ac.copy(xT[q % 2][:].rearrange("p k t -> p (k t)"), bank[0][:].bitcast(fp16)[:, 0:3 * P])\
                      .then_inc(s_xftsb, 1)
                if not fixed or t >= 3:
                    par = (q - 3) % 2
                    act.wait_ge(s_y, t - 3 + 1 + LEAD)
                    act.wait_ge(s_ysb, t - 5 + 1 + LEAD)
                    ac.activation(y_lo[par][:], bank[5 + par][:, D:2 * D], ACT.Copy, scale=scale[:, 6:7]).then_inc(s_ylo, 1)
                if not fixed or 1 <= t <= SLOTS:
                    par = (q - 1) % 2
                    act.wait_ge(s_ht, t + LEAD)
                    act.wait_ge(s_y, t)
                    ac.activation(hT[par][:, 0, :, :].rearrange("p c k -> p (c k)"), bank[3 + par][:], ACT.Copy,
                                  scale=scale[:, 4:5]).then_inc(s_hi, 1)
            run_experts(act, experts)
            out_v = out.rearrange("b p d -> p b d")
            for g in range(TILES // BACK):
                act.wait_ge(s_fin, g + 1)
                act.dma_start(out_v[:, BACK * g:BACK * (g + 1), :], h[:, BACK * g:BACK * (g + 1), :])\
                   .then_inc(s_out[g % 4], 16)
            for g in range(4):
                act.wait_ge(s_out[g], 16 * TILES // BACK // 4)


def kernel(x, mask_BS_i1_0, pos_BS, L0_tok_word_emb, L0_tok_pos_emb, L0_tok_type_emb, L0_tok_gamma,
           L0_tok_beta, L0_attn_Wk, L0_attn_Wq, L0_attn_Wv, L0_ffn_router_w, L0_ffn_w1, L0_ffn_w2):
    import numpy as np
    import concourse.bacc as bacc
    from concourse.bass_utils import run_bass_kernel_spmd

    B, S = x.shape
    E, I, D = L0_ffn_w1.shape
    w2 = np.asarray(L0_ffn_w2).reshape(E, D, I // 128, 128)
    arrays = {
        "ids": np.asarray(x).T,
        "pt_rows": np.stack([np.asarray(pos_BS).reshape(1, B // 4, 4 * S),
                             np.asarray(mask_BS_i1_0).reshape(1, B // 4, 4 * S)], axis=2),
        "word_emb": np.asarray(L0_tok_word_emb),
        "pos_emb": np.asarray(L0_tok_pos_emb),
        "type_emb": np.asarray(L0_tok_type_emb),
        "gamma": np.asarray(L0_tok_gamma).reshape(1, D),
        "beta": np.asarray(L0_tok_beta).reshape(1, D),
        "wq": np.asarray(L0_attn_Wq),
        "wk": np.asarray(L0_attn_Wk),
        "wv_t": np.asarray(L0_attn_Wv).T,
        "router_t": np.asarray(L0_ffn_router_w).T,
        "w1_t": np.asarray(L0_ffn_w1).transpose(2, 0, 1).reshape(D, E * I),
        "w2_t": w2.transpose(3, 0, 2, 1).reshape(128, E * (I // 128) * D),
    }
    arrays = {k: np.ascontiguousarray(v) for k, v in arrays.items()}
    nc = bacc.Bacc("TRN2", target_bir_lowering=False, num_devices=1)
    args = [nc.dram_tensor(k, v.shape, mybir.dt.from_np(v.dtype), kind="ExternalInput").ap()
            for k, v in arrays.items()]
    out = nc.dram_tensor("out", (B, S, D), mybir.dt.float32, kind="ExternalOutput").ap()
    tower_kernel(nc, *args, out)
    r = run_bass_kernel_spmd(nc, [arrays], core_ids=[0])
    return r.results[0]["out"]
```
